# Optimizing a Trainium2 kernel written in Bass

```python
import numpy as np
import jax
import jax.numpy as jnp

def _softmax(x, axis=-1):
    return jax.nn.softmax(x, axis=axis)

def _gelu(x):
    return jax.nn.gelu(x, approximate=True)

def _silu(x):
    return jax.nn.silu(x)

def _sigmoid(x):
    return jax.nn.sigmoid(x)

def _layernorm(x, axis=-1, eps=1e-05):
    m = jnp.mean(x, axis=axis, keepdims=True)
    v = jnp.var(x, axis=axis, keepdims=True)
    return (x - m) / jnp.sqrt(v + eps)

def _scatter_add(tgt, idx, src, axis=0):
    return tgt.at[idx].add(src)

def _segment_sum(src, seg, n):
    return jax.ops.segment_sum(src, seg, n)
kernel_name = 'mk_perceiver_d2_seqx_r4_9c4c27'

def setup_inputs(seed: int=0):
    np.random.seed(seed)
    _w = jnp.asarray

    def _rec_inputs():
        import jax
        import jax.numpy as jnp
        _rk = jax.random.key(seed)
        x = 7.22e-05 + 1 * jax.random.normal(jax.random.fold_in(_rk, 1), (8, 64, 512), jnp.float32)
        _lenS = 64 - jax.random.randint(jax.random.fold_in(_rk, 7), (8,), 0, max(1, 64 // 4) + 1, jnp.int32)
        _lenS2 = 256 - jax.random.randint(jax.random.fold_in(_rk, 8), (8,), 0, max(1, 256 // 4) + 1, jnp.int32)
        _ctx_512P = jax.random.normal(jax.random.fold_in(_rk, 11), (8, 16, 128), jnp.float32)
        _ctx_512c = jax.random.dirichlet(jax.random.fold_in(_rk, 511), 0.3 * jnp.ones((16,), jnp.float32), (8, 256))
        _ctx_512t = jnp.einsum('bsk,bkd->bsd', _ctx_512c, _ctx_512P)
        _ctx_512t = _ctx_512t * jax.lax.rsqrt(jnp.mean(jnp.square(_ctx_512t)) + 1e-12) * 0.953939
        ctx_512 = -0.000514642 + 1.00011 * (_ctx_512t + 0.3 * jax.random.normal(jax.random.fold_in(_rk, 611), (8, 256, 128), jnp.float32))
        return (x, ctx_512)
    x, ctx_512 = _rec_inputs()

    def _L0_xattn_setup():
        import jax, jax.numpy as jnp
        import numpy as np
        B, S, H, NH, L = (2, 512, 512, 16, 128)
        HD = H // NH
        key = jax.random.key(seed)
        k1, k2, k3, k4, k5 = jax.random.split(key, 5)
        scale = 0.02
        return {'q': jax.random.normal(k1, (B, S, H), dtype=jnp.float32), 'latent_kv': jax.random.normal(k2, (B, S, L), dtype=jnp.float32), 'Wq': jax.random.normal(k3, (H, H), dtype=jnp.float32) * scale, 'Wkv_expand': jax.random.normal(k4, (2 * H, L), dtype=jnp.float32) * scale, 'Wout': jax.random.normal(k5, (H, H), dtype=jnp.float32) * scale}
    _L0_xattn_all = _L0_xattn_setup()
    _L0_xattn_in = {k: v for k, v in _L0_xattn_all.items() if k in ('Wq', 'Wkv_expand', 'Wout')}
    del _L0_xattn_all

    def _L0_attn_setup():
        import jax, jax.numpy as jnp
        import numpy as np
        HIDDEN = 512
        KEY = 512
        EPS = 1e-05
        key = jax.random.key(seed)
        k1, k2, k3 = jax.random.split(key, 3)
        B, S = (4, 512)
        x = jax.random.normal(k1, (B, S, HIDDEN), dtype=jnp.float32)
        bq = 1.0 / np.sqrt(HIDDEN)
        qkv = jax.random.uniform(k2, (HIDDEN, KEY * 3), minval=-bq, maxval=bq, dtype=jnp.float32)
        bo = 1.0 / np.sqrt(KEY)
        o_proj = jax.random.uniform(k3, (KEY, HIDDEN), minval=-bo, maxval=bo, dtype=jnp.float32)
        gamma = jnp.ones((HIDDEN,), dtype=jnp.float32)
        beta = jnp.zeros((HIDDEN,), dtype=jnp.float32)
        return {'x': x, 'qkv': qkv, 'o_proj': o_proj, 'gamma': gamma, 'beta': beta}
    _L0_attn_all = _L0_attn_setup()
    _L0_attn_in = {k: v for k, v in _L0_attn_all.items() if k in ('qkv', 'o_proj', 'gamma', 'beta')}
    del _L0_attn_all

    def _L0_ffn_setup():
        import jax, jax.numpy as jnp
        import numpy as np
        EPS = 1e-06
        Q_B = 128.0

        def layer_norm(x):
            mean = jnp.mean(x, axis=-1, keepdims=True)
            var = jnp.var(x, axis=-1, keepdims=True)
            return (x - mean) / jnp.sqrt(var + EPS)

        def absmax_quant(x):
            gamma = jnp.max(jnp.abs(x), axis=-1, keepdims=True)
            x_hat = jnp.clip(x * Q_B / gamma, -Q_B + EPS, Q_B - EPS)
            return x_hat * gamma / Q_B

        def ternarize_weights(w):
            gamma = jnp.mean(jnp.abs(w))
            return jnp.sign(jnp.round(w / (gamma + EPS))) * gamma

        def bitlinear(x, w):
            xn = layer_norm(x)
            x_hat = xn + jax.lax.stop_gradient(absmax_quant(xn) - xn)
            w_hat = w + jax.lax.stop_gradient(ternarize_weights(w) - w)
            return jnp.einsum('bsd,od->bso', x_hat, w_hat)
        key = jax.random.key(seed)
        k1, k2, k3 = jax.random.split(key, 3)
        B, S, D = (4, 512, 512)
        x = jax.random.normal(k1, (B, S, D), dtype=jnp.float32)
        w_fc = jax.random.normal(k2, (4 * D, D), dtype=jnp.float32) / np.sqrt(D)
        w_proj = jax.random.normal(k3, (D, 4 * D), dtype=jnp.float32) / np.sqrt(4 * D)
        return {'x': x, 'w_fc': w_fc, 'w_proj': w_proj}
    _L0_ffn_all = _L0_ffn_setup()
    _L0_ffn_in = {k: v for k, v in _L0_ffn_all.items() if k in ('w_fc', 'w_proj')}
    del _L0_ffn_all

    def _L1_xattn_setup():
        import jax, jax.numpy as jnp
        import numpy as np
        B, S, L = (2, 256, 256)
        DIM_Q, H, K, D_C, D_CQ, R = (512, 16, 128, 128, 384, 64)

        def _rope_tables(seq_len, dim, dtype):
            inv_freq = 1.0 / 10000.0 ** (jnp.arange(0, dim, 2, dtype=dtype) / dim)
            t = jnp.arange(seq_len, dtype=dtype)
            freqs = t[:, None] * inv_freq[None, :]
            sin = jnp.repeat(jnp.sin(freqs), 2, axis=-1)
            cos = jnp.repeat(jnp.cos(freqs), 2, axis=-1)
            return (sin, cos)

        def _rotate_half(x):
            h = x.shape[-1] // 2
            return jnp.concatenate([-x[..., h:], x[..., :h]], axis=-1)
        key = jax.random.key(seed)
        ks = jax.random.split(key, 8)
        s_in = 1.0 / np.sqrt(DIM_Q)
        s_k = 1.0 / np.sqrt(K)
        s_cq = 1.0 / np.sqrt(D_CQ)
        s_c = 1.0 / np.sqrt(D_C)
        return {'hidden_q': jax.random.normal(ks[0], (B, S, DIM_Q), jnp.float32), 'kv_c': jax.random.normal(ks[1], (B, L, D_C), jnp.float32), 'Wq': jax.random.normal(ks[2], (H * K, DIM_Q), jnp.float32) * s_in, 'w_kc_q': jax.random.normal(ks[3], (H, K, D_CQ), jnp.float32) * s_k, 'w_kc_kv': jax.random.normal(ks[4], (H, K, D_C), jnp.float32) * s_k, 'W_qr': jax.random.normal(ks[5], (H, D_CQ, R), jnp.float32) * s_cq / np.sqrt(R), 'W_kr': jax.random.normal(ks[6], (H, D_C, R), jnp.float32) * s_c, 'Wo': jax.random.normal(ks[7], (DIM_Q, H * K), jnp.float32) * s_k}
    _L1_xattn_all = _L1_xattn_setup()
    _L1_xattn_in = {k: v for k, v in _L1_xattn_all.items() if k in ('Wq', 'w_kc_q', 'w_kc_kv', 'W_qr', 'W_kr', 'Wo')}
    del _L1_xattn_all

    def _L1_attn_setup():
        import jax, jax.numpy as jnp
        import numpy as np
        NDIM = 16
        key = jax.random.key(seed)
        ks = jax.random.split(key, 5)
        L, B, D, N = (1024, 8, 512, NDIM)
        return {'x': jax.random.normal(ks[0], (L, B, D), dtype=jnp.float32), 'delta': jax.random.normal(ks[1], (D, N, 1), dtype=jnp.float32), 'alpha': jax.random.normal(ks[2], (D, N, 1), dtype=jnp.float32), 'beta': jax.random.normal(ks[3], (D, N, 1), dtype=jnp.float32), 'gamma': jax.random.normal(ks[4], (D, N), dtype=jnp.float32)}
    _L1_attn_all = _L1_attn_setup()
    _L1_attn_in = {k: v for k, v in _L1_attn_all.items() if k in ('delta', 'alpha', 'beta', 'gamma')}
    del _L1_attn_all

    def _L1_ffn_setup():
        import jax, jax.numpy as jnp
        import numpy as np
        B, S, D = (4, 512, 512)
        DFF = 1408
        E, K, R = (8, 2, 16)
        SCALING = 32.0 / 16.0
        key = jax.random.key(seed)
        ks = jax.random.split(key, 12)
        s = lambda k, shape, scale: jax.random.normal(k, shape, dtype=jnp.float32) * scale
        return {'x': s(ks[0], (B, S, D), 1.0), 'Wg': s(ks[1], (DFF, D), 0.02), 'Wu': s(ks[2], (DFF, D), 0.02), 'Wd': s(ks[3], (D, DFF), 0.02), 'Wr': s(ks[4], (E, D), 0.02), 'Ag': s(ks[5], (E, R, D), 0.02), 'Bg': s(ks[6], (E, DFF, R), 0.02), 'Au': s(ks[7], (E, R, D), 0.02), 'Bu': s(ks[8], (E, DFF, R), 0.02), 'Ad': s(ks[9], (E, R, DFF), 0.02), 'Bd': s(ks[10], (E, D, R), 0.02)}
    _L1_ffn_all = _L1_ffn_setup()
    _L1_ffn_in = {k: v for k, v in _L1_ffn_all.items() if k in ('Wg', 'Wu', 'Wd', 'Wr', 'Ag', 'Bg', 'Au', 'Bu', 'Ad', 'Bd')}
    del _L1_ffn_all
    return {'x': x, 'ctx_512': ctx_512, 'L0_xattn_Wq': _L0_xattn_in['Wq'], 'L0_xattn_Wkv_expand': _L0_xattn_in['Wkv_expand'], 'L0_xattn_Wout': _L0_xattn_in['Wout'], 'L0_attn_qkv': _L0_attn_in['qkv'], 'L0_attn_o_proj': _L0_attn_in['o_proj'], 'L0_attn_gamma': _L0_attn_in['gamma'], 'L0_attn_beta': _L0_attn_in['beta'], 'L0_ffn_w_fc': _L0_ffn_in['w_fc'], 'L0_ffn_w_proj': _L0_ffn_in['w_proj'], 'L1_xattn_Wq': _L1_xattn_in['Wq'], 'L1_xattn_w_kc_q': _L1_xattn_in['w_kc_q'], 'L1_xattn_w_kc_kv': _L1_xattn_in['w_kc_kv'], 'L1_xattn_W_qr': _L1_xattn_in['W_qr'], 'L1_xattn_W_kr': _L1_xattn_in['W_kr'], 'L1_xattn_Wo': _L1_xattn_in['Wo'], 'L1_attn_delta': _L1_attn_in['delta'], 'L1_attn_alpha': _L1_attn_in['alpha'], 'L1_attn_beta': _L1_attn_in['beta'], 'L1_attn_gamma': _L1_attn_in['gamma'], 'L1_ffn_Wg': _L1_ffn_in['Wg'], 'L1_ffn_Wu': _L1_ffn_in['Wu'], 'L1_ffn_Wd': _L1_ffn_in['Wd'], 'L1_ffn_Wr': _L1_ffn_in['Wr'], 'L1_ffn_Ag': _L1_ffn_in['Ag'], 'L1_ffn_Bg': _L1_ffn_in['Bg'], 'L1_ffn_Au': _L1_ffn_in['Au'], 'L1_ffn_Bu': _L1_ffn_in['Bu'], 'L1_ffn_Ad': _L1_ffn_in['Ad'], 'L1_ffn_Bd': _L1_ffn_in['Bd']}

def reference(x, ctx_512, L0_xattn_Wq, L0_xattn_Wkv_expand, L0_xattn_Wout, L0_attn_qkv, L0_attn_o_proj, L0_attn_gamma, L0_attn_beta, L0_ffn_w_fc, L0_ffn_w_proj, L1_xattn_Wq, L1_xattn_w_kc_q, L1_xattn_w_kc_kv, L1_xattn_W_qr, L1_xattn_W_kr, L1_xattn_Wo, L1_attn_delta, L1_attn_alpha, L1_attn_beta, L1_attn_gamma, L1_ffn_Wg, L1_ffn_Wu, L1_ffn_Wd, L1_ffn_Wr, L1_ffn_Ag, L1_ffn_Bg, L1_ffn_Au, L1_ffn_Bu, L1_ffn_Ad, L1_ffn_Bd):
    import jax
    import jax.numpy as jnp

    def _L0_xattn_ref(q, latent_kv, Wq, Wkv_expand, Wout):
        import jax, jax.numpy as jnp
        import numpy as np
        B, S, H, NH, L = (2, 512, 512, 16, 128)
        HD = H // NH
        b, sq, _ = q.shape
        sk = latent_kv.shape[1]
        qp = q @ Wq.T
        kv = latent_kv @ Wkv_expand.T
        k, v = jnp.split(kv, 2, axis=-1)
        qh = qp.reshape(b, sq, NH, HD).transpose(0, 2, 1, 3)
        kh = k.reshape(b, sk, NH, HD).transpose(0, 2, 1, 3)
        vh = v.reshape(b, sk, NH, HD).transpose(0, 2, 1, 3)
        inv_sqrt_d = 1.0 / jnp.sqrt(jnp.float32(HD))
        scores = jnp.einsum('bhqd,bhkd->bhqk', qh, kh) * inv_sqrt_d
        causal = jnp.tril(jnp.ones((sq, sk), dtype=bool))
        scores = jnp.where(causal, scores, jnp.finfo(scores.dtype).min)
        attn = jax.nn.softmax(scores, axis=-1)
        out = jnp.einsum('bhqk,bhkd->bhqd', attn, vh)
        out = out.transpose(0, 2, 1, 3).reshape(b, sq, H)
        return out @ Wout.T

    def _L0_attn_ref(x, qkv, o_proj, gamma, beta):
        import jax, jax.numpy as jnp
        import numpy as np
        HIDDEN = 512
        KEY = 512
        EPS = 1e-05
        residual = x
        mu = jnp.mean(x, axis=-1, keepdims=True)
        var = jnp.mean((x - mu) ** 2, axis=-1, keepdims=True)
        x_norm = (x - mu) / jnp.sqrt(var + EPS) * gamma + beta
        q = x_norm @ qkv[:, :KEY]
        k = x_norm @ qkv[:, KEY:2 * KEY]
        v = x_norm @ qkv[:, 2 * KEY:]
        scale = 1.0 / jnp.sqrt(jnp.float32(KEY))
        scores = jnp.einsum('bsk,btk->bst', q, k) * scale
        S_len = x.shape[1]
        causal = jnp.tril(jnp.ones((S_len, S_len), dtype=bool))
        scores = jnp.where(causal[None], scores, -jnp.inf)
        attn = jax.nn.softmax(scores, axis=-1)
        out = attn @ v
        out = out @ o_proj
        return out + residual

    def _L0_ffn_ref(x, w_fc, w_proj):
        import jax, jax.numpy as jnp
        import numpy as np
        EPS = 1e-06
        Q_B = 128.0

        def layer_norm(x):
            mean = jnp.mean(x, axis=-1, keepdims=True)
            var = jnp.var(x, axis=-1, keepdims=True)
            return (x - mean) / jnp.sqrt(var + EPS)

        def absmax_quant(x):
            gamma = jnp.max(jnp.abs(x), axis=-1, keepdims=True)
            x_hat = jnp.clip(x * Q_B / gamma, -Q_B + EPS, Q_B - EPS)
            return x_hat * gamma / Q_B

        def ternarize_weights(w):
            gamma = jnp.mean(jnp.abs(w))
            return jnp.sign(jnp.round(w / (gamma + EPS))) * gamma

        def bitlinear(x, w):
            xn = layer_norm(x)
            x_hat = xn + jax.lax.stop_gradient(absmax_quant(xn) - xn)
            w_hat = w + jax.lax.stop_gradient(ternarize_weights(w) - w)
            return jnp.einsum('bsd,od->bso', x_hat, w_hat)
        h = bitlinear(x, w_fc)
        h = jax.nn.gelu(h, approximate=False)
        return bitlinear(h, w_proj)

    def _L1_xattn_ref(hidden_q, kv_c, Wq, w_kc_q, w_kc_kv, W_qr, W_kr, Wo):
        import jax, jax.numpy as jnp
        import numpy as np
        B, S, L = (2, 256, 256)
        DIM_Q, H, K, D_C, D_CQ, R = (512, 16, 128, 128, 384, 64)

        def _rope_tables(seq_len, dim, dtype):
            inv_freq = 1.0 / 10000.0 ** (jnp.arange(0, dim, 2, dtype=dtype) / dim)
            t = jnp.arange(seq_len, dtype=dtype)
            freqs = t[:, None] * inv_freq[None, :]
            sin = jnp.repeat(jnp.sin(freqs), 2, axis=-1)
            cos = jnp.repeat(jnp.cos(freqs), 2, axis=-1)
            return (sin, cos)

        def _rotate_half(x):
            h = x.shape[-1] // 2
            return jnp.concatenate([-x[..., h:], x[..., :h]], axis=-1)
        b, s, _ = hidden_q.shape
        l = kv_c.shape[1]
        q_hk = (hidden_q @ Wq.T).reshape(b, s, H, K)
        q_big = jnp.einsum('bshk,hkq->bshq', q_hk, w_kc_q)
        sin, cos = _rope_tables(l, D_C, kv_c.dtype)
        kv_rope = kv_c * cos[None] + _rotate_half(kv_c) * sin[None]
        q_r = jnp.einsum('bshq,hqr->bhsr', q_big, W_qr)
        k_r = jnp.einsum('bld,hdr->bhlr', kv_rope, W_kr)
        scores = jnp.einsum('bhsr,bhlr->bhsl', q_r, k_r)
        attn = jax.nn.softmax(scores, axis=-1)
        ctx_c = jnp.einsum('bhsl,bld->bhsd', attn, kv_rope)
        ctx_lat = jnp.einsum('bhsd,hkd->bshk', ctx_c, w_kc_kv)
        out = ctx_lat.reshape(b, s, H * K) @ Wo.T
        return out

    def _L1_attn_ref(x, delta, alpha, beta, gamma):
        import jax, jax.numpy as jnp
        import numpy as np
        NDIM = 16
        L, B, D = x.shape
        scale = jnp.sqrt(jnp.asarray(1.0 / NDIM, dtype=x.dtype))
        p = jax.nn.sigmoid(delta) * jax.nn.sigmoid(alpha)
        q = 1.0 - p
        g = gamma * scale
        xt = jnp.transpose(x, (1, 2, 0))
        log_q = jnp.log(q)
        vander = jnp.exp(jnp.arange(L, dtype=x.dtype)[None, None, :] * log_q)
        k = jnp.einsum('dnl,dn->dl', p * beta * vander, g)
        fft_len = 2 * L
        k_f = jnp.fft.rfft(k.astype(jnp.float32), n=fft_len)
        x_f = jnp.fft.rfft(xt.astype(jnp.float32), n=fft_len)
        out = jnp.fft.irfft(x_f * k_f, n=fft_len)[..., :L].astype(x.dtype)
        return jax.nn.silu(jnp.transpose(out, (2, 0, 1)))

    def _L1_ffn_ref(x, Wg, Wu, Wd, Wr, Ag, Bg, Au, Bu, Ad, Bd):
        import jax, jax.numpy as jnp
        import numpy as np
        B, S, D = (4, 512, 512)
        DFF = 1408
        E, K, R = (8, 2, 16)
        SCALING = 32.0 / 16.0
        b, s, d = x.shape
        xf = x.reshape(-1, d)
        gate_base = xf @ Wg.T
        up_base = xf @ Wu.T
        base_out = jax.nn.silu(gate_base) * up_base @ Wd.T
        router_logits = xf @ Wr.T
        probs = jax.nn.softmax(router_logits.astype(jnp.float32), axis=-1)
        topw, topi = jax.lax.top_k(probs, K)
        topw = topw.astype(x.dtype)
        expert_w = jnp.sum(jax.nn.one_hot(topi, E, dtype=x.dtype) * topw[..., None], axis=1)

        def expert_step(acc, params):
            Ag_e, Bg_e, Au_e, Bu_e, Ad_e, Bd_e, we = params
            g_lora = xf @ Ag_e.T @ Bg_e.T * SCALING
            u_lora = xf @ Au_e.T @ Bu_e.T * SCALING
            h = jax.nn.silu(gate_base + g_lora) * (up_base + u_lora)
            d_delta = h @ Ad_e.T @ Bd_e.T * SCALING
            return (acc + d_delta * we[:, None], None)
        acc0 = jnp.zeros_like(base_out)
        acc, _ = jax.lax.scan(expert_step, acc0, (Ag, Bg, Au, Bu, Ad, Bd, expert_w.T))
        return (base_out + acc).reshape(b, s, d)
    x = x + _L0_xattn_ref(_layernorm(x, axis=-1), ctx_512, L0_xattn_Wq, L0_xattn_Wkv_expand, L0_xattn_Wout)
    x = x + _L0_attn_ref(_layernorm(x, axis=-1), L0_attn_qkv, L0_attn_o_proj, L0_attn_gamma, L0_attn_beta)
    x = x + _L0_ffn_ref(_layernorm(x, axis=-1), L0_ffn_w_fc, L0_ffn_w_proj)
    x = x + _L1_xattn_ref(_layernorm(x, axis=-1), ctx_512, L1_xattn_Wq, L1_xattn_w_kc_q, L1_xattn_w_kc_kv, L1_xattn_W_qr, L1_xattn_W_kr, L1_xattn_Wo)
    x = x + _L1_attn_ref(_layernorm(x, axis=-1), L1_attn_delta, L1_attn_alpha, L1_attn_beta, L1_attn_gamma)
    x = x + _L1_ffn_ref(_layernorm(x, axis=-1), L1_ffn_Wg, L1_ffn_Wu, L1_ffn_Wd, L1_ffn_Wr, L1_ffn_Ag, L1_ffn_Bg, L1_ffn_Au, L1_ffn_Bu, L1_ffn_Ad, L1_ffn_Bd)
    return x

_drawn_inputs = setup_inputs


def setup_inputs(seed=0):
    import zlib

    import numpy as np

    out = dict(_drawn_inputs(seed))
    spreads = {'L0_attn_gamma': (1.0, 0.6), 'L0_attn_beta': (0.0, 0.574)}
    factors = {'L0_xattn_Wq': 8.0,
     'L1_ffn_Wr': 8.0,
     'L1_ffn_Ag': 8.0,
     'L1_ffn_Bg': 8.0,
     'L1_ffn_Au': 8.0,
     'L1_ffn_Bu': 8.0,
     'L1_ffn_Ad': 8.0,
     'L1_ffn_Bd': 8.0,
     'L1_ffn_Wd': 47.709}
    for name, (base, spread) in spreads.items():
        noise = np.random.default_rng([zlib.crc32(name.encode()), seed]).standard_normal(out[name].shape)
        drawn = base * np.exp(spread * noise) if base else spread * noise
        out[name] = jnp.asarray(drawn.astype(out[name].dtype))
    for name, factor in factors.items():
        out[name] = (out[name] * factor).astype(out[name].dtype)
    return out
```

```python
from contextlib import ExitStack

import numpy as np

import concourse.bass as bass
from concourse import mybir

F32 = mybir.dt.float32
F32R = mybir.dt.float32r
I32 = mybir.dt.int32
ALU = mybir.AluOpType
ACT = mybir.ActivationFunctionType
AX_X = mybir.AxisListType.X

P = 128
NB, SQ, D = 8, 64, 512
T = NB * SQ // P
KC = D // P
DCTX, SK = 128, 256
H0, HD0 = 16, 32
G0 = 4
F0 = 2048
NFB = F0 // 512
H1, R1 = 16, 64
G1, HG = 4, 4
NSSM, LAGS = 16, NB
DFF, E1, R = 1408, 8, 16
NF = DFF // P
CH = 8 * P + 3 * P
MAGIC = 12582912.0
RSQRT_SEED = float(0x5F3759DF)
HIDDEN = -3.0e38


def psum_plan():
    order = [("K", 0), ("K", 1)] + [("V", p) for p in range(4)]
    order += [("T0", t) for t in range(T)] + [("q", m) for m in range(KC)]
    S = lambda g: [("S", g, 0), ("S", g, 1)]
    PT = lambda g: [("PT", g, 0), ("PT", g, 1)]
    O = lambda g: [("O", g, 0), ("O", g, 1)]
    order += S(0) + [("K", 2), ("Wqk", 0)] + S(1) + [("K", 3)] + PT(0) + [("Wqk", 1), ("Wqk", 2)] + O(0)
    order += S(2) + PT(1) + [("Wqk", 3)] + O(1) + S(3) + PT(2) + [("Wvo", 0), ("Wvo", 1)] + O(2)
    order += PT(3) + [("Wvo", 2), ("Wvo", 3)] + O(3)
    order += [("TO", t) for t in range(T)] + [("y0", t) for t in range(T)]
    order += [("T1", c) for c in range(KC)] + [("t", m) for m in range(KC)] + [("s1",), ("wf",)]
    order += [("v", t) for t in range(T)] + [("pt1",)] + [("y1", t) for t in range(T)]
    order += [("T2", t) for t in range(T)]
    fc = lambda t: [("fc", t, n) for n in range(NFB)]
    TH = lambda t: [("TH", t, j) for j in range(4)]
    order += fc(0) + fc(1) + [("wp",)] + TH(0) + [("y2", 0)] + fc(2) + TH(1) + [("y2", 1)]
    order += fc(3) + TH(2) + [("y2", 2)] + TH(3) + [("y2", 3)]
    order += [("kn", j) for j in range(4)] + fold_order(0)
    order += [("T3", t) for t in range(T)]
    for g in range(G1):
        order += attention_order(g)
    order += [("T4", c) for c in range(KC)] + [("TY", c) for c in range(KC)]
    bank_of, turn_of, turns = {}, {}, [0] * 8

    def take(x, b):
        turns[b] += 1
        bank_of[x], turn_of[x] = b, turns[b]

    for n, x in enumerate(order):
        take(x, n % 8)
    for x, b in mlp_order():
        take(x, b)
    return bank_of, turn_of


def fold_order(g):
    return [("w12", g), ("w3", g, 0), ("w3", g, 1)] + [("wo2", g, h) for h in range(HG)]


def attention_order(g):
    order = [("qr", g, 0), ("qr", g, 1)] + [("qp", g, h) for h in range(HG)]
    for s in range(NB + 4):
        if s < NB:
            order.append(("sc", g, s))
        if 0 <= s - 2 < NB:
            order.append(("ptr", g, s - 2))
        if s >= 4 and s % 2 == 0 and (s - 4) // 2 < NB // 2:
            order.append(("cc", g, (s - 4) // 2))
        if g + 1 < G1 and s < 7:
            order.append(fold_order(g + 1)[s])
    return order + [("y3", g, t) for t in range(T)]


def gate_order():
    order = [(0, 0)]
    for f in range(NF):
        order += [(f, 1)] + ([(f + 1, 0)] if f + 1 < NF else []) + [(f, 2)]
    return order


def mlp_order():
    order = [(("T5", t), t) for t in range(T)] + [(("lg",), 4), (("ug",), 6), (("uu",), 7)]
    order += [(("gu", 0, 0), 0)] + [(("tm", k), 4 + k % 2) for k in range(4)]
    order += [(("gu", f, n), 2 * (f % 2)) for f, n in gate_order()[1:]]
    order += [(("z", 1), 4), (("z", 2), 5)]
    return order + [(("y4", t), (6, 7, 0, 2)[t]) for t in range(T)]


def perceiver_blocks(nc, a, out):
    bank_of, turn_of = psum_plan()
    ctx = ExitStack()
    with ctx:
        taken = [0]

        def place(name, dt, cols, at):
            with ExitStack() as s:
                if at:
                    s.enter_context(nc.sbuf_tensor("ahead_of_" + name, [P, at], F32))
                taken[0] = max(taken[0], at + cols)
                return s.enter_context(nc.sbuf_tensor(name, [P, cols], dt))

        X = place("X", F32, T * D, 0)
        XT = place("XT", F32R, 2 * KC * 512, 2048)
        CONST = place("CONST", F32, 1536, 6144)
        STG = place("STG", F32, 8192, 7680)
        M = 15872
        QT = place("QT", F32, 2048, M)
        KBD = place("KBD", F32, 4096, M + 2048)
        VBD = place("VBD", F32, 4096, M + 6144)
        OTOK = place("OTOK", F32, 2048, M + 10240)
        N0 = place("N0", F32, 2048, M + 10240)
        PR = place("PR", F32, 2048, M + 12288)
        PTB = place("PTB", F32, 2048, M + 14336)
        KVRAW = place("KVRAW", F32, 1536, M + 14336)
        WQO = place("WQO", F32R, 8192, M + 16384)
        WQKVO = place("WQKVO", F32R, 8192, M + 24576)
        XF = place("XF", F32, 2048, M)
        TT = place("TT", F32, 2048, M + 2048)
        VF = place("VF", F32, 2048, M + 4096)
        P1 = place("P1", F32, 512, M + 6144)
        PT1 = place("PT1", F32, 512, M + 6656)
        NX = place("NX", F32, 2048, M + 12288)
        HB = place("HB", F32, 4096, M)
        HT = place("HT", F32R, 8192, M + 4096)
        FCT = place("FCT", F32R, 8192, M + 16384)
        PJT = place("PJT", F32R, 8192, M + 24576)
        QP = place("QP", F32R, 4096, M)
        PW = place("PW", F32, 2048, M + 4096)
        KR = place("KR", F32R, 2048, M + 6144)
        KVN = place("KVN", F32R, 4096, M + 8192)
        CC = place("CC", F32R, 4096, M + 12288)
        W3 = place("W3", F32R, 2048, M + 16384)
        QR = place("QR", F32R, 2048, M + 18432)
        PTW = [place("PTW0", F32R, 2048, M + 20480), place("PTW1", F32R, 2048, M + 30720)]
        WO2 = place("WO2", F32R, 8192, M + 22528)
        KVT = place("KVT", F32R, 4096, M + 32768)
        XM = place("XM", F32, 2048, M)
        YM = place("YM", F32, 2048, M + 2048)
        H0T = place("H0T", F32R, 2 * NF * 512, M)
        UM = place("UM", F32R, 4096, M + 11264)
        HS0 = place("HS0", F32R, 1024, M + 15360)
        HS1 = place("HS1", F32R, 1024, M + 16384)
        RING = place("RING", F32R, 3 * 2 * CH, M + 17408)
        WDT = place("WDT", F32R, 2 * NF * 512, M + 25856)
        AGU = place("AGU", F32R, 2 * 1056, M + 25856)
        MLPF = STG[:, 4096:8192]
        ctx.enter_context(nc.sbuf_tensor("all_phases", [P, taken[0]], F32))

        small = ctx.enter_context(nc.sbuf_tensor("small", [P, 64], F32))
        bank = [ctx.enter_context(nc.psum_tensor(f"bank{b}", [P, 512], F32)) for b in range(8)]

        def sem(name):
            return ctx.enter_context(nc.semaphore(name))

        bank_full = [sem(f"bank_full{b}") for b in range(8)]
        bank_free = [sem(f"bank_free{b}") for b in range(8)]

        def psum(x):
            return bank[bank_of[x]]

        def full(x):
            return bank_full[bank_of[x]], turn_of[x]

        def emptied(x):
            return bank_free[bank_of[x]], turn_of[x]

        def freed(x):
            return bank_free[bank_of[x]], 1

        x_in = [sem(f"x_in{t}") for t in range(T)]
        consts_in, kv0_in, wq_in, wout_in, ssm_in = sem("consts_in"), sem("kv0_in"), sem("wq_in"), sem("wout_in"), sem("ssm_in")
        fold0_in = [sem("fold_qk_in"), sem("fold_vo_in")]
        fc_in = [sem(f"fc_in{i}") for i in range(4)]
        pj_in = [sem(f"pj_in{i}") for i in range(4)]
        kv1_in, kr_in, agu_in, bd_in = sem("kv1_in"), sem("kr_in"), sem("agu_in"), sem("bd_in")
        group_in = [sem(f"group_in{g}") for g in range(G1)]
        ring_in = [sem(f"ring_in{i}") for i in range(2)]
        wd_in = [sem(f"wd_in{j}") for j in range(3)]
        out_done = sem("out_done")
        zeroed = sem("zeroed")
        wq_high, wq_split, wout_high, wout_split = sem("wq_high"), sem("wq_split"), sem("wout_high"), sem("wout_split")
        fold0_high = sem("fold0_high")
        fc_summed, pj_summed = sem("fc_summed"), sem("pj_summed")
        fc_rounded, fc_signed, pj_rounded, pj_signed = sem("fc_rounded"), sem("fc_signed"), sem("pj_rounded"), sem("pj_signed")
        kv_roped, kvt_high, kvt_split, kvn_high = sem("kv_roped"), sem("kvt_high"), sem("kvt_split"), sem("kvn_high")
        kr_high, kr_split = sem("kr_high"), sem("kr_split")
        w3_high, wo2_high = sem("w3_high"), sem("wo2_high")
        agu_high, agu_split = sem("agu_high"), sem("agu_split")
        ring_high, ring_split, ring_used = sem("ring_high"), sem("ring_split"), sem("ring_used")
        wd_high, wd_split = sem("wd_high"), sem("wd_split")
        normed = sem("normed")
        xt_high = sem("xt_high")
        xt1_split = sem("xt1_split")
        s0_ready, p0_exp, p0_ready = sem("s0_ready"), sem("p0_exp"), sem("p0_ready")
        ot_high = sem("ot_high")
        s1_ready, p1_exp = sem("s1_ready"), sem("p1_exp")
        h_scales, h_normed, h_quant, ht_high = sem("h_scales"), sem("h_normed"), sem("h_quant"), sem("ht_high")
        qr_high, qp_high, ptw_high, cc_high = sem("qr_high"), sem("qp_high"), sem("ptw_high"), sem("cc_high")
        max_made, sums_made, recip_made, pw_ready = sem("max_made"), sem("sums_made"), sem("recip_made"), sem("pw_ready")
        sig_made, ym_made, ym_silu = sem("sig_made"), sem("ym_made"), sem("ym_silu")
        rt_ready, rt_exp, masks_ready = sem("rt_ready"), sem("rt_exp"), sem("masks_ready")
        um_made, um_high, um_split = sem("um_made"), sem("um_high"), sem("um_split")
        silu_made, hs_high, hs_split, z_made, x_final = sem("silu_made"), sem("hs_high"), sem("hs_split"), sem("z_made"), sem("x_final")
        dve_step, pool_step, dve_tick, x_stat = sem("dve_step"), sem("pool_step"), sem("dve_tick"), sem("x_stat")
        gates = gate_order()

        xt = XT[:, :].rearrange("p (s c n) -> p s c n", s=2, c=KC)
        xt_tiles = XT[:, :].rearrange("p (s c t n) -> p s c t n", s=2, c=KC, t=T)
        x3 = X[:, :].rearrange("p (t d) -> p t d", t=T)
        n0 = N0[:, :].rearrange("p (t d) -> p t d", t=T)
        nx = NX[:, :].rearrange("p (t d) -> p t d", t=T)
        ident = CONST[:, 0:128]
        mask0 = CONST[:, 128:192]
        mask1 = CONST[:, 192:320]
        gammaT, betaT = CONST[:, 320:324], CONST[:, 324:328]
        ones = CONST[:, 328:456]
        expert_rank = CONST[:, 456:464]
        minus_magic = CONST[:, 464:465]
        stats = CONST[:, 480:504].rearrange("p (t k) -> p t k", k=6)
        mv = CONST[:, 504:512].rearrange("p (t k) -> p t k", k=2)
        var2, rs, rs_t = CONST[:, 512:520], CONST[:, 520:528], CONST[:, 528:536]
        lna, lnb = CONST[:, 536:540], CONST[:, 540:544]
        nmax0 = CONST[:, 544:576]
        rsum0 = CONST[:, 576:608]
        parts, wtot = CONST[:, 608:616], CONST[:, 616:632]
        lagw = CONST[:, 640:672].rearrange("p (c l) -> p c l", c=KC)
        nmax1, rsum1 = CONST[:, 672:680], CONST[:, 680:696]
        hstats = CONST[:, 696:744].rearrange("p (u n k) -> p u n k", u=2, k=6)
        hmv = CONST[:, 744:752]
        hsc = CONST[:, 752:768]
        xabs = CONST[:, 768:784]
        mxs = CONST[:, 784:848]
        ssm = CONST[:, 896:1152].rearrange("p (k c n) -> p k c n", k=4, c=KC)
        sw = CONST[:, 1152:1344].rearrange("p (k c n) -> p k c n", k=3, c=KC)
        rt = CONST[:, 1344:1536].rearrange("p (k t e) -> p k t e", k=6, t=T)
        wq = WQO[:, 0:4096].rearrange("p (s c n) -> p s c n", s=2, c=KC)
        wout = WQO[:, 4096:8192].rearrange("p (s c n) -> p s c n", s=2, c=KC)
        wqk = WQKVO[:, 0:4096].rearrange("p (s c n) -> p s c n", s=2, c=KC)
        wvo = WQKVO[:, 4096:8192].rearrange("p (s c n) -> p s c n", s=2, c=KC)
        qt = QT[:, :].rearrange("p (m n) -> p m n", m=KC)
        kbd = KBD[:, :].rearrange("p (u b h k) -> p u b h k", u=2, b=NB, h=4)
        vbd = VBD[:, :].rearrange("p (m b x) -> p m b x", m=8, b=NB)
        otok = OTOK[:, :].rearrange("p (t d) -> p t d", t=T)
        pr = PR[:, :].rearrange("p (u w) -> p u w", u=2)
        ptb = PTB[:, :].rearrange("p (u t m n) -> p u t m n", u=2, t=T, m=2)
        stg4 = STG[:, :].rearrange("p (u w) -> p u w", u=4)
        xf = XF[:, :].rearrange("p (c n) -> p c n", c=KC)
        tt = TT[:, :].rearrange("p (c n) -> p c n", c=KC)
        vf = VF[:, :].rearrange("p (t d) -> p t d", t=T)
        hb = HB[:, :].rearrange("p (u f) -> p u f", u=2)
        ht = HT[:, :].rearrange("p (u s f n) -> p u s f n", u=2, s=2, f=F0 // P)
        fct = FCT[:, :].rearrange("p (c f) -> p c f", c=KC)
        pjt = PJT[:, :].rearrange("p (f d) -> p f d", f=F0 // P)
        kvt = KVT[:, :].rearrange("p (s b l) -> p s b l", s=2, b=NB)
        kvn = KVN[:, :].rearrange("p (s b k d) -> p s b k d", s=2, b=NB, k=2)
        w3 = W3[:, :].rearrange("p (s c r) -> p s c r", s=2, c=KC)
        qr = QR[:, :].rearrange("p (s i n) -> p s i n", s=2, i=2)
        kr = KR[:, :].rearrange("p (s j d) -> p s j d", s=2, j=H1 // 2)
        qp = QP[:, :].rearrange("p (s b h q) -> p s b h q", s=2, b=NB, h=HG)
        pw = PW[:, :].rearrange("p (u i k) -> p u i k", u=4, i=2)
        ptw = [PTW[b // 2][:, 1024 * (b % 2):1024 * (b % 2) + 1024].rearrange("p (s k n) -> p s k n", s=2, k=2) for b in range(4)]
        wo2 = WO2[:, :].rearrange("p (u s h d) -> p u s h d", u=2, s=2, h=HG)
        cc = CC[:, :].rearrange("p (s h n) -> p s h n", s=2, h=HG)
        kv_raw, kv_rot = STG[:, 0:2048], STG[:, 2048:4096]
        cos_t, sin_t = STG[:, 4096:4352], STG[:, 4352:4608]
        kcq = STG[:, 0:1536].rearrange("p (h c k) -> p h c k", h=HG, c=3)
        wqr = STG[:, 1536:2304].rearrange("p (h c r) -> p h c r", h=HG, c=3)
        wq1 = STG[:, 2304:4352].rearrange("p (h c) -> p h c", h=HG)
        kckv = STG[:, 4352:4864].rearrange("p (h d) -> p h d", h=HG)
        woT = STG[:, 4864:6912].rearrange("p (h d) -> p h d", h=HG)
        kr_raw = STG[:, 6912:7936]
        w12 = STG[:, 7936:8192]
        xm = XM[:, :].rearrange("p (c n) -> p c n", c=KC)
        ym = YM[:, :].rearrange("p (c n) -> p c n", c=KC)
        h0t = H0T[:, :].rearrange("p (s f n) -> p s f n", s=2, f=NF)
        um = UM[:, :].rearrange("p (k s n) -> p k s n", k=4, s=2)
        hs = [t_[:, :].rearrange("p (s n) -> p s n", s=2) for t_ in (HS0, HS1)]
        ring = RING[:, :].rearrange("p (u s w) -> p u s w", u=3, s=2)
        wdt = WDT[:, :].rearrange("p (s f d) -> p s f d", s=2, f=NF)
        agu = AGU[:, :].rearrange("p (s w) -> p s w", s=2)
        sg = [MLPF[:, 0:512], MLPF[:, 512:1024]]
        hh = [MLPF[:, 1024:1536], MLPF[:, 1536:2048]]
        mk = MLPF[:, 2048:4096].rearrange("p (k n) -> p k n", k=4)
        bd = mk[:, 0, :]
        maskt = NX[:, :].rearrange("p (k t e) -> p k t e", k=4, t=T)

        def over(ap, n):
            return ap.unsqueeze(2).broadcast_to([ap.shape[0], ap.shape[1], n])

        def in_order(engine, s):
            done = [0]

            def link(ins):
                done[0] += 1
                ins.then_inc(s, 1)
                engine.wait_ge(s, done[0])
            return link

        block = ctx.enter_context(nc.Block())

        @block.sync
        def _(sp):
            for t in range(T):
                sp.dma_start(x3[:, t, :], a["x"].rearrange("(t p) d -> t p d", p=P)[t]).then_inc(x_in[t], 16)
            sp.dma_start(KVRAW[:, :], a["kv0"]).then_inc(kv0_in, 16)
            sp.dma_start(CONST[:, 0:465], a["consts"]).then_inc(consts_in, 16)
            sp.dma_start(STG[:, 0:2048], a["wq"]).then_inc(wq_in, 16)
            sp.dma_start(CONST[:, 896:1152], a["ssm"]).then_inc(ssm_in, 16)
            sp.dma_start(STG[:, 4096:8192], a["fold_qk"]).then_inc(fold0_in[0], 16)
            sp.dma_start(STG[:, 2048:4096], a["wout"]).then_inc(wout_in, 16)
            sp.wait_ge(wq_split, 1)
            sp.wait_ge(wout_split, 1)
            sp.dma_start(STG[:, 0:4096], a["fold_vo"]).then_inc(fold0_in[1], 16)
            sp.wait_ge(*full(("Wqk", KC - 1)))
            for i in (2, 3):
                sp.dma_start(stg4[:, i, :], a["fc"][i]).then_inc(fc_in[i], 16)
            sp.wait_ge(*full(("Wvo", KC - 1)))
            for i in (0, 1):
                sp.dma_start(stg4[:, i, :], a["fc"][i]).then_inc(fc_in[i], 16)
            for i in range(4):
                sp.wait_ge(fc_signed, i + 1)
                sp.dma_start(stg4[:, i, :], a["pj"][i]).then_inc(pj_in[i], 16)
            sp.wait_ge(pj_signed, 4)
            sp.dma_start(STG[:, 0:4608], a["kv1"]).then_inc(kv1_in, 16)
            sp.dma_start(kr_raw, a["kr"]).then_inc(kr_in, 16)
            sp.wait_ge(kvt_split, 1)
            sp.wait_ge(*full(("kn", 3)))
            for g in range(G1):
                if g:
                    sp.wait_ge(*full(("wo2", g - 1, HG - 1)))
                sp.dma_start(STG[:, 0:4352], a["group_in"][g]).then_inc(group_in[g], 16)
                sp.dma_start(STG[:, 4352:6912], a["group_out"][g]).then_inc(group_in[g], 16)
            sp.wait_ge(*full(("wo2", G1 - 1, HG - 1)))
            sp.wait_ge(kr_split, 1)
            sp.dma_start(STG[:, 6144:7200], a["agu"]).then_inc(agu_in, 16)
            for f in range(NF):
                if f >= 2:
                    sp.wait_ge(ring_split, f - 1)
                sp.dma_start(STG[:, 2048 * (f % 2):2048 * (f % 2) + CH], a["mlp"][f]).then_inc(ring_in[f % 2], 16)
                if f == 2:
                    sp.wait_ge(um_made, 4)
                    sp.dma_start(bd, a["bd"]).then_inc(bd_in, 16)
            sp.wait_ge(ring_split, NF)
            for j in range(3):
                n = 512 * min(4, NF - 4 * j)
                if j == 2:
                    sp.wait_ge(wd_split, 1)
                sp.dma_start(STG[:, 2048 * (j % 2):2048 * (j % 2) + n], a["wd"][:, 2048 * j:2048 * j + n]).then_inc(wd_in[j], 16)
            for t in range(T):
                sp.wait_ge(x_final, t + 1)
                sp.dma_start(out.rearrange("(t p) d -> t p d", p=P)[t], x3[:, t, :]).then_inc(out_done, 16)
            sp.wait_ge(out_done, 16 * T)

        @block.tensor
        def _(pe):
            def begin(x):
                if turn_of[x] > 1:
                    pe.wait_ge(bank_free[bank_of[x]], turn_of[x] - 1)
                return psum(x)

            def three(o, w, m, start, stop):
                pe.matmul(o, w[0], m[0], start=start, stop=False)
                pe.matmul(o, w[0], m[1], start=False, stop=False)
                return pe.matmul(o, w[1], m[0], start=False, stop=stop)

            def filled(x, last):
                last.then_inc(bank_full[bank_of[x]], 1)

            def to_features(name, i, src):
                o = begin((name, i))
                for j in range(4):
                    last = pe.transpose(o[:, P * j:P * (j + 1)], src(j), ident)
                filled((name, i), last)

            def keys0(g):
                o = begin(("K", g))
                filled(("K", g), pe.matmul(o[:, :], KVRAW[:, 512 + P * g:512 + P * (g + 1)], KVRAW[:, 0:512],
                                           start=True, stop=True))

            pe.wait_ge(kv0_in, 16)
            keys0(0)
            keys0(1)
            for p in range(4):
                o = begin(("V", p))
                filled(("V", p), pe.matmul(o[:, :], KVRAW[:, P * p:P * (p + 1)], KVRAW[:, 1024:1536],
                                           start=True, stop=True))
            pe.wait_ge(consts_in, 16)
            for t in range(T):
                pe.wait_ge(normed, t + 1)
                to_features("T0", t, lambda j: n0[:, t, P * j:P * (j + 1)])
            pe.wait_ge(wq_split, 1)
            for t in range(T):
                pe.wait_ge(*emptied(("T0", t)))
            for m in range(KC):
                o = begin(("q", m))
                for k in range(KC):
                    last = three(o[:, :], [wq[:, s, k, P * m:P * (m + 1)] for s in (0, 1)],
                                 [xt[:, s, k, :] for s in (0, 1)], k == 0, k == KC - 1)
                filled(("q", m), last)

            def scores0(g):
                pe.wait_ge(*emptied(("q", g)))
                pe.wait_ge(*emptied(("K", g)))
                for i in (0, 1):
                    o = begin(("S", g, i))
                    for b in range(4 * i, 4 * i + 4):
                        last = pe.matmul(o[64 * (b % 2):64 * (b % 2) + 64, 256 * (b // 2 % 2):256 * (b // 2 % 2) + 256],
                                         qt[:, g, SQ * b:SQ * (b + 1)],
                                         kbd[:, g % 2, b, :, :].rearrange("p h k -> p (h k)"), start=True, stop=True)
                    filled(("S", g, i), last)

            def probs0_transposed(g):
                pe.wait_ge(p0_ready, g + 1)
                for i in (0, 1):
                    o = begin(("PT", g, i))
                    for t in (0, 1):
                        for m in (0, 1):
                            at = 256 * (2 * i + t) + P * m
                            last = pe.transpose(o[:, 256 * t + P * m:256 * t + P * (m + 1)],
                                                pr[:, g % 2, at:at + P], ident)
                    filled(("PT", g, i), last)

            def values0(g):
                for i in (0, 1):
                    pe.wait_ge(*emptied(("PT", g, i)))
                    for p in (2 * i, 2 * i + 1):
                        pe.wait_ge(*emptied(("V", p)))
                    o = begin(("O", g, i))
                    for t in (0, 1):
                        for m in (0, 1):
                            last = pe.matmul(o[:, 256 * t + P * m:256 * t + P * (m + 1)], ptb[:, g % 2, 2 * i + t, m, :],
                                             vbd[:, 2 * g + m, 2 * (2 * i + t):2 * (2 * i + t) + 2, :]
                                             .rearrange("p b x -> p (b x)"), start=True, stop=True)
                    filled(("O", g, i), last)

            def fold0(name, n, raw, loaded):
                pe.wait_ge(loaded, 16)
                o = begin((name, n))
                for k in range(KC):
                    last = pe.matmul(o[:, :], raw[:, 512 * k + P * n:512 * k + P * (n + 1)],
                                     raw[:, 2048 + 512 * k:2048 + 512 * (k + 1)], start=(k == 0), stop=(k == KC - 1))
                filled((name, n), last)

            fold_qk = lambda n: fold0("Wqk", n, STG[:, 4096:8192], fold0_in[0])
            fold_vo = lambda n: fold0("Wvo", n, STG[:, 0:4096], fold0_in[1])
            scores0(0)
            keys0(2)
            fold_qk(0)
            scores0(1)
            keys0(3)
            probs0_transposed(0)
            fold_qk(1)
            fold_qk(2)
            values0(0)
            scores0(2)
            probs0_transposed(1)
            fold_qk(3)
            values0(1)
            scores0(3)
            probs0_transposed(2)
            fold_vo(0)
            fold_vo(1)
            values0(2)
            probs0_transposed(3)
            fold_vo(2)
            fold_vo(3)
            values0(3)
            for t in range(T):
                pe.wait_ge(*emptied(("O", G0 - 1, t // 2)))
                to_features("TO", t, lambda j: otok[:, t, P * j:P * (j + 1)])
            pe.wait_ge(wout_split, 1)
            for t in range(T):
                pe.wait_ge(*emptied(("TO", t)))
                o = begin(("y0", t))
                for k in range(KC):
                    last = three(o[:, :], [xt[:, s, k, P * t:P * (t + 1)] for s in (0, 1)],
                                 [wout[:, s, k, :] for s in (0, 1)], k == 0, k == KC - 1)
                filled(("y0", t), last)

            for t in range(T):
                pe.wait_ge(normed, T + t + 1)
            for c in range(KC):
                to_features("T1", c, lambda j: nx[:, j, P * c:P * (c + 1)])
            for n in range(KC):
                pe.wait_ge(*emptied(("Wqk", n)))
            pe.wait_ge(xt1_split, KC)
            for m in range(KC):
                o = begin(("t", m))
                for k in range(KC):
                    last = three(o[:, :], [wqk[:, s, k, P * m:P * (m + 1)] for s in (0, 1)],
                                 [xt[:, s, k, :] for s in (0, 1)], k == 0, k == KC - 1)
                filled(("t", m), last)
            for m in range(KC):
                pe.wait_ge(*emptied(("t", m)))
            o = begin(("s1",))
            for t in range(T):
                for k in range(KC):
                    last = pe.matmul(o[:, P * t:P * (t + 1)], tt[:, k, P * t:P * (t + 1)], xf[:, k, P * t:P * (t + 1)],
                                     start=(k == 0), stop=(k == KC - 1))
            filled(("s1",), last)
            pe.wait_ge(fc_summed, 4)
            o = begin(("wf",))
            filled(("wf",), pe.matmul(o[:, 0:4], ones, parts[:, 0:4], start=True, stop=True))
            for n in range(KC):
                pe.wait_ge(*emptied(("Wvo", n)))
            for t in range(T):
                o = begin(("v", t))
                for k in range(KC):
                    last = three(o[:, :], [xt[:, s, k, P * t:P * (t + 1)] for s in (0, 1)],
                                 [wvo[:, s, k, :] for s in (0, 1)], k == 0, k == KC - 1)
                filled(("v", t), last)
            pe.wait_ge(p1_exp, 1)
            o = begin(("pt1",))
            for t in range(T):
                last = pe.transpose(o[:, P * t:P * (t + 1)], P1[:, P * t:P * (t + 1)], ident)
            filled(("pt1",), last)
            pe.wait_ge(*emptied(("pt1",)))
            for t in range(T):
                pe.wait_ge(*emptied(("v", t)))
                o = begin(("y1", t))
                filled(("y1", t), pe.matmul(o[:, :], PT1[:, P * t:P * (t + 1)], vf[:, t, :], start=True, stop=True))

            for t in range(T):
                pe.wait_ge(normed, 2 * T + t + 1)
                to_features("T2", t, lambda j: nx[:, t, P * j:P * (j + 1)])

            def up0(t):
                pe.wait_ge(*emptied(("T2", t)))
                for n in range(NFB):
                    o = begin(("fc", t, n))
                    for k in range(KC):
                        if t == 0:
                            pe.wait_ge(fc_signed, k + 1)
                        for s in (0, 1):
                            last = pe.matmul(o[:, :], xt[:, s, k, P * t:P * (t + 1)], fct[:, k, 512 * n:512 * (n + 1)],
                                             start=(k == 0 and s == 0), stop=(k == KC - 1 and s == 1))
                    filled(("fc", t, n), last)

            def hidden_transposed(t):
                pe.wait_ge(h_quant, t + 1)
                for j in range(4):
                    o = begin(("TH", t, j))
                    for i in range(4):
                        f = 4 * j + i
                        last = pe.transpose(o[:, P * i:P * (i + 1)], hb[:, t % 2, P * f:P * (f + 1)], ident)
                    filled(("TH", t, j), last)

            def down0(t):
                o = begin(("y2", t))
                for f in range(F0 // P):
                    if f % 4 == 0:
                        pe.wait_ge(*emptied(("TH", t, f // 4)))
                        if t == 0:
                            pe.wait_ge(pj_signed, f // 4 + 1)
                    for s in (0, 1):
                        last = pe.matmul(o[:, :], ht[:, t % 2, s, f, :], pjt[:, f, :],
                                         start=(f == 0 and s == 0), stop=(f == F0 // P - 1 and s == 1))
                filled(("y2", t), last)

            up0(0)
            up0(1)
            pe.wait_ge(pj_summed, 4)
            o = begin(("wp",))
            filled(("wp",), pe.matmul(o[:, 0:4], ones, parts[:, 4:8], start=True, stop=True))
            hidden_transposed(0)
            down0(0)
            up0(2)
            hidden_transposed(1)
            down0(1)
            up0(3)
            hidden_transposed(2)
            down0(2)
            hidden_transposed(3)
            down0(3)

            pe.wait_ge(kv_roped, 1)
            for j in range(4):
                o = begin(("kn", j))
                for i in range(4):
                    at = P * (4 * j + i)
                    last = pe.transpose(o[:, P * i:P * (i + 1)], kv_raw[:, at:at + P], ident)
                filled(("kn", j), last)

            def fold1(g, step):
                if step == 0:
                    pe.wait_ge(group_in[g], 32)
                    o = begin(("w12", g))
                    for h in range(HG):
                        for k in range(3):
                            last = pe.matmul(o[:, R1 * h:R1 * (h + 1)], kcq[:, h, k, :], wqr[:, h, k, :],
                                             start=(k == 0), stop=(k == 2))
                    filled(("w12", g), last)
                elif step < 3:
                    i = step - 1
                    pe.wait_ge(*emptied(("w12", g)))
                    o = begin(("w3", g, i))
                    for c in (2 * i, 2 * i + 1):
                        for h in range(HG):
                            at = 256 * (c % 2) + R1 * h
                            last = pe.matmul(o[:, at:at + R1], wq1[:, h, P * c:P * (c + 1)], w12[:, R1 * h:R1 * (h + 1)],
                                             start=True, stop=True)
                    filled(("w3", g, i), last)
                else:
                    h = step - 3
                    o = begin(("wo2", g, h))
                    last = pe.matmul(o[:, :], kckv[:, h, :], woT[:, h, :], start=True, stop=True)
                    filled(("wo2", g, h), last)

            for step in range(7):
                fold1(0, step)
            for t in range(T):
                pe.wait_ge(normed, 3 * T + t + 1)
                to_features("T3", t, lambda j: nx[:, t, P * j:P * (j + 1)])

            def attention1(g):
                for i in (0, 1):
                    pe.wait_ge(*emptied(("w3", g, i)))
                for t in range(T):
                    pe.wait_ge(*emptied(("T3", t)))
                for i in (0, 1):
                    o = begin(("qr", g, i))
                    for k in range(KC):
                        last = three(o[:, :], [w3[:, s, k, P * i:P * (i + 1)] for s in (0, 1)],
                                     [xt[:, s, k, :] for s in (0, 1)], k == 0, k == KC - 1)
                    filled(("qr", g, i), last)
                if g == 0:
                    pe.wait_ge(kr_split, 1)
                for h in range(HG):
                    pe.wait_ge(*emptied(("qr", g, h // 2)))
                    o = begin(("qp", g, h))
                    r = slice(R1 * (h % 2), R1 * (h % 2) + R1)
                    last = three(o[:, :], [kr[r, s, 2 * g + h // 2, :] for s in (0, 1)],
                                 [qr[r, s, h // 2, :] for s in (0, 1)], True, True)
                    filled(("qp", g, h), last)
                for s_ in range(NB + 4):
                    if s_ < NB:
                        b = s_
                        if b == 0:
                            for h in range(HG):
                                pe.wait_ge(*emptied(("qp", g, h)))
                            if g == 0:
                                pe.wait_ge(kvt_split, 1)
                        o = begin(("sc", g, b))
                        for i in (0, 1):
                            last = three(o[:, 256 * i:256 * (i + 1)],
                                         [qp[:, s, b, 2 * i:2 * i + 2, :].rearrange("p h q -> p (h q)") for s in (0, 1)],
                                         [kvt[:, s, b, :] for s in (0, 1)], True, True)
                        filled(("sc", g, b), last)
                    if 0 <= s_ - 2 < NB:
                        b = s_ - 2
                        pe.wait_ge(pw_ready, NB * g + b + 1)
                        o = begin(("ptr", g, b))
                        for i in (0, 1):
                            for k in (0, 1):
                                last = pe.transpose(o[:, 256 * k + P * i:256 * k + P * (i + 1)],
                                                    pw[:, b % 4, i, P * k:P * (k + 1)], ident)
                        filled(("ptr", g, b), last)
                    if s_ >= 4 and s_ % 2 == 0 and (s_ - 4) // 2 < NB // 2:
                        n = (s_ - 4) // 2
                        if g == 0:
                            pe.wait_ge(*emptied(("kn", n)))
                        o = begin(("cc", g, n))
                        for b in (2 * n, 2 * n + 1):
                            pe.wait_ge(*emptied(("ptr", g, b)))
                            for k in (0, 1):
                                last = three(o[:, 256 * (b % 2):256 * (b % 2) + 256], [kvn[:, s, b, k, :] for s in (0, 1)],
                                             [ptw[b % 4][:, s, k, :] for s in (0, 1)], k == 0, k == 1)
                        filled(("cc", g, n), last)
                    if g + 1 < G1 and s_ < 7:
                        fold1(g + 1, s_)
                for h in range(HG):
                    pe.wait_ge(*emptied(("wo2", g, h)))
                for t in range(T):
                    pe.wait_ge(*emptied(("cc", g, t)))
                    o = begin(("y3", g, t))
                    for h in range(HG):
                        last = three(o[:, :], [cc[:, s, h, P * t:P * (t + 1)] for s in (0, 1)],
                                     [wo2[:, g % 2, s, h, :] for s in (0, 1)], h == 0, h == HG - 1)
                    filled(("y3", g, t), last)

            for g in range(G1):
                attention1(g)

            for t in range(T):
                pe.wait_ge(normed, 4 * T + t + 1)
            for c in range(KC):
                to_features("T4", c, lambda j: nx[:, j, P * c:P * (c + 1)])
            for c in range(KC):
                pe.wait_ge(ym_silu, c + 1)
                to_features("TY", c, lambda j: ym[:, c, P * j:P * (j + 1)])

            for t in range(T):
                pe.wait_ge(normed, 5 * T + t + 1)
                to_features("T5", t, lambda j: nx[:, t, P * j:P * (j + 1)])
            pe.wait_ge(agu_split, 1)
            for t in range(T):
                pe.wait_ge(*emptied(("T5", t)))
            o = begin(("lg",))
            for t in range(T):
                for k in range(KC):
                    last = three(o[:, E1 * t:E1 * (t + 1)], [xt[:, s, k, P * t:P * (t + 1)] for s in (0, 1)],
                                 [agu[:, s, 1024 + E1 * k:1024 + E1 * (k + 1)] for s in (0, 1)], k == 0, k == KC - 1)
            filled(("lg",), last)
            for n, x in enumerate((("ug",), ("uu",))):
                o = begin(x)
                for k in range(KC):
                    at = 512 * n + P * k
                    last = three(o[:, :], [agu[:, s, at:at + P] for s in (0, 1)], [xt[:, s, k, :] for s in (0, 1)],
                                 k == 0, k == KC - 1)
                filled(x, last)

            def mask_transposed(k):
                o = begin(("tm", k))
                for t in range(T):
                    last = pe.transpose(o[:, P * t:P * (t + 1)], maskt[:, k, t, :], ident)
                filled(("tm", k), last)

            def base(f, part):
                if part == 0:
                    begin(("gu", f, 0))
                    if f < 2:
                        pe.wait_ge(*emptied(("T5", 2 * f + 1)))
                    pe.wait_ge(ring_split, f + 1)
                o = bank[bank_of[("gu", f, 0)] + part]
                for k in range(KC):
                    at = 512 * part + P * k
                    last = three(o[:, :], [ring[:, f % 3, s, at:at + P] for s in (0, 1)],
                                 [xt[:, s, k, :] for s in (0, 1)], k == 0, k == KC - 1)
                if part == 1:
                    filled(("gu", f, 0), last)

            def expert(f, n):
                begin(("gu", f, n))
                if f == 0:
                    pe.wait_ge(um_split, 2 * n)
                for part in (0, 1):
                    at = 1024 + P * part
                    o = bank[bank_of[("gu", f, n)] + part]
                    w = [ring[:, f % 3, s, at:at + P] for s in (0, 1)]
                    m = [um[:, 2 * (n - 1) + part, s, :] for s in (0, 1)]
                    pe.matmul(o[:, :], w[0], m[0], start=False, stop=False, skip_group_check=True)
                    pe.matmul(o[:, :], w[0], m[1], start=False, stop=False, skip_group_check=True)
                    last = pe.matmul(o[:, :], w[1], m[0], start=False, stop=True, skip_group_check=True)
                filled(("gu", f, n), last)

            def expert_down(f, n):
                pe.wait_ge(hs_split, gates.index((f, n)) + 1)
                o = begin(("z", n)) if f == 0 else psum(("z", n))
                w = [ring[:, f % 3, s, 1280:1408] for s in (0, 1)]
                m = [hs[n - 1][:, s, :] for s in (0, 1)]
                pe.matmul(o[:, :], w[0], m[0], start=(f == 0), stop=False, skip_group_check=True)
                pe.matmul(o[:, :], w[0], m[1], start=False, stop=False, skip_group_check=True)
                last = pe.matmul(o[:, :], w[1], m[0], start=False, stop=(f == NF - 1), skip_group_check=True)
                if f == NF - 1:
                    filled(("z", n), last)
                elif n == 2:
                    last.then_inc(ring_used, 1)

            base(0, 0)
            base(0, 1)
            pe.wait_ge(masks_ready, 1)
            for k in range(4):
                mask_transposed(k)
            for f in range(NF):
                if f + 1 < NF:
                    base(f + 1, 0)
                expert(f, 1)
                if f + 1 < NF:
                    base(f + 1, 1)
                if f > 0:
                    expert_down(f - 1, 2)
                expert(f, 2)
                expert_down(f, 1)
            expert_down(NF - 1, 2)
            for t in range(T):
                if t < 2:
                    pe.wait_ge(um_made, 4)
                    o = psum(("y4", t))
                else:
                    o = begin(("y4", t))
                for f in range(NF):
                    if t == 0 and f % 4 == 0:
                        pe.wait_ge(wd_split, f // 4 + 1)
                    three(o[:, :], [h0t[:, s, f, P * t:P * (t + 1)] for s in (0, 1)],
                          [wdt[:, s, f, :] for s in (0, 1)], f == 0, False)
                if t == 0:
                    pe.wait_ge(z_made, 1)
                    pe.wait_ge(bd_in, 16)
                filled(("y4", t), pe.matmul(o[:, :], hh[0][:, P * t:P * (t + 1)], bd, start=False, stop=True))

        @block.scalar
        def _(act):
            def high(dst, x, done, src=None):
                act.wait_ge(*full(x))
                act.copy(dst, psum(x)[:, :] if src is None else src).then_inc(done, 1)

            def copy_out(dst, x, src=None):
                act.wait_ge(*full(x))
                act.copy(dst, psum(x)[:, :] if src is None else src).then_inc(*freed(x))

            def high_tile(name, t, done):
                high(xt_tiles[:, 0, :, t, :], (name, t), done, psum((name, t))[:, :].rearrange("p (c n) -> p c n", c=KC))

            def key_blocks(g):
                x = ("K", g)
                act.wait_ge(*full(x))
                if g >= 2:
                    act.wait_ge(*full(("S", g - 2, 1)))
                for h in range(4):
                    r = slice(32 * h, 32 * h + 32)
                    last = act.copy(kbd[r, g % 2, :, h, :], psum(x)[r, :].rearrange("p (b k) -> p b k", b=NB))
                last.then_inc(*freed(x))

            act.wait_ge(ssm_in, 16)
            act.activation(ssm[:, 0:2, :, :], ssm[:, 0:2, :, :], ACT.Sigmoid).then_inc(sig_made, 1)
            act.wait_ge(zeroed, 2)
            key_blocks(0)
            key_blocks(1)
            for p in range(4):
                x = ("V", p)
                act.wait_ge(*full(x))
                for b in (0, 1):
                    src = psum(x)[64 * b:64 * b + 64, :].rearrange("p (m h x) -> p m h x", m=8, h=2)
                    for h in (0, 1):
                        last = act.copy(vbd[64 * h:64 * h + 64, :, 2 * p + b, 32 * h:32 * h + 32], src[:, :, h, :])
                last.then_inc(*freed(x))
            act.wait_ge(wq_in, 16)
            act.copy(WQO[:, 0:2048], STG[:, 0:2048]).then_inc(wq_high, 1)
            for t in range(T):
                high_tile("T0", t, xt_high)
            act.wait_ge(wout_in, 16)
            act.copy(WQO[:, 4096:6144], STG[:, 2048:4096]).then_inc(wout_high, 1)
            for m in range(KC):
                copy_out(qt[:, m, :], ("q", m))

            def exp0(g):
                act.wait_ge(s0_ready, g + 1)
                act.activation(pr[:, g % 2, :], pr[:, g % 2, :], ACT.Exp).then_inc(p0_exp, 1)

            def probs_out0(g):
                for i in (0, 1):
                    copy_out(ptb[:, g % 2, 2 * i:2 * i + 2, :, :].rearrange("p t m n -> p (t m n)"), ("PT", g, i))

            def out0(g):
                for i in (0, 1):
                    x = ("O", g, i)
                    act.wait_ge(*full(x))
                    src = psum(x)[:, :].rearrange("p (t m b x) -> p t m b x", t=2, m=2, b=2)
                    for b in (0, 1):
                        r = slice(64 * b, 64 * b + 64)
                        dst = otok[r, 2 * i:2 * i + 2, P * g:P * (g + 1)].rearrange("p t (m x) -> p t m x", m=2)
                        last = act.copy(dst, src[r, :, :, b, :])
                    last.then_inc(*freed(x))

            def fold_high(name, n):
                high((wqk if name == "Wqk" else wvo)[:, 0, n, :], (name, n), fold0_high)

            exp0(0)
            key_blocks(2)
            fold_high("Wqk", 0)
            exp0(1)
            key_blocks(3)
            probs_out0(0)
            fold_high("Wqk", 1)
            fold_high("Wqk", 2)
            out0(0)
            exp0(2)
            probs_out0(1)
            fold_high("Wqk", 3)
            out0(1)
            exp0(3)
            probs_out0(2)
            fold_high("Wvo", 0)
            fold_high("Wvo", 1)
            out0(2)
            probs_out0(3)
            fold_high("Wvo", 2)
            fold_high("Wvo", 3)
            out0(3)
            for t in range(T):
                high_tile("TO", t, ot_high)

            for c in range(KC):
                act.wait_ge(*emptied(("T1", c)))
                act.copy(xt[:, 0, c, :], xf[:, c, :]).then_inc(xt_high, 1)
            for m in range(KC):
                copy_out(tt[:, m, :], ("t", m))
            act.wait_ge(s1_ready, 1)
            act.activation(P1[:, :], P1[:, :], ACT.Exp).then_inc(p1_exp, 1)
            for t in range(T):
                copy_out(vf[:, t, :], ("v", t))
            copy_out(PT1[:, :], ("pt1",))

            def signs(i, rounded, signed, dst):
                act.wait_ge(rounded, i + 1)
                act.activation(dst[:, 2048 * i:2048 * (i + 1)], stg4[:, i, :], ACT.Sign, bias=minus_magic).then_inc(signed, 1)

            for i in range(4):
                signs(i, fc_rounded, fc_signed, FCT)
            for t in range(T):
                high_tile("T2", t, xt_high)

            def gelu(t):
                for n in range(NFB):
                    x = ("fc", t, n)
                    act.wait_ge(*full(x))
                    act.activation(hb[:, t % 2, 512 * n:512 * (n + 1)], psum(x)[:, :], ACT.Gelu,
                                   scale=wtot[:, 2:3]).then_inc(*freed(x))

            def norm_hidden(t):
                act.wait_ge(h_scales, t + 1)
                u = 8 * (t % 2)
                act.activation(hb[:, t % 2, :], hb[:, t % 2, :], ACT.Identity, scale=hsc[:, u:u + 1],
                               bias=hsc[:, u + 1:u + 2]).then_inc(h_normed, 1)

            def hidden_high(t):
                for j in range(4):
                    high(ht[:, t % 2, 0, 4 * j:4 * j + 4, :].rearrange("p f n -> p (f n)"), ("TH", t, j), ht_high)

            gelu(0)
            norm_hidden(0)
            gelu(1)
            for i in range(4):
                signs(i, pj_rounded, pj_signed, PJT)
            hidden_high(0)
            norm_hidden(1)
            gelu(2)
            hidden_high(1)
            norm_hidden(2)
            gelu(3)
            hidden_high(2)
            norm_hidden(3)
            act.wait_ge(kv_roped, 1)
            act.copy(KVT[:, 0:2048], kv_raw).then_inc(kvt_high, 1)
            hidden_high(3)

            act.wait_ge(*full(("y2", 3)))
            act.wait_ge(kr_in, 16)
            act.copy(KR[:, 0:1024], kr_raw).then_inc(kr_high, 1)
            for j in range(4):
                high(kvn[:, 0, 2 * j:2 * j + 2, :, :].rearrange("p b k d -> p (b k d)"), ("kn", j), kvn_high)

            def fold1_high(g, step):
                if step == 0:
                    copy_out(w12, ("w12", g), psum(("w12", g))[:, 0:256])
                elif step < 3:
                    i = step - 1
                    high(w3[:, 0, 2 * i:2 * i + 2, :].rearrange("p c r -> p (c r)"), ("w3", g, i), w3_high)
                else:
                    high(wo2[:, g % 2, 0, step - 3, :], ("wo2", g, step - 3), wo2_high)

            for step in range(7):
                fold1_high(0, step)
            for t in range(T):
                high_tile("T3", t, xt_high)
            for g in range(G1):
                for i in (0, 1):
                    high(qr[:, 0, i, :], ("qr", g, i), qr_high)
                for h in range(HG):
                    high(qp[:, 0, :, h, :], ("qp", g, h), qp_high,
                         psum(("qp", g, h))[:, :].rearrange("p (b q) -> p b q", b=NB))
                for s in range(NB + 4):
                    if 0 <= s - 2 < NB:
                        b = s - 2
                        if b >= 4:
                            act.wait_ge(*full(("cc", g, (b - 4) // 2)))
                        high(ptw[b % 4][:, 0, :, :].rearrange("p k n -> p (k n)"), ("ptr", g, b), ptw_high)
                    if s < NB:
                        b = s
                        u = 16 * (b % 4)
                        x = ("sc", g, b)
                        act.wait_ge(max_made, NB * g + b + 1)
                        act.activation(pw[:, b % 4, 0, :], psum(x)[:, 0:256], ACT.Exp, bias=mxs[:, u:u + 1],
                                       accum_out=mxs[:, u + 2:u + 3]).then_inc(sums_made, 1)
                        act.activation(pw[:, b % 4, 1, :], psum(x)[:, 256:512], ACT.Exp, bias=mxs[:, u + 1:u + 2],
                                       accum_out=mxs[:, u + 3:u + 4]).then_inc(*freed(x))
                    if s >= 4 and s % 2 == 0 and (s - 4) // 2 < NB // 2:
                        n = (s - 4) // 2
                        high(cc[:, 0, :, P * n:P * (n + 1)].rearrange("p h (b q) -> p b h q", b=2), ("cc", g, n), cc_high,
                             psum(("cc", g, n))[:, :].rearrange("p (b h q) -> p b h q", b=2, h=HG))
                    if g + 1 < G1 and s < 7:
                        fold1_high(g + 1, s)

            for c in range(KC):
                copy_out(xm[:, c, :], ("T4", c))
            act.wait_ge(agu_in, 16)
            act.copy(agu[:, 0, :], STG[:, 6144:7200]).then_inc(agu_high, 1)

            def chunk_high(f):
                act.wait_ge(ring_in[f % 2], 16 * (f // 2 + 1))
                if f >= 3:
                    act.wait_ge(ring_used, f - 2)
                act.copy(ring[:, f % 3, 0, :], STG[:, 2048 * (f % 2):2048 * (f % 2) + CH]).then_inc(ring_high, 1)

            chunk_high(0)
            chunk_high(1)
            for c in range(KC):
                act.wait_ge(ym_made, c + 1)
                act.activation(ym[:, c, :], ym[:, c, :], ACT.Silu).then_inc(ym_silu, 1)
            for t in range(T):
                high_tile("T5", t, xt_high)
            copy_out(rt[:, 0, :, :], ("lg",), psum(("lg",))[:, 0:T * E1].rearrange("p (t e) -> p t e", t=T))
            act.wait_ge(rt_ready, 1)
            act.activation(rt[:, 0, :, :], rt[:, 0, :, :], ACT.Exp).then_inc(rt_exp, 1)

            def gate(k):
                x = ("gu",) + gates[k]
                act.wait_ge(*full(x))
                if k == 1:
                    act.wait_ge(um_split, 3)
                if k >= 2:
                    act.wait_ge(*emptied(("gu",) + gates[k - 2]))
                act.activation(sg[k % 2], psum(x)[:, :], ACT.Silu).then_inc(silu_made, 1)

            def gated_high(k):
                f, n = gates[k]
                act.wait_ge(*emptied(("gu", f, n)))
                act.copy(h0t[:, 0, f, :] if n == 0 else hs[n - 1][:, 0, :], hh[k % 2]).then_inc(hs_high, 1)

            gate(0)
            gated_high(0)
            for k in range(4):
                copy_out(mk[:, k, :], ("tm", k))
            for k in range(4):
                act.wait_ge(um_made, k + 1)
                act.copy(um[:, k, 0, :], (sg[1], hh[1])[k % 2]).then_inc(um_high, 1)
            chunk_high(2)
            for k in range(1, len(gates)):
                f, n = gates[k]
                gate(k)
                if k >= 2:
                    gated_high(k - 1)
                if n == 1 and 1 <= f < NF - 2:
                    chunk_high(f + 2)
            gated_high(len(gates) - 1)
            for j in range(3):
                n = 512 * min(4, NF - 4 * j)
                act.wait_ge(wd_in[j], 16)
                act.copy(WDT[:, 2048 * j:2048 * j + n], STG[:, 2048 * (j % 2):2048 * (j % 2) + n]).then_inc(wd_high, 1)

        @block.vector
        def _(dve):
            link = in_order(dve, dve_step)

            def low(dst, x, high_done, count, high, src=None):
                dve.wait_ge(high_done, count)
                dve.tensor_tensor(dst, psum(x)[:, :] if src is None else src, high.bitcast(F32),
                                  ALU.subtract).then_inc(*freed(x))

            def low_tile(name, t, high_done, count):
                low(xt_tiles[:, 1, :, t, :], (name, t), high_done, count, xt_tiles[:, 0, :, t, :],
                    psum((name, t))[:, :].rearrange("p (c n) -> p c n", c=KC))

            def rsqrt(n):
                v, y, s = var2[:, 0:n], rs[:, 0:n], rs_t[:, 0:n]
                link(dve.tensor_scalar(s.bitcast(I32), v.bitcast(I32), 1, None, ALU.logical_shift_right))
                link(dve.tensor_scalar(y.bitcast(I32), s.bitcast(I32), -1.0, RSQRT_SEED, ALU.mult, ALU.add))
                for _ in range(3):
                    link(dve.tensor_tensor(s, y, y, ALU.mult))
                    link(dve.scalar_tensor_tensor(out=s, in0=s, scalar=-0.5, in1=v, op0=ALU.mult, op1=ALU.mult))
                    link(dve.scalar_tensor_tensor(out=y, in0=s, scalar=1.5, in1=y, op0=ALU.add, op1=ALU.mult))

            def x_stats(t):
                link(dve.bn_stats(stats[:, t, :], x3[:, t, :]))
                dve.bn_aggr(mv[:, t, :], stats[:, t, :]).then_inc(x_stat, 1)

            def scales(first, eps1, eps2=None):
                dve.wait_ge(x_stat, T * (first + 1))
                v = mv[:, :, 1]
                dve.tensor_scalar(var2[:, 0:4], v, eps1, None, ALU.add).then_inc(dve_tick, 1)
                if eps2 is not None:
                    dve.tensor_scalar(var2[:, 4:8], v, 1.0 + eps2, eps1 * eps2, ALU.mult, ALU.add).then_inc(dve_tick, 1)
                ticks[0] += 1 if eps2 is None else 2
                dve.wait_ge(dve_tick, ticks[0])
                rsqrt(4 if eps2 is None else 8)

            def normalise(dst, at):
                for t in range(T):
                    dve.tensor_scalar(dst[:, t, :], x3[:, t, :], mv[:, t, 0:1], rs[:, at + t:at + t + 1],
                                      ALU.subtract, ALU.mult).then_inc(normed, 1)

            def add_to_x(x, t):
                dve.wait_ge(*full(x))
                dve.tensor_tensor(x3[:, t, :], x3[:, t, :], psum(x)[:, :], ALU.add).then_inc(*freed(x))
                dve.wait_ge(*emptied(x))

            ticks = [0]

            for t in range(T):
                dve.wait_ge(x_in[t], 16)
                x_stats(t)
            scales(0, 1e-5)
            normalise(n0, 0)
            dve.wait_ge(wq_high, 1)
            dve.tensor_tensor(WQO[:, 2048:4096], STG[:, 0:2048], WQO[:, 0:2048].bitcast(F32), ALU.subtract).then_inc(wq_split, 1)
            for t in range(T):
                low_tile("T0", t, xt_high, t + 1)
            dve.wait_ge(wout_high, 1)
            dve.tensor_tensor(WQO[:, 6144:8192], STG[:, 2048:4096], WQO[:, 4096:6144].bitcast(F32),
                              ALU.subtract).then_inc(wout_split, 1)

            dve.wait_ge(sig_made, 1)
            w, q = sw[:, 1, :, :], sw[:, 2, :, :]
            link(dve.tensor_tensor(sw[:, 0, :, :], ssm[:, 0, :, :], ssm[:, 1, :, :], ALU.mult))
            link(dve.tensor_tensor(w, sw[:, 0, :, :], ssm[:, 2, :, :], ALU.mult))
            link(dve.scalar_tensor_tensor(out=w, in0=w, scalar=NSSM ** -0.5, in1=ssm[:, 3, :, :], op0=ALU.mult, op1=ALU.mult))
            link(dve.tensor_scalar(q, sw[:, 0, :, :], -1.0, 1.0, ALU.mult, ALU.add))
            for l in range(LAGS):
                link(dve.tensor_reduce(lagw[:, :, l], w, AX_X, ALU.add))
                if l + 1 < LAGS:
                    link(dve.tensor_tensor(w, w, q, ALU.mult))

            def rows16(g):
                return pr[:, g % 2, :].rearrange("p (r k) -> p r k", k=SQ)

            def softmax0_shift(g):
                if g >= 2:
                    dve.wait_ge(*full(("PT", g - 2, 1)))
                nm = nmax0[:, 16 * (g % 2):16 * (g % 2) + 16]
                for i in (0, 1):
                    x = ("S", g, i)
                    dve.wait_ge(*full(x))
                    dve.scalar_tensor_tensor(out=rows16(g)[:, 8 * i:8 * i + 8, :],
                                             in0=psum(x)[:, :].rearrange("p (r k) -> p r k", k=SQ), scalar=HD0 ** -0.5,
                                             in1=mask0.unsqueeze(1).broadcast_to([P, 8, SQ]), op0=ALU.mult,
                                             op1=ALU.add).then_inc(*freed(x))
                    dve.wait_ge(*emptied(x))
                link(dve.tensor_reduce(nm, rows16(g), AX_X, ALU.max, negate=True))
                dve.tensor_tensor(rows16(g), rows16(g), over(nm, SQ), ALU.add).then_inc(s0_ready, 1)

            def softmax0_divide(g):
                sm = rsum0[:, 16 * (g % 2):16 * (g % 2) + 16]
                dve.wait_ge(p0_exp, g + 1)
                link(dve.tensor_reduce(sm, rows16(g), AX_X, ALU.add))
                link(dve.reciprocal(sm, sm))
                dve.tensor_tensor(rows16(g), rows16(g), over(sm, SQ), ALU.mult).then_inc(p0_ready, 1)

            def fold_low(name, n):
                w_ = wqk if name == "Wqk" else wvo
                low(w_[:, 1, n, :], (name, n), fold0_high, n + 1 + (KC if name == "Wvo" else 0), w_[:, 0, n, :])

            softmax0_shift(0)
            softmax0_divide(0)
            fold_low("Wqk", 0)
            softmax0_shift(1)
            fold_low("Wqk", 1)
            fold_low("Wqk", 2)
            softmax0_divide(1)
            softmax0_shift(2)
            fold_low("Wqk", 3)
            softmax0_divide(2)
            softmax0_shift(3)
            fold_low("Wvo", 0)
            fold_low("Wvo", 1)
            softmax0_divide(3)
            fold_low("Wvo", 2)
            fold_low("Wvo", 3)
            for t in range(T):
                low_tile("TO", t, ot_high, t + 1)
            for t in range(T):
                add_to_x(("y0", t), t)
                x_stats(t)

            scales(1, 1e-5, 1e-5)
            normalise(nx, 4)
            link(dve.tensor_tensor(lnb, mv[:, :, 0], rs[:, 0:4], ALU.mult))
            link(dve.tensor_scalar(lna, rs[:, 0:4], 1.0, None, ALU.add))
            for t in range(T):
                link(dve.tensor_scalar(x3[:, t, :], x3[:, t, :], lna[:, t:t + 1], lnb[:, t:t + 1], ALU.mult, ALU.subtract))
            for c in range(KC):
                x = ("T1", c)
                dve.wait_ge(*full(x))
                dve.tensor_scalar(xf[:, c, :], psum(x)[:, :], gammaT[:, c:c + 1], betaT[:, c:c + 1],
                                  ALU.mult, ALU.add).then_inc(*freed(x))
            for c in range(KC):
                dve.wait_ge(*emptied(("T1", c)))
                dve.wait_ge(xt_high, T + c + 1)
                dve.tensor_tensor(xt[:, 1, c, :], xf[:, c, :], xt[:, 0, c, :].bitcast(F32), ALU.subtract).then_inc(xt1_split, 1)
            for i in (2, 3, 0, 1):
                dve.wait_ge(fc_in[i], 16)
                dve.tensor_reduce(parts[:, i:i + 1], stg4[:, i, :], AX_X, ALU.add, apply_absolute_value=True).then_inc(fc_summed, 1)
            p1 = P1[:, :].rearrange("p (t k) -> p t k", t=T)
            dve.wait_ge(*full(("s1",)))
            dve.scalar_tensor_tensor(out=p1, in0=psum(("s1",))[:, :].rearrange("p (t k) -> p t k", t=T), scalar=D ** -0.5,
                                     in1=mask1.unsqueeze(1).broadcast_to([P, T, P]), op0=ALU.mult,
                                     op1=ALU.add).then_inc(*freed(("s1",)))
            dve.wait_ge(*emptied(("s1",)))
            link(dve.tensor_reduce(nmax1[:, 0:4], p1, AX_X, ALU.max, negate=True))
            dve.tensor_tensor(p1, p1, over(nmax1[:, 0:4], P), ALU.add).then_inc(s1_ready, 1)

            def mean_abs(x, at, size):
                dve.wait_ge(*full(x))
                dve.tensor_reduce(wtot[:, at:at + 1], psum(x)[:, 0:4], AX_X, ALU.add).then_inc(*freed(x))
                dve.wait_ge(*emptied(x))
                link(dve.tensor_scalar(wtot[:, at + 2:at + 3], wtot[:, at:at + 1], 1.0 / size, None, ALU.mult))
                link(dve.tensor_scalar(wtot[:, at + 1:at + 2], wtot[:, at + 2:at + 3], 1e-6, None, ALU.add))
                link(dve.reciprocal(wtot[:, at + 3:at + 4], wtot[:, at + 1:at + 2]))

            def round_quarter(i, at, done):
                dve.tensor_scalar(stg4[:, i, :], stg4[:, i, :], wtot[:, at + 3:at + 4], MAGIC, ALU.mult,
                                  ALU.add).then_inc(done, 1)

            mean_abs(("wf",), 0, F0 * D)
            for i in range(4):
                round_quarter(i, 0, fc_rounded)
            dve.wait_ge(p1_exp, 1)
            link(dve.tensor_reduce(rsum1[:, 0:4], p1, AX_X, ALU.add))
            link(dve.reciprocal(rsum1[:, 4:8], rsum1[:, 0:4]))
            for t in range(T):
                x = ("y1", t)
                dve.wait_ge(*full(x))
                dve.scalar_tensor_tensor(out=x3[:, t, :], in0=psum(x)[:, :], scalar=rsum1[:, 4 + t:5 + t], in1=x3[:, t, :],
                                         op0=ALU.mult, op1=ALU.add).then_inc(*freed(x))
                dve.wait_ge(*emptied(x))
                x_stats(t)

            clip = 128.0 - 1e-6

            def quantise(tile, gm, done):
                link(dve.reciprocal(gm[:, 1:2], gm[:, 0:1]))
                link(dve.tensor_scalar(gm[:, 2:3], gm[:, 1:2], 128.0, None, ALU.mult))
                link(dve.tensor_scalar(gm[:, 3:4], gm[:, 0:1], 1.0 / 128.0, None, ALU.mult))
                link(dve.tensor_scalar(tile, tile, gm[:, 2:3], clip, ALU.mult, ALU.min))
                dve.tensor_scalar(tile, tile, -clip, gm[:, 3:4], ALU.max, ALU.mult).then_inc(done, 1)

            scales(2, 1e-5, 1e-6)
            for t in range(T):
                link(dve.tensor_scalar(nx[:, t, :], x3[:, t, :], mv[:, t, 0:1], rs[:, 4 + t:5 + t], ALU.subtract, ALU.mult))
                gm = xabs[:, 4 * t:4 * t + 4]
                link(dve.tensor_reduce(gm[:, 0:1], nx[:, t, :], AX_X, ALU.max, apply_absolute_value=True))
                quantise(nx[:, t, :], gm, normed)
            for t in range(T):
                low_tile("T2", t, xt_high, 2 * T + t + 1)
            for i in range(4):
                dve.wait_ge(pj_in[i], 16)
                dve.tensor_reduce(parts[:, 4 + i:5 + i], stg4[:, i, :], AX_X, ALU.add, apply_absolute_value=True).then_inc(pj_summed, 1)

            def hidden(t):
                u = 8 * (t % 2)
                for n in range(NFB):
                    dve.wait_ge(*emptied(("fc", t, n)))
                    last = dve.bn_stats(hstats[:, t % 2, n, :], hb[:, t % 2, 512 * n:512 * (n + 1)])
                link(last)
                link(dve.bn_aggr(hmv[:, 0:2], hstats[:, t % 2, :, :].rearrange("p n k -> p (n k)")))
                link(dve.tensor_scalar(var2[:, 0:1], hmv[:, 1:2], 1e-6, None, ALU.add))
                rsqrt(1)
                link(dve.tensor_copy(hsc[:, u:u + 1], rs[:, 0:1]))
                dve.scalar_tensor_tensor(out=hsc[:, u + 1:u + 2], in0=hmv[:, 0:1], scalar=-1.0, in1=rs[:, 0:1],
                                         op0=ALU.mult, op1=ALU.mult).then_inc(h_scales, 1)
                dve.wait_ge(h_normed, t + 1)
                gm = hsc[:, u + 4:u + 8]
                link(dve.tensor_reduce(gm[:, 0:1], hb[:, t % 2, :], AX_X, ALU.max, apply_absolute_value=True))
                quantise(hb[:, t % 2, :], gm, h_quant)

            def hidden_low(t):
                for j in range(4):
                    low(ht[:, t % 2, 1, 4 * j:4 * j + 4, :].rearrange("p f n -> p (f n)"), ("TH", t, j), ht_high, 4 * t + j + 1,
                        ht[:, t % 2, 0, 4 * j:4 * j + 4, :].rearrange("p f n -> p (f n)"))

            def out_hidden(t):
                x = ("y2", t)
                dve.wait_ge(*full(x))
                dve.scalar_tensor_tensor(out=x3[:, t, :], in0=psum(x)[:, :], scalar=wtot[:, 10:11], in1=x3[:, t, :],
                                         op0=ALU.mult, op1=ALU.add).then_inc(*freed(x))
                dve.wait_ge(*emptied(x))
                x_stats(t)

            hidden(0)
            mean_abs(("wp",), 8, F0 * D)
            for i in range(4):
                round_quarter(i, 8, pj_rounded)
            hidden_low(0)
            hidden(1)
            out_hidden(0)
            hidden_low(1)
            hidden(2)
            out_hidden(1)
            hidden_low(2)
            hidden(3)
            out_hidden(2)
            hidden_low(3)
            out_hidden(3)

            scales(3, 1e-5)
            normalise(nx, 0)
            for j in range(4):
                s_ = slice(2 * j, 2 * j + 2)
                low(kvn[:, 1, s_, :, :].rearrange("p b k d -> p (b k d)"), ("kn", j), kvn_high, j + 1,
                    kvn[:, 0, s_, :, :].rearrange("p b k d -> p (b k d)"))

            def fold1_low(g, step):
                if 1 <= step < 3:
                    i = step - 1
                    low(w3[:, 1, 2 * i:2 * i + 2, :].rearrange("p c r -> p (c r)"), ("w3", g, i), w3_high, 2 * g + i + 1,
                        w3[:, 0, 2 * i:2 * i + 2, :].rearrange("p c r -> p (c r)"))
                elif step >= 3:
                    h = step - 3
                    low(wo2[:, g % 2, 1, h, :], ("wo2", g, h), wo2_high, HG * g + h + 1, wo2[:, g % 2, 0, h, :])

            for step in range(7):
                fold1_low(0, step)
            for t in range(T):
                low_tile("T3", t, xt_high, 3 * T + t + 1)
            for g in range(G1):
                for i in (0, 1):
                    low(qr[:, 1, i, :], ("qr", g, i), qr_high, 2 * g + i + 1, qr[:, 0, i, :])
                for h in range(HG):
                    low(qp[:, 1, :, h, :], ("qp", g, h), qp_high, HG * g + h + 1, qp[:, 0, :, h, :],
                        psum(("qp", g, h))[:, :].rearrange("p (b q) -> p b q", b=NB))
                for s in range(NB + 4):
                    if 0 <= s - 2 < NB:
                        b = s - 2
                        low(ptw[b % 4][:, 1, :, :].rearrange("p k n -> p (k n)"), ("ptr", g, b), ptw_high, NB * g + b + 1,
                            ptw[b % 4][:, 0, :, :].rearrange("p k n -> p (k n)"))
                    if s < NB:
                        u = 16 * (s % 4)
                        dve.wait_ge(*full(("sc", g, s)))
                        dve.tensor_reduce(mxs[:, u:u + 2], psum(("sc", g, s))[:, :].rearrange("p (i k) -> p i k", i=2),
                                          AX_X, ALU.max, negate=True).then_inc(max_made, 1)
                    if 0 <= s - 1 < NB:
                        b = s - 1
                        u = 16 * (b % 4)
                        dve.wait_ge(*emptied(("sc", g, b)))
                        dve.reciprocal(mxs[:, u + 4:u + 6], mxs[:, u + 2:u + 4]).then_inc(recip_made, 1)
                    if s >= 4 and s % 2 == 0 and (s - 4) // 2 < NB // 2:
                        n = (s - 4) // 2
                        view = [cc[:, k, :, P * n:P * (n + 1)].rearrange("p h (b q) -> p b h q", b=2) for k in (0, 1)]
                        low(view[1], ("cc", g, n), cc_high, T * g + n + 1, view[0],
                            psum(("cc", g, n))[:, :].rearrange("p (b h q) -> p b h q", b=2, h=HG))
                    if g + 1 < G1 and s < 7:
                        fold1_low(g + 1, s)
                for t in range(T):
                    add_to_x(("y3", g, t), t)
                    if g == G1 - 1:
                        x_stats(t)

            scales(4, 1e-5)
            normalise(nx, 0)
            for c in range(KC):
                dve.wait_ge(*emptied(("T4", c)))
                link(dve.tensor_scalar(ym[:, c, :], xm[:, c, :], lagw[:, c, 0:1], None, ALU.mult))
                for l in range(1, LAGS):
                    n = 512 - SQ * l
                    ins = dve.scalar_tensor_tensor(out=ym[:, c, SQ * l:], in0=xm[:, c, 0:n], scalar=lagw[:, c, l:l + 1],
                                                   in1=ym[:, c, SQ * l:], op0=ALU.mult, op1=ALU.add)
                    if l + 1 < LAGS:
                        link(ins)
                ins.then_inc(ym_made, 1)
            for c in range(KC):
                x = ("TY", c)
                dve.wait_ge(*full(x))
                dve.tensor_tensor(x3[:, :, P * c:P * (c + 1)], x3[:, :, P * c:P * (c + 1)],
                                  psum(x)[:, :].rearrange("p (t n) -> p t n", t=T), ALU.add).then_inc(*freed(x))
            for c in range(KC):
                dve.wait_ge(*emptied(("TY", c)))
            for t in range(T):
                x_stats(t)
            scales(5, 1e-5)
            normalise(nx, 0)
            for t in range(T):
                low_tile("T5", t, xt_high, 4 * T + t + 1)

            p_, tmp, first, second = rt[:, 0, :, :], rt[:, 1, :, :], rt[:, 2, :, :], rt[:, 3, :, :]
            m4 = [small[:, 4 * k:4 * k + 4] for k in range(6)]
            dve.wait_ge(*emptied(("lg",)))
            link(dve.tensor_reduce(m4[0], p_, AX_X, ALU.max, negate=True))
            dve.tensor_tensor(p_, p_, over(m4[0], E1), ALU.add).then_inc(rt_ready, 1)
            dve.wait_ge(rt_exp, 1)
            link(dve.tensor_reduce(m4[1], p_, AX_X, ALU.add))
            link(dve.reciprocal(m4[2], m4[1]))
            link(dve.tensor_tensor(p_, p_, over(m4[2], E1), ALU.mult))

            def largest(src, best, onehot):
                link(dve.tensor_reduce(best, src, AX_X, ALU.max))
                link(dve.tensor_tensor(onehot, src, over(best, E1), ALU.is_equal))
                link(dve.tensor_tensor(onehot, onehot, expert_rank.unsqueeze(1).broadcast_to([P, T, E1]), ALU.mult))
                link(dve.tensor_reduce(m4[5], onehot, AX_X, ALU.max))
                link(dve.tensor_tensor(onehot, onehot, over(m4[5], E1), ALU.is_equal))

            largest(p_, m4[3], first)
            link(dve.scalar_tensor_tensor(out=tmp, in0=first, scalar=-2.0, in1=p_, op0=ALU.mult, op1=ALU.add))
            largest(tmp, m4[4], second)
            link(dve.tensor_tensor(tmp, second, first, ALU.subtract))
            masks = []
            for k, src in enumerate((first, tmp, first, second)):
                if k >= 2:
                    link(dve.tensor_tensor(src, src, over(m4[3 + k - 2], E1), ALU.mult))
                last = dve.tensor_scalar(maskt[:, k, :, :].rearrange("p t (e r) -> p (t e) r", r=R),
                                         over(src.rearrange("p t e -> p (t e)"), R), 2.0, None, ALU.mult)
                if k < 3:
                    link(last)
            last.then_inc(masks_ready, 1)

            def gated(k):
                x = ("gu",) + gates[k]
                dve.wait_ge(silu_made, k + 1)
                if k == 1:
                    dve.wait_ge(um_split, 4)
                if k >= 2:
                    dve.wait_ge(hs_split, k - 1)
                dve.tensor_tensor(hh[k % 2], sg[k % 2], bank[bank_of[x] + 1][:, :], ALU.mult).then_inc(*freed(x))

            def gated_low(k):
                f, n = gates[k]
                dst = h0t[:, :, f, :] if n == 0 else hs[n - 1]
                dve.wait_ge(*emptied(("gu", f, n)))
                dve.wait_ge(hs_high, k + 1)
                dve.tensor_tensor(dst[:, 1, :], hh[k % 2], dst[:, 0, :].bitcast(F32), ALU.subtract).then_inc(hs_split, 1)

            gated(0)
            gated_low(0)
            um_tile = (sg[1], hh[1])

            def um_low(k):
                dve.wait_ge(um_made, k + 1)
                dve.wait_ge(um_high, k + 1)
                dve.tensor_tensor(um[:, k, 1, :], um_tile[k % 2], um[:, k, 0, :].bitcast(F32), ALU.subtract).then_inc(um_split, 1)

            for k in range(4):
                x = ("ug",) if k % 2 == 0 else ("uu",)
                dve.wait_ge(*full(x))
                dve.wait_ge(*emptied(("tm", k // 2)))
                if k == 0:
                    dve.wait_ge(*full(("tm", 3)))
                if k >= 2:
                    um_low(k - 2)
                    dve.wait_ge(um_split, k - 1)
                ins = dve.tensor_tensor(um_tile[k % 2], psum(x)[:, :], mk[:, k // 2, :], ALU.mult)
                ins.then_inc(um_made, 1)
            um_low(2)
            um_low(3)
            for k in range(1, len(gates)):
                gated(k)
                if k >= 2:
                    gated_low(k - 1)
            gated_low(len(gates) - 1)
            dve.wait_ge(hs_split, len(gates))
            for n in (1, 2):
                dve.wait_ge(*full(("z", n)))
                dve.wait_ge(*emptied(("tm", 1 + n)))
                dve.tensor_tensor(hh[n - 1], psum(("z", n))[:, :], mk[:, 1 + n, :], ALU.mult).then_inc(*freed(("z", n)))
            for n in (1, 2):
                dve.wait_ge(*emptied(("z", n)))
            dve.tensor_tensor(hh[0], hh[0], hh[1], ALU.add).then_inc(z_made, 1)
            for t in range(T):
                x = ("y4", t)
                dve.wait_ge(*full(x))
                dve.tensor_tensor(x3[:, t, :], x3[:, t, :], psum(x)[:, :], ALU.add).then_inc(x_final, 1)

        @block.gpsimd
        def _(pool):
            link = in_order(pool, pool_step)
            pool.memset(KBD[:, :], 0.0).then_inc(zeroed, 1)
            pool.memset(VBD[:, :], 0.0).then_inc(zeroed, 1)
            eight = lambda ap: ap.rearrange("p (b l) -> p b l", b=NB)
            pool.wait_ge(kv1_in, 16)
            link(pool.tensor_tensor(eight(kv_raw), eight(kv_raw), cos_t.unsqueeze(1).broadcast_to([P, NB, SK]), ALU.mult))
            link(pool.tensor_tensor(eight(kv_rot), eight(kv_rot), sin_t.unsqueeze(1).broadcast_to([P, NB, SK]), ALU.mult))
            pool.tensor_tensor(kv_raw, kv_raw, kv_rot, ALU.add).then_inc(kv_roped, 1)
            pool.wait_ge(kvt_high, 1)
            pool.tensor_tensor(KVT[:, 2048:4096], kv_raw, KVT[:, 0:2048].bitcast(F32), ALU.subtract).then_inc(kvt_split, 1)
            pool.wait_ge(kr_high, 1)
            pool.tensor_tensor(KR[:, 1024:2048], kr_raw, KR[:, 0:1024].bitcast(F32), ALU.subtract).then_inc(kr_split, 1)
            for n in range(NB * G1):
                b = n % NB
                u = 16 * (b % 4)
                pool.wait_ge(recip_made, n + 1)
                for i in (0, 1):
                    last = pool.tensor_scalar(pw[:, b % 4, i, :], pw[:, b % 4, i, :], mxs[:, u + 4 + i:u + 5 + i], None, ALU.mult)
                last.then_inc(pw_ready, 1)
            pool.wait_ge(agu_high, 1)
            pool.tensor_tensor(agu[:, 1, :], STG[:, 6144:7200], agu[:, 0, :].bitcast(F32), ALU.subtract).then_inc(agu_split, 1)
            for f in range(NF):
                pool.wait_ge(ring_high, f + 1)
                pool.tensor_tensor(ring[:, f % 3, 1, :], STG[:, 2048 * (f % 2):2048 * (f % 2) + CH],
                                   ring[:, f % 3, 0, :].bitcast(F32), ALU.subtract).then_inc(ring_split, 1)
            for j in range(3):
                n = 512 * min(4, NF - 4 * j)
                at = 2048 * j
                pool.wait_ge(wd_high, j + 1)
                pool.tensor_tensor(WDT[:, NF * 512 + at:NF * 512 + at + n], STG[:, 2048 * (j % 2):2048 * (j % 2) + n],
                                   WDT[:, at:at + n].bitcast(F32), ALU.subtract).then_inc(wd_split, 1)


def _constants():
    c = np.zeros((P, 465), np.float32)
    c[:, 0:128] = np.eye(P)
    row, key = np.arange(P)[:, None], np.arange(P)[None, :]
    c[:, 128:192] = np.where(key[:, :SQ] <= row % SQ, 0.0, HIDDEN)
    c[:, 192:320] = np.where((row // SQ == key // SQ) & (key <= row), 0.0, HIDDEN)
    c[:, 328:456] = 1.0
    c[:, 456:464] = np.arange(E1, 0, -1)
    c[:, 464] = -MAGIC
    return c


def _rope_tables():
    inv = (np.float32(1.0) / np.float32(10000.0) ** (np.arange(0, DCTX, 2, dtype=np.float32) / np.float32(DCTX))).astype(np.float32)
    freqs = np.arange(SK, dtype=np.float32)[:, None] * inv[None, :]
    sin, cos = np.repeat(np.sin(freqs), 2, axis=-1).T, np.repeat(np.cos(freqs), 2, axis=-1).T
    sign = np.where(np.arange(DCTX) < DCTX // 2, -1.0, 1.0).astype(np.float32)[:, None]
    return np.concatenate([cos, sin * sign], axis=1).astype(np.float32)


def _layout(i):
    def chunks(w):
        return w.reshape(-1, P, w.shape[1]).transpose(1, 0, 2).reshape(P, -1)

    def cat(*parts):
        return np.concatenate([p.reshape(P, -1) for p in parts], axis=1)

    ctx = i["ctx_512"]
    ctx_t = ctx.reshape(-1, DCTX).T
    consts = _constants()
    consts[:, 320:324] = i["L0_attn_gamma"].reshape(KC, P).T
    consts[:, 324:328] = i["L0_attn_beta"].reshape(KC, P).T
    qkv = i["L0_attn_qkv"]
    half = DCTX // 2
    kcq = i["L1_xattn_w_kc_q"].reshape(H1, P, 3, P).transpose(3, 0, 2, 1)
    wqr = i["L1_xattn_W_qr"].reshape(H1, 3, P, R1).transpose(2, 0, 1, 3)
    wq1 = i["L1_xattn_Wq"].reshape(H1, P, D).transpose(1, 0, 2)
    kckv = i["L1_xattn_w_kc_kv"].transpose(1, 0, 2)
    wo1 = i["L1_xattn_Wo"].T.reshape(H1, P, D).transpose(1, 0, 2)
    heads = lambda w, g: w[:, HG * g:HG * (g + 1)]
    kr = i["L1_xattn_W_kr"].transpose(0, 2, 1).reshape(H1 // 2, 2 * R1, DCTX).transpose(1, 0, 2)
    agu = [i[n].reshape(E1 * R, D).T for n in ("L1_ffn_Ag", "L1_ffn_Au")]
    bgu = [i[n].transpose(0, 2, 1).reshape(E1 * R, DFF) for n in ("L1_ffn_Bg", "L1_ffn_Bu")]
    ad = i["L1_ffn_Ad"].reshape(E1 * R, DFF).T

    def mlp(f):
        s = slice(P * f, P * (f + 1))
        return cat(chunks(i["L1_ffn_Wg"][s].T), chunks(i["L1_ffn_Wu"][s].T), bgu[0][:, s], bgu[1][:, s], ad[s])

    laid = {
        "x": i["x"].reshape(NB * SQ, D),
        "kv0": cat(ctx[:, :SQ].reshape(-1, DCTX).T, i["L0_xattn_Wkv_expand"].T),
        "consts": consts,
        "wq": chunks(i["L0_xattn_Wq"].T),
        "wout": chunks(i["L0_xattn_Wout"].T),
        "fold_qk": cat(chunks(qkv[:, :D].T), chunks(qkv[:, D:2 * D].T)),
        "fold_vo": cat(chunks(qkv[:, 2 * D:].T), chunks(i["L0_attn_o_proj"])),
        "fc": chunks(i["L0_ffn_w_fc"].T).reshape(P, 4, 2048).transpose(1, 0, 2),
        "pj": chunks(i["L0_ffn_w_proj"].T).reshape(P, 4, 2048).transpose(1, 0, 2),
        "kv1": cat(ctx_t, np.concatenate([ctx_t[half:], ctx_t[:half]]), _rope_tables()),
        "kr": kr.reshape(P, -1),
        "group_in": np.stack([cat(heads(kcq, g), heads(wqr, g), heads(wq1, g)) for g in range(G1)]),
        "group_out": np.stack([cat(heads(kckv, g), heads(wo1, g)) for g in range(G1)]),
        "ssm": cat(*[chunks(i["L1_attn_" + n].reshape(D, NSSM)) for n in ("delta", "alpha", "beta", "gamma")]),
        "agu": cat(chunks(agu[0]), chunks(agu[1]), chunks(i["L1_ffn_Wr"].T)),
        "mlp": np.stack([mlp(f) for f in range(NF)]),
        "wd": chunks(i["L1_ffn_Wd"].T),
        "bd": i["L1_ffn_Bd"].transpose(0, 2, 1).reshape(E1 * R, D),
    }
    return {n: np.ascontiguousarray(v) for n, v in laid.items()}


def kernel(**inputs):
    import concourse.bacc as bacc
    from concourse.bass_utils import run_bass_kernel_spmd

    laid = _layout({n: np.asarray(v) for n, v in inputs.items()})
    nc = bacc.Bacc("TRN2", target_bir_lowering=False, num_devices=1)
    arrays = {f"in_{n}": v for n, v in laid.items()}
    aps = {n: nc.dram_tensor(f"in_{n}", v.shape, F32, kind="ExternalInput").ap() for n, v in laid.items()}
    out = nc.dram_tensor("out_x", (NB * SQ, D), F32, kind="ExternalOutput").ap()
    perceiver_blocks(nc, aps, out)
    r = run_bass_kernel_spmd(nc, [arrays], core_ids=[0])
    return r.results[0]["out_x"].reshape(NB, SQ, D)
```

```python
from contextlib import ExitStack

import numpy as np

import concourse.bass as bass
from concourse import mybir

F32 = mybir.dt.float32
F32R = mybir.dt.float32r
I32 = mybir.dt.int32
ALU = mybir.AluOpType
ACT = mybir.ActivationFunctionType
AX_X = mybir.AxisListType.X

P = 128
NB, SQ, D = 8, 64, 512
T = NB * SQ // P
KC = D // P
DCTX, SK = 128, 256
H0, HD0 = 16, 32
G0 = 4
F0 = 2048
NFB = F0 // 512
H1, R1 = 16, 64
G1, HG = 4, 4
NSSM, LAGS = 16, NB
DFF, E1, R = 1408, 8, 16
NF = DFF // P
CH = 8 * P + 3 * P
STEPS = NB * G1 + 4
MAGIC = 12582912.0
RSQRT_SEED = float(0x5F3759DF)
HIDDEN = -3.0e38


def psum_plan():
    order = [("K", 0), ("K", 1)] + [("V", p) for p in range(4)]
    order += [("T0", t) for t in range(T)] + [("q", m) for m in range(KC)]
    S = lambda g: [("S", g, 0), ("S", g, 1)]
    PT = lambda g: [("PT", g, 0), ("PT", g, 1)]
    O = lambda g: [("O", g, 0), ("O", g, 1)]
    order += S(0) + [("K", 2), ("Wqk", 0)] + S(1) + [("K", 3)] + PT(0) + [("Wqk", 1), ("Wqk", 2)] + O(0)
    order += S(2) + PT(1) + [("Wqk", 3)] + O(1) + S(3) + PT(2) + [("Wvo", 0), ("Wvo", 1)] + O(2)
    order += PT(3) + [("Wvo", 2), ("Wvo", 3)] + O(3)
    order += [("TO", t) for t in range(T)] + [("y0", t) for t in range(T)]
    order += [("T1", c) for c in range(KC)] + [("t", m) for m in range(KC)] + [("s1",), ("wf",)]
    order += [("v", t) for t in range(T)] + [("pt1",)] + [("y1", t) for t in range(T)]
    order += [("T2", t) for t in range(T)]
    fc = lambda t: [("fc", t, n) for n in range(NFB)]
    TH = lambda t: [("TH", t, j) for j in range(4)]
    order += fc(0) + fc(1) + [("wp",)] + TH(0) + [("y2", 0)] + fc(2) + TH(1) + [("y2", 1)]
    order += fc(3) + TH(2) + [("y2", 2)] + TH(3) + [("y2", 3)]
    order += [("kn", j) for j in range(4)] + [("w12", 0), ("w3", 0, 0), ("w3", 0, 1)]
    order += [("T3", t) for t in range(T)] + [("qr", 0, 0), ("qr", 0, 1)] + [("qp", 0, h) for h in range(HG)]
    for n in range(STEPS):
        order += attention_step(n)
    order += [("T4", t) for t in range(T)] + [("YC", 0)]
    for c in range(KC):
        order += ([("YC", c + 1)] if c + 1 < KC else []) + [("TY", c)]
    bank_of, turn_of, turns = {}, {}, [0] * 8

    def take(x, b):
        turns[b] += 1
        bank_of[x], turn_of[x] = b, turns[b]

    for n, x in enumerate(order):
        take(x, n % 8)
    for x, b in mlp_order():
        take(x, b)
    return bank_of, turn_of


def attention_step(n):
    g, s = n // NB, n % NB
    order = [("sc", g, s)] if n < NB * G1 else []
    if 2 <= n < NB * G1 + 2:
        order.append(("ptr", (n - 2) // NB, (n - 2) % NB))
    if g + 1 < G1:
        order += {1: [("w12", g + 1)], 2: [("w3", g + 1, 0)], 3: [("w3", g + 1, 1)],
                  4: [("qr", g + 1, 0)], 5: [("qr", g + 1, 1)], 6: [("qp", g + 1, 0), ("qp", g + 1, 1)],
                  7: [("qp", g + 1, 2), ("qp", g + 1, 3)]}.get(s, [])
    if s < T and g > 0:
        order.append(("y3", g - 1, s))
    if s >= NB - HG and g < G1:
        order.append(("wo2", g, s - (NB - HG)))
    if n >= 4 and n % 2 == 0:
        pair = (n - 4) // 2
        order.append(("cc", pair // T, pair % T))
    return order


def gate_order():
    order = [(0, 0), (1, 0), (0, 1), (0, 2)]
    for f in range(1, NF):
        order += [(f, 1)] + ([(f + 1, 0)] if f + 1 < NF else []) + [(f, 2)]
    return order


def mlp_order():
    order = [(("T5", t), t) for t in range(T)] + [(("lg",), 4), (("ug",), 6), (("uu",), 7)]
    order += [(("gu", 0, 0), 0), (("gu", 1, 0), 2)] + [(("tm", k), 4 + k % 2) for k in range(4)]
    order += [(("gu", f, n), 2 * (f % 2)) for f, n in gate_order()[2:]]
    order += [(("z", 1), 4), (("z", 2), 5)]
    return order + [(("y4", t), (6, 7, 0, 2)[t]) for t in range(T)]


def perceiver_blocks(nc, a, out):
    bank_of, turn_of = psum_plan()
    ctx = ExitStack()
    with ctx:
        taken = [0]

        def place(name, dt, cols, at):
            with ExitStack() as s:
                if at:
                    s.enter_context(nc.sbuf_tensor("ahead_of_" + name, [P, at], F32))
                taken[0] = max(taken[0], at + cols)
                return s.enter_context(nc.sbuf_tensor(name, [P, cols], dt))

        X = place("X", F32, T * D, 0)
        XT = place("XT", F32R, 2 * KC * 512, 2048)
        CONST = place("CONST", F32, 1536, 6144)
        STG = place("STG", F32, 8192, 7680)
        M = 15872
        QT = place("QT", F32, 2048, M)
        KBD = place("KBD", F32, 4096, M + 2048)
        VBD = place("VBD", F32, 4096, M + 6144)
        OTOK = place("OTOK", F32, 2048, M + 10240)
        N0 = place("N0", F32, 2048, M + 10240)
        PR = place("PR", F32, 2048, M + 12288)
        PTB = place("PTB", F32, 2048, M + 14336)
        KVRAW = place("KVRAW", F32, 1536, M + 14336)
        WQO = place("WQO", F32R, 8192, M + 16384)
        WQKVO = place("WQKVO", F32R, 8192, M + 24576)
        XF = place("XF", F32, 2048, M)
        TT = place("TT", F32, 2048, M + 2048)
        VF = place("VF", F32, 2048, M + 4096)
        P1 = place("P1", F32, 512, M + 6144)
        PT1 = place("PT1", F32, 512, M + 6656)
        NX = place("NX", F32, 2048, M + 12288)
        HB = place("HB", F32, 4096, M)
        HT = place("HT", F32R, 8192, M + 4096)
        FCT = place("FCT", F32R, 8192, M + 16384)
        PJT = place("PJT", F32R, 8192, M + 24576)
        QP = [place("QP0", F32R, 4096, M), place("QP1", F32R, 4096, M + 26624)]
        PW = place("PW", F32, 2048, M + 4096)
        KR = place("KR", F32R, 2048, M + 6144)
        KVN = place("KVN", F32R, 4096, M + 8192)
        CC = place("CC", F32R, 4096, M + 12288)
        W3 = place("W3", F32R, 2048, M + 16384)
        QR = place("QR", F32R, 2048, M + 18432)
        PTW = [place("PTW0", F32R, 2048, M + 20480), place("PTW1", F32R, 2048, M + 30720)]
        WO2 = place("WO2", F32R, 4096, M + 22528)
        KVT = place("KVT", F32R, 4096, M + 32768)
        KVF = place("KVF", F32, 2048, M + 14336)
        KVROT = place("KVROT", F32, 2048, M + 32768)
        ROPE = place("ROPE", F32, 512, M + 34816)
        LAGH = place("LAGH", F32R, 4096, M)
        LAGL = place("LAGL", F32R, 4096, M + 32768)
        YM = place("YM", F32, 2048, M + 4096)
        LAGS_RAW = place("LAGS_RAW", F32, 512, M + 35328)
        H0T = place("H0T", F32R, 2 * NF * 512, M)
        UM = place("UM", F32R, 4096, M + 11264)
        HS0 = place("HS0", F32R, 1024, M + 15360)
        HS1 = place("HS1", F32R, 1024, M + 16384)
        RING = place("RING", F32R, 3 * 2 * CH, M + 17408)
        WDT = place("WDT", F32R, 2 * NF * 512, M + 25856)
        WDF = place("WDF", F32, NF * 512, M + 25856 + NF * 512)
        AGU = place("AGU", F32R, 2 * 1056, M + 25856)
        MLPF = STG[:, 4096:8192]
        ctx.enter_context(nc.sbuf_tensor("all_phases", [P, taken[0]], F32))

        small = ctx.enter_context(nc.sbuf_tensor("small", [P, 64], F32))
        LAG2 = ctx.enter_context(nc.sbuf_tensor("LAG2", [P, 2 * KC * LAGS], F32R))
        bank = [ctx.enter_context(nc.psum_tensor(f"bank{b}", [P, 512], F32)) for b in range(8)]

        def sem(name):
            return ctx.enter_context(nc.semaphore(name))

        bank_full = [sem(f"bank_full{b}") for b in range(8)]
        bank_free = [sem(f"bank_free{b}") for b in range(8)]

        def psum(x):
            return bank[bank_of[x]]

        def full(x):
            return bank_full[bank_of[x]], turn_of[x]

        def emptied(x):
            return bank_free[bank_of[x]], turn_of[x]

        def freed(x):
            return bank_free[bank_of[x]], 1

        x_in = [sem(f"x_in{t}") for t in range(T)]
        consts_in, kv0_in, wq_in, wout_in, ssm_in = sem("consts_in"), sem("kv0_in"), sem("wq_in"), sem("wout_in"), sem("ssm_in")
        fold0_in = [sem("fold_qk_in"), sem("fold_vo_in")]
        fc_in = [sem(f"fc_in{i}") for i in range(4)]
        pj_in = [sem(f"pj_in{i}") for i in range(4)]
        kv1_in, kr_in, agu_in, bd_in = sem("kv1_in"), sem("kr_in"), sem("agu_in"), sem("bd_in")
        query_in = [sem(f"query_in{g}") for g in range(G1)]
        value_in = [sem(f"value_in{g}") for g in range(G1)]
        ring_in = [sem(f"ring_in{i}") for i in range(2)]
        wd_in = [sem(f"wd_in{j}") for j in range(3)]
        out_done = sem("out_done")
        zeroed = sem("zeroed")
        wq_high, wq_split, wout_high, wout_split = sem("wq_high"), sem("wq_split"), sem("wout_high"), sem("wout_split")
        fold0_high = sem("fold0_high")
        fc_summed, pj_summed = sem("fc_summed"), sem("pj_summed")
        fc_rounded, fc_signed, pj_rounded, pj_signed = sem("fc_rounded"), sem("fc_signed"), sem("pj_rounded"), sem("pj_signed")
        kv_roped, kvt_high, kvt_split, kvn_high = sem("kv_roped"), sem("kvt_high"), sem("kvt_split"), sem("kvn_high")
        kr_high, kr_split = sem("kr_high"), sem("kr_split")
        w3_high, wo2_high = sem("w3_high"), sem("wo2_high")
        agu_high, agu_split = sem("agu_high"), sem("agu_split")
        ring_high, ring_split, ring_used = sem("ring_high"), sem("ring_split"), sem("ring_used")
        wd_high, wd_split = sem("wd_high"), sem("wd_split")
        normed = sem("normed")
        xt_high = sem("xt_high")
        xt1_split = sem("xt1_split")
        s0_ready, p0_exp, p0_ready = sem("s0_ready"), sem("p0_exp"), sem("p0_ready")
        ot_high = sem("ot_high")
        s1_ready, p1_exp = sem("s1_ready"), sem("p1_exp")
        h_scales, h_normed, h_quant, ht_high = sem("h_scales"), sem("h_normed"), sem("h_quant"), sem("ht_high")
        qr_high, qp_high, ptw_high, cc_high = sem("qr_high"), sem("qp_high"), sem("ptw_high"), sem("cc_high")
        max_made, sums_made, recip_made, pw_ready = sem("max_made"), sem("sums_made"), sem("recip_made"), sem("pw_ready")
        exp_made, states_made, lags_made = sem("exp_made"), sem("states_made"), sem("lags_made")
        rates_made, lag_tiles = sem("rates_made"), sem("lag_tiles")
        rt_ready, rt_exp, masks_ready = sem("rt_ready"), sem("rt_exp"), sem("masks_ready")
        um_made, um_high, um_split = sem("um_made"), sem("um_high"), sem("um_split")
        silu_made, hs_high, hs_split, z_made, x_final = sem("silu_made"), sem("hs_high"), sem("hs_split"), sem("z_made"), sem("x_final")
        dve_step, pool_step, dve_tick, x_stat = sem("dve_step"), sem("pool_step"), sem("dve_tick"), sem("x_stat")
        gates = gate_order()

        xt = XT[:, :].rearrange("p (s c n) -> p s c n", s=2, c=KC)
        xt_tiles = XT[:, :].rearrange("p (s c t n) -> p s c t n", s=2, c=KC, t=T)
        x3 = X[:, :].rearrange("p (t d) -> p t d", t=T)
        n0 = N0[:, :].rearrange("p (t d) -> p t d", t=T)
        nx = NX[:, :].rearrange("p (t d) -> p t d", t=T)
        ident = CONST[:, 0:128]
        mask0 = CONST[:, 128:192]
        mask1 = CONST[:, 192:320]
        gammaT, betaT = CONST[:, 320:324], CONST[:, 324:328]
        ones = CONST[:, 328:456]
        expert_rank = CONST[:, 456:464]
        minus_magic = CONST[:, 464:465]
        stats = CONST[:, 480:504].rearrange("p (t k) -> p t k", k=6)
        mv = CONST[:, 504:512].rearrange("p (t k) -> p t k", k=2)
        var2, rs, rs_t = CONST[:, 512:520], CONST[:, 520:528], CONST[:, 528:536]
        lna, lnb = CONST[:, 536:540], CONST[:, 540:544]
        nmax0 = CONST[:, 544:576]
        rsum0 = CONST[:, 576:608]
        parts, wtot = CONST[:, 608:616], CONST[:, 616:632]
        lagw = CONST[:, 640:672].rearrange("p (c l) -> p c l", c=KC)
        nmax1, rsum1 = CONST[:, 672:680], CONST[:, 680:696]
        hstats = CONST[:, 696:744].rearrange("p (u n k) -> p u n k", u=2, k=6)
        hmv = CONST[:, 744:752]
        hsc = CONST[:, 752:768]
        xabs = CONST[:, 768:784]
        mxs = CONST[:, 784:848]
        ssm = CONST[:, 896:1152].rearrange("p (k c n) -> p k c n", k=4, c=KC)
        sw = CONST[:, 1152:1344].rearrange("p (k c n) -> p k c n", k=3, c=KC)
        rt = CONST[:, 1344:1536].rearrange("p (k t e) -> p k t e", k=6, t=T)
        wq = WQO[:, 0:4096].rearrange("p (s c n) -> p s c n", s=2, c=KC)
        wout = WQO[:, 4096:8192].rearrange("p (s c n) -> p s c n", s=2, c=KC)
        wqk = WQKVO[:, 0:4096].rearrange("p (s c n) -> p s c n", s=2, c=KC)
        wvo = WQKVO[:, 4096:8192].rearrange("p (s c n) -> p s c n", s=2, c=KC)
        qt = QT[:, :].rearrange("p (m n) -> p m n", m=KC)
        kbd = KBD[:, :].rearrange("p (u b h k) -> p u b h k", u=2, b=NB, h=4)
        vbd = VBD[:, :].rearrange("p (m b x) -> p m b x", m=8, b=NB)
        otok = OTOK[:, :].rearrange("p (t d) -> p t d", t=T)
        pr = PR[:, :].rearrange("p (u w) -> p u w", u=2)
        ptb = PTB[:, :].rearrange("p (u t m n) -> p u t m n", u=2, t=T, m=2)
        stg4 = STG[:, :].rearrange("p (u w) -> p u w", u=4)
        xf = XF[:, :].rearrange("p (c n) -> p c n", c=KC)
        tt = TT[:, :].rearrange("p (c n) -> p c n", c=KC)
        vf = VF[:, :].rearrange("p (t d) -> p t d", t=T)
        hb = HB[:, :].rearrange("p (u f) -> p u f", u=2)
        ht = HT[:, :].rearrange("p (u s f n) -> p u s f n", u=2, s=2, f=F0 // P)
        fct = FCT[:, :].rearrange("p (c f) -> p c f", c=KC)
        pjt = PJT[:, :].rearrange("p (f d) -> p f d", f=F0 // P)
        kvt = KVT[:, :].rearrange("p (s b l) -> p s b l", s=2, b=NB)
        kvn = KVN[:, :].rearrange("p (s b k d) -> p s b k d", s=2, b=NB, k=2)
        w3 = W3[:, :].rearrange("p (s c r) -> p s c r", s=2, c=KC)
        qr = QR[:, :].rearrange("p (s i n) -> p s i n", s=2, i=2)
        kr = KR[:, :].rearrange("p (s j d) -> p s j d", s=2, j=H1 // 2)
        qp = [t_[:, :].rearrange("p (s b h q) -> p s b h q", s=2, b=NB, h=HG) for t_ in QP]
        pw = PW[:, :].rearrange("p (u i k) -> p u i k", u=4, i=2)
        ptw = [PTW[b // 2][:, 1024 * (b % 2):1024 * (b % 2) + 1024].rearrange("p (s k n) -> p s k n", s=2, k=2) for b in range(4)]
        wo2 = WO2[:, :].rearrange("p (s h d) -> p s h d", s=2, h=HG)
        cc = CC[:, :].rearrange("p (s h n) -> p s h n", s=2, h=HG)
        kv_raw, kv_rot = KVF[:, :], KVROT[:, :]
        cos_t, sin_t = ROPE[:, 0:256], ROPE[:, 256:512]
        kcq = STG[:, 0:1536].rearrange("p (h c k) -> p h c k", h=HG, c=3)
        wqr = STG[:, 1536:2304].rearrange("p (h c r) -> p h c r", h=HG, c=3)
        wq1 = STG[:, 2304:4352].rearrange("p (h c) -> p h c", h=HG)
        kckv = STG[:, 4352:4864].rearrange("p (h d) -> p h d", h=HG)
        woT = STG[:, 4864:6912].rearrange("p (h d) -> p h d", h=HG)
        kr_raw = STG[:, 6912:7936]
        w12 = STG[:, 7936:8192]
        lag2 = LAG2[:, :].rearrange("p (s c l) -> p s c l", s=2, c=KC)
        lags_raw = LAGS_RAW[:, :].rearrange("p (l c n) -> p c l n", l=LAGS, c=KC)
        lag_tile = [t_[:, :].rearrange("p (c l n) -> p c l n", c=KC, l=LAGS) for t_ in (LAGH, LAGL)]
        ym = YM[:, :].rearrange("p (c n) -> p c n", c=KC)
        h0t = H0T[:, :].rearrange("p (s f n) -> p s f n", s=2, f=NF)
        um = UM[:, :].rearrange("p (k s n) -> p k s n", k=4, s=2)
        hs = [t_[:, :].rearrange("p (s n) -> p s n", s=2) for t_ in (HS0, HS1)]
        ring = RING[:, :].rearrange("p (u s w) -> p u s w", u=3, s=2)
        wdt = WDT[:, :].rearrange("p (s f d) -> p s f d", s=2, f=NF)
        agu = AGU[:, :].rearrange("p (s w) -> p s w", s=2)
        sg = [MLPF[:, 0:512], MLPF[:, 512:1024]]
        hh = [MLPF[:, 1024:1536], MLPF[:, 1536:2048]]
        mk = MLPF[:, 2048:4096].rearrange("p (k n) -> p k n", k=4)
        bd = mk[:, 0, :]
        maskt = NX[:, :].rearrange("p (k t e) -> p k t e", k=4, t=T)

        def over(ap, n):
            return ap.unsqueeze(2).broadcast_to([ap.shape[0], ap.shape[1], n])

        def in_order(engine, s):
            done = [0]

            def link(ins):
                done[0] += 1
                ins.then_inc(s, 1)
                engine.wait_ge(s, done[0])
            return link

        block = ctx.enter_context(nc.Block())

        @block.sync
        def _(sp):
            sp.dma_start(x3[:, 0, :], a["x"].rearrange("(t p) d -> t p d", p=P)[0]).then_inc(x_in[0], 16)
            sp.dma_start(KVRAW[:, :], a["kv0"]).then_inc(kv0_in, 16)
            for t in range(1, T):
                sp.dma_start(x3[:, t, :], a["x"].rearrange("(t p) d -> t p d", p=P)[t]).then_inc(x_in[t], 16)
            sp.dma_start(CONST[:, 0:465], a["consts"]).then_inc(consts_in, 16)
            sp.dma_start(STG[:, 0:2048], a["wq"]).then_inc(wq_in, 16)
            sp.dma_start(CONST[:, 896:1152], a["ssm"]).then_inc(ssm_in, 16)
            sp.dma_start(STG[:, 4096:8192], a["fold_qk"]).then_inc(fold0_in[0], 16)
            sp.dma_start(STG[:, 2048:4096], a["wout"]).then_inc(wout_in, 16)
            sp.dma_start(KVROT[:, :], a["kv1"][:, 2048:4096]).then_inc(kv1_in, 16)
            sp.dma_start(ROPE[:, :], a["kv1"][:, 4096:4608]).then_inc(kv1_in, 16)
            sp.wait_ge(wq_split, 1)
            sp.wait_ge(wout_split, 1)
            sp.dma_start(STG[:, 0:4096], a["fold_vo"]).then_inc(fold0_in[1], 16)
            sp.wait_ge(*full(("Wqk", KC - 1)))
            for i in (2, 3):
                sp.dma_start(stg4[:, i, :], a["fc"][i]).then_inc(fc_in[i], 16)
            sp.wait_ge(*full(("O", G0 - 1, 1)))
            sp.dma_start(KVF[:, :], a["kv1"][:, 0:2048]).then_inc(kv1_in, 16)
            sp.wait_ge(*full(("Wvo", KC - 1)))
            for i in (0, 1):
                sp.dma_start(stg4[:, i, :], a["fc"][i]).then_inc(fc_in[i], 16)
            for i in range(4):
                sp.wait_ge(fc_signed, i + 1)
                sp.dma_start(stg4[:, i, :], a["pj"][i]).then_inc(pj_in[i], 16)
            sp.wait_ge(pj_signed, 4)
            sp.dma_start(STG[:, 0:4352], a["queries"][0]).then_inc(query_in[0], 16)
            sp.dma_start(kr_raw, a["kr"]).then_inc(kr_in, 16)
            sp.dma_start(STG[:, 4352:6912], a["values"][0]).then_inc(value_in[0], 16)
            for g in range(1, G1):
                sp.wait_ge(*full(("w3", g - 1, 1)))
                sp.dma_start(STG[:, 0:4352], a["queries"][g]).then_inc(query_in[g], 16)
                if g >= 2:
                    sp.wait_ge(*full(("wo2", g - 2, HG - 1)))
                    sp.dma_start(STG[:, 4352:6912], a["values"][g - 1]).then_inc(value_in[g - 1], 16)
            sp.wait_ge(*full(("wo2", G1 - 2, HG - 1)))
            sp.dma_start(STG[:, 4352:6912], a["values"][G1 - 1]).then_inc(value_in[G1 - 1], 16)
            sp.wait_ge(*full(("wo2", G1 - 1, HG - 1)))
            sp.wait_ge(kr_split, 1)
            sp.dma_start(STG[:, 6144:7200], a["agu"]).then_inc(agu_in, 16)
            for f in range(NF):
                if f >= 2:
                    sp.wait_ge(ring_split, f - 1)
                sp.dma_start(STG[:, 2048 * (f % 2):2048 * (f % 2) + CH], a["mlp"][f]).then_inc(ring_in[f % 2], 16)
                if f in (4, 5, 6):
                    j = f - 4
                    w = slice(2048 * j, 2048 * j + 512 * min(4, NF - 4 * j))
                    sp.dma_start(WDF[:, w], a["wd"][:, w]).then_inc(wd_in[j], 16)
                if f == 2:
                    sp.wait_ge(um_made, 4)
                    sp.dma_start(bd, a["bd"]).then_inc(bd_in, 16)
            for t in range(T):
                sp.wait_ge(x_final, t + 1)
                sp.dma_start(out.rearrange("(t p) d -> t p d", p=P)[t], x3[:, t, :]).then_inc(out_done, 16)
            sp.wait_ge(out_done, 16 * T)

        @block.tensor
        def _(pe):
            def begin(x):
                if turn_of[x] > 1:
                    pe.wait_ge(bank_free[bank_of[x]], turn_of[x] - 1)
                return psum(x)

            def three(o, w, m, start, stop):
                pe.matmul(o, w[0], m[0], start=start, stop=False)
                pe.matmul(o, w[0], m[1], start=False, stop=False)
                return pe.matmul(o, w[1], m[0], start=False, stop=stop)

            def filled(x, last):
                last.then_inc(bank_full[bank_of[x]], 1)

            def to_features(name, i, src):
                o = begin((name, i))
                for j in range(4):
                    last = pe.transpose(o[:, P * j:P * (j + 1)], src(j), ident)
                filled((name, i), last)

            def keys0(g):
                o = begin(("K", g))
                filled(("K", g), pe.matmul(o[:, :], KVRAW[:, 512 + P * g:512 + P * (g + 1)], KVRAW[:, 0:512],
                                           start=True, stop=True))

            pe.wait_ge(kv0_in, 16)
            keys0(0)
            keys0(1)
            for p in range(4):
                o = begin(("V", p))
                filled(("V", p), pe.matmul(o[:, :], KVRAW[:, P * p:P * (p + 1)], KVRAW[:, 1024:1536],
                                           start=True, stop=True))
            pe.wait_ge(consts_in, 16)
            for t in range(T):
                pe.wait_ge(normed, t + 1)
                to_features("T0", t, lambda j: n0[:, t, P * j:P * (j + 1)])
            pe.wait_ge(wq_split, 1)
            for t in range(T):
                pe.wait_ge(*emptied(("T0", t)))
            for m in range(KC):
                o = begin(("q", m))
                for k in range(KC):
                    last = three(o[:, :], [wq[:, s, k, P * m:P * (m + 1)] for s in (0, 1)],
                                 [xt[:, s, k, :] for s in (0, 1)], k == 0, k == KC - 1)
                filled(("q", m), last)

            def scores0(g):
                pe.wait_ge(*emptied(("q", g)))
                pe.wait_ge(*emptied(("K", g)))
                for i in (0, 1):
                    o = begin(("S", g, i))
                    for b in range(4 * i, 4 * i + 4):
                        last = pe.matmul(o[64 * (b % 2):64 * (b % 2) + 64, 256 * (b // 2 % 2):256 * (b // 2 % 2) + 256],
                                         qt[:, g, SQ * b:SQ * (b + 1)],
                                         kbd[:, g % 2, b, :, :].rearrange("p h k -> p (h k)"), start=True, stop=True)
                    filled(("S", g, i), last)

            def probs0_transposed(g):
                pe.wait_ge(p0_ready, g + 1)
                for i in (0, 1):
                    o = begin(("PT", g, i))
                    for t in (0, 1):
                        for m in (0, 1):
                            at = 256 * (2 * i + t) + P * m
                            last = pe.transpose(o[:, 256 * t + P * m:256 * t + P * (m + 1)],
                                                pr[:, g % 2, at:at + P], ident)
                    filled(("PT", g, i), last)

            def values0(g):
                for i in (0, 1):
                    pe.wait_ge(*emptied(("PT", g, i)))
                    for p in (2 * i, 2 * i + 1):
                        pe.wait_ge(*emptied(("V", p)))
                    o = begin(("O", g, i))
                    for t in (0, 1):
                        for m in (0, 1):
                            last = pe.matmul(o[:, 256 * t + P * m:256 * t + P * (m + 1)], ptb[:, g % 2, 2 * i + t, m, :],
                                             vbd[:, 2 * g + m, 2 * (2 * i + t):2 * (2 * i + t) + 2, :]
                                             .rearrange("p b x -> p (b x)"), start=True, stop=True)
                    filled(("O", g, i), last)

            def fold0(name, n, raw, loaded):
                pe.wait_ge(loaded, 16)
                o = begin((name, n))
                for k in range(KC):
                    last = pe.matmul(o[:, :], raw[:, 512 * k + P * n:512 * k + P * (n + 1)],
                                     raw[:, 2048 + 512 * k:2048 + 512 * (k + 1)], start=(k == 0), stop=(k == KC - 1))
                filled((name, n), last)

            fold_qk = lambda n: fold0("Wqk", n, STG[:, 4096:8192], fold0_in[0])
            fold_vo = lambda n: fold0("Wvo", n, STG[:, 0:4096], fold0_in[1])
            scores0(0)
            keys0(2)
            fold_qk(0)
            scores0(1)
            keys0(3)
            probs0_transposed(0)
            fold_qk(1)
            fold_qk(2)
            values0(0)
            scores0(2)
            probs0_transposed(1)
            fold_qk(3)
            values0(1)
            scores0(3)
            probs0_transposed(2)
            fold_vo(0)
            fold_vo(1)
            values0(2)
            probs0_transposed(3)
            fold_vo(2)
            fold_vo(3)
            values0(3)
            for t in range(T):
                pe.wait_ge(*emptied(("O", G0 - 1, t // 2)))
                to_features("TO", t, lambda j: otok[:, t, P * j:P * (j + 1)])
            pe.wait_ge(wout_split, 1)
            for t in range(T):
                pe.wait_ge(*emptied(("TO", t)))
                o = begin(("y0", t))
                for k in range(KC):
                    last = three(o[:, :], [xt[:, s, k, P * t:P * (t + 1)] for s in (0, 1)],
                                 [wout[:, s, k, :] for s in (0, 1)], k == 0, k == KC - 1)
                filled(("y0", t), last)

            for t in range(T):
                pe.wait_ge(normed, T + t + 1)
            for c in range(KC):
                to_features("T1", c, lambda j: nx[:, j, P * c:P * (c + 1)])
            for n in range(KC):
                pe.wait_ge(*emptied(("Wqk", n)))
            pe.wait_ge(xt1_split, KC)
            for m in range(KC):
                o = begin(("t", m))
                for k in range(KC):
                    last = three(o[:, :], [wqk[:, s, k, P * m:P * (m + 1)] for s in (0, 1)],
                                 [xt[:, s, k, :] for s in (0, 1)], k == 0, k == KC - 1)
                filled(("t", m), last)
            for m in range(KC):
                pe.wait_ge(*emptied(("t", m)))
            o = begin(("s1",))
            for t in range(T):
                for k in range(KC):
                    last = pe.matmul(o[:, P * t:P * (t + 1)], tt[:, k, P * t:P * (t + 1)], xf[:, k, P * t:P * (t + 1)],
                                     start=(k == 0), stop=(k == KC - 1))
            filled(("s1",), last)
            pe.wait_ge(fc_summed, 4)
            o = begin(("wf",))
            filled(("wf",), pe.matmul(o[:, 0:4], ones, parts[:, 0:4], start=True, stop=True))
            for n in range(KC):
                pe.wait_ge(*emptied(("Wvo", n)))
            for t in range(T):
                o = begin(("v", t))
                for k in range(KC):
                    last = three(o[:, :], [xt[:, s, k, P * t:P * (t + 1)] for s in (0, 1)],
                                 [wvo[:, s, k, :] for s in (0, 1)], k == 0, k == KC - 1)
                filled(("v", t), last)
            pe.wait_ge(p1_exp, 1)
            o = begin(("pt1",))
            for t in range(T):
                last = pe.transpose(o[:, P * t:P * (t + 1)], P1[:, P * t:P * (t + 1)], ident)
            filled(("pt1",), last)
            pe.wait_ge(*emptied(("pt1",)))
            for t in range(T):
                pe.wait_ge(*emptied(("v", t)))
                o = begin(("y1", t))
                filled(("y1", t), pe.matmul(o[:, :], PT1[:, P * t:P * (t + 1)], vf[:, t, :], start=True, stop=True))

            for t in range(T):
                pe.wait_ge(normed, 2 * T + t + 1)
                to_features("T2", t, lambda j: nx[:, t, P * j:P * (j + 1)])

            def up0(t):
                pe.wait_ge(*emptied(("T2", t)))
                for n in range(NFB):
                    o = begin(("fc", t, n))
                    for k in range(KC):
                        if t == 0:
                            pe.wait_ge(fc_signed, k + 1)
                        for s in (0, 1):
                            last = pe.matmul(o[:, :], xt[:, s, k, P * t:P * (t + 1)], fct[:, k, 512 * n:512 * (n + 1)],
                                             start=(k == 0 and s == 0), stop=(k == KC - 1 and s == 1))
                    filled(("fc", t, n), last)

            def hidden_transposed(t):
                pe.wait_ge(h_quant, t + 1)
                for j in range(4):
                    o = begin(("TH", t, j))
                    for i in range(4):
                        f = 4 * j + i
                        last = pe.transpose(o[:, P * i:P * (i + 1)], hb[:, t % 2, P * f:P * (f + 1)], ident)
                    filled(("TH", t, j), last)

            def down0(t):
                o = begin(("y2", t))
                for f in range(F0 // P):
                    if f % 4 == 0:
                        pe.wait_ge(*emptied(("TH", t, f // 4)))
                        if t == 0:
                            pe.wait_ge(pj_signed, f // 4 + 1)
                    for s in (0, 1):
                        last = pe.matmul(o[:, :], ht[:, t % 2, s, f, :], pjt[:, f, :],
                                         start=(f == 0 and s == 0), stop=(f == F0 // P - 1 and s == 1))
                filled(("y2", t), last)

            up0(0)
            up0(1)
            pe.wait_ge(pj_summed, 4)
            o = begin(("wp",))
            filled(("wp",), pe.matmul(o[:, 0:4], ones, parts[:, 4:8], start=True, stop=True))
            hidden_transposed(0)
            down0(0)
            up0(2)
            hidden_transposed(1)
            down0(1)
            up0(3)
            hidden_transposed(2)
            down0(2)
            hidden_transposed(3)
            down0(3)

            pe.wait_ge(kv_roped, 1)
            for j in range(4):
                o = begin(("kn", j))
                for i in range(4):
                    at = P * (4 * j + i)
                    last = pe.transpose(o[:, P * i:P * (i + 1)], kv_raw[:, at:at + P], ident)
                filled(("kn", j), last)

            def fold_queries(g, step):
                if step == 0:
                    pe.wait_ge(query_in[g], 16)
                    o = begin(("w12", g))
                    for h in range(HG):
                        for k in range(3):
                            last = pe.matmul(o[:, R1 * h:R1 * (h + 1)], kcq[:, h, k, :], wqr[:, h, k, :],
                                             start=(k == 0), stop=(k == 2))
                    filled(("w12", g), last)
                else:
                    i = step - 1
                    pe.wait_ge(*emptied(("w12", g)))
                    o = begin(("w3", g, i))
                    for c in (2 * i, 2 * i + 1):
                        for h in range(HG):
                            at = 256 * (c % 2) + R1 * h
                            last = pe.matmul(o[:, at:at + R1], wq1[:, h, P * c:P * (c + 1)], w12[:, R1 * h:R1 * (h + 1)],
                                             start=True, stop=True)
                    filled(("w3", g, i), last)

            def fold_values(g, h):
                if h == 0:
                    pe.wait_ge(value_in[g], 16)
                o = begin(("wo2", g, h))
                filled(("wo2", g, h), pe.matmul(o[:, :], kckv[:, h, :], woT[:, h, :], start=True, stop=True))

            def queries(g, i):
                for j in (0, 1):
                    pe.wait_ge(*emptied(("w3", g, j)))
                o = begin(("qr", g, i))
                for k in range(KC):
                    last = three(o[:, :], [w3[:, s, k, P * i:P * (i + 1)] for s in (0, 1)],
                                 [xt[:, s, k, :] for s in (0, 1)], k == 0, k == KC - 1)
                filled(("qr", g, i), last)

            def queries_in_context(g, h):
                pe.wait_ge(*emptied(("qr", g, h // 2)))
                o = begin(("qp", g, h))
                r = slice(R1 * (h % 2), R1 * (h % 2) + R1)
                last = three(o[:, :], [kr[r, s, 2 * g + h // 2, :] for s in (0, 1)],
                             [qr[r, s, h // 2, :] for s in (0, 1)], True, True)
                filled(("qp", g, h), last)

            def scores(g, b):
                if b == 0:
                    for h in range(HG):
                        pe.wait_ge(*emptied(("qp", g, h)))
                o = begin(("sc", g, b))
                for i in (0, 1):
                    last = three(o[:, 256 * i:256 * (i + 1)],
                                 [qp[g % 2][:, s, b, 2 * i:2 * i + 2, :].rearrange("p h q -> p (h q)") for s in (0, 1)],
                                 [kvt[:, s, b, :] for s in (0, 1)], True, True)
                filled(("sc", g, b), last)

            def probs_transposed(g, b):
                pe.wait_ge(pw_ready, NB * g + b + 1)
                o = begin(("ptr", g, b))
                for i in (0, 1):
                    for k in (0, 1):
                        last = pe.transpose(o[:, 256 * k + P * i:256 * k + P * (i + 1)],
                                            pw[:, b % 4, i, P * k:P * (k + 1)], ident)
                filled(("ptr", g, b), last)

            def contexts(g, n):
                if g == 0:
                    pe.wait_ge(*emptied(("kn", n)))
                o = begin(("cc", g, n))
                for b in (2 * n, 2 * n + 1):
                    pe.wait_ge(*emptied(("ptr", g, b)))
                    for k in (0, 1):
                        last = three(o[:, 256 * (b % 2):256 * (b % 2) + 256], [kvn[:, s, b, k, :] for s in (0, 1)],
                                     [ptw[b % 4][:, s, k, :] for s in (0, 1)], k == 0, k == 1)
                filled(("cc", g, n), last)

            def output(g, t):
                if t == 0:
                    for h in range(HG):
                        pe.wait_ge(*emptied(("wo2", g, h)))
                pe.wait_ge(*emptied(("cc", g, t)))
                o = begin(("y3", g, t))
                for h in range(HG):
                    last = three(o[:, :], [cc[:, s, h, P * t:P * (t + 1)] for s in (0, 1)],
                                 [wo2[:, s, h, :] for s in (0, 1)], h == 0, h == HG - 1)
                filled(("y3", g, t), last)

            for step in range(3):
                fold_queries(0, step)
            for t in range(T):
                pe.wait_ge(normed, 3 * T + t + 1)
                to_features("T3", t, lambda j: nx[:, t, P * j:P * (j + 1)])
            for t in range(T):
                pe.wait_ge(*emptied(("T3", t)))
            queries(0, 0)
            queries(0, 1)
            pe.wait_ge(kr_split, 1)
            for h in range(HG):
                queries_in_context(0, h)
            pe.wait_ge(kvt_split, 1)
            for n in range(STEPS):
                for x in attention_step(n):
                    if x[0] == "sc":
                        scores(*x[1:])
                    elif x[0] == "ptr":
                        probs_transposed(*x[1:])
                    elif x[0] == "w12":
                        fold_queries(x[1], 0)
                    elif x[0] == "w3":
                        fold_queries(x[1], 1 + x[2])
                    elif x[0] == "qr":
                        queries(*x[1:])
                    elif x[0] == "qp":
                        queries_in_context(*x[1:])
                    elif x[0] == "y3":
                        output(*x[1:])
                    elif x[0] == "wo2":
                        fold_values(*x[1:])
                    else:
                        contexts(*x[1:])

            for t in range(T):
                pe.wait_ge(normed, 4 * T + t + 1)
            for t in range(T):
                to_features("T4", t, lambda j: nx[:, t, P * j:P * (j + 1)])
            for t in range(T):
                pe.wait_ge(*emptied(("T4", t)))
            pe.wait_ge(lag_tiles, NB)

            def lagged(c):
                o = begin(("YC", c))
                for l in range(LAGS):
                    n = 512 - SQ * l
                    last = three(o[:, SQ * l:], [lag_tile[s][:, c, l, :] for s in (0, 1)],
                                 [xt[:, s, c, 0:n] for s in (0, 1)], l == 0, l == LAGS - 1)
                filled(("YC", c), last)

            lagged(0)
            for c in range(KC):
                if c + 1 < KC:
                    lagged(c + 1)
                pe.wait_ge(*emptied(("YC", c)))
                to_features("TY", c, lambda j: ym[:, c, P * j:P * (j + 1)])

            for t in range(T):
                pe.wait_ge(normed, 5 * T + t + 1)
                to_features("T5", t, lambda j: nx[:, t, P * j:P * (j + 1)])
            pe.wait_ge(agu_split, 1)
            for t in range(T):
                pe.wait_ge(*emptied(("T5", t)))
            o = begin(("lg",))
            for t in range(T):
                for k in range(KC):
                    last = three(o[:, E1 * t:E1 * (t + 1)], [xt[:, s, k, P * t:P * (t + 1)] for s in (0, 1)],
                                 [agu[:, s, 1024 + E1 * k:1024 + E1 * (k + 1)] for s in (0, 1)], k == 0, k == KC - 1)
            filled(("lg",), last)
            for n, x in enumerate((("ug",), ("uu",))):
                o = begin(x)
                for k in range(KC):
                    at = 512 * n + P * k
                    last = three(o[:, :], [agu[:, s, at:at + P] for s in (0, 1)], [xt[:, s, k, :] for s in (0, 1)],
                                 k == 0, k == KC - 1)
                filled(x, last)

            def mask_transposed(k):
                o = begin(("tm", k))
                for t in range(T):
                    last = pe.transpose(o[:, P * t:P * (t + 1)], maskt[:, k, t, :], ident)
                filled(("tm", k), last)

            def base(f, part):
                if part == 0:
                    begin(("gu", f, 0))
                    if f < 2:
                        pe.wait_ge(*emptied(("T5", 2 * f + 1)))
                    pe.wait_ge(ring_split, f + 1)
                o = bank[bank_of[("gu", f, 0)] + part]
                for k in range(KC):
                    at = 512 * part + P * k
                    last = three(o[:, :], [ring[:, f % 3, s, at:at + P] for s in (0, 1)],
                                 [xt[:, s, k, :] for s in (0, 1)], k == 0, k == KC - 1)
                if part == 1:
                    filled(("gu", f, 0), last)

            def expert(f, n):
                begin(("gu", f, n))
                if f == 0:
                    pe.wait_ge(um_split, 2 * n)
                for part in (0, 1):
                    at = 1024 + P * part
                    o = bank[bank_of[("gu", f, n)] + part]
                    w = [ring[:, f % 3, s, at:at + P] for s in (0, 1)]
                    m = [um[:, 2 * (n - 1) + part, s, :] for s in (0, 1)]
                    pe.matmul(o[:, :], w[0], m[0], start=False, stop=False, skip_group_check=True)
                    pe.matmul(o[:, :], w[0], m[1], start=False, stop=False, skip_group_check=True)
                    last = pe.matmul(o[:, :], w[1], m[0], start=False, stop=True, skip_group_check=True)
                filled(("gu", f, n), last)

            def expert_down(f, n):
                pe.wait_ge(hs_split, gates.index((f, n)) + 1)
                o = begin(("z", n)) if f == 0 else psum(("z", n))
                w = [ring[:, f % 3, s, 1280:1408] for s in (0, 1)]
                m = [hs[n - 1][:, s, :] for s in (0, 1)]
                pe.matmul(o[:, :], w[0], m[0], start=(f == 0), stop=False, skip_group_check=True)
                pe.matmul(o[:, :], w[0], m[1], start=False, stop=False, skip_group_check=True)
                last = pe.matmul(o[:, :], w[1], m[0], start=False, stop=(f == NF - 1), skip_group_check=True)
                if f == NF - 1:
                    filled(("z", n), last)
                elif n == 2:
                    last.then_inc(ring_used, 1)

            for f in (0, 1):
                base(f, 0)
                base(f, 1)
            pe.wait_ge(masks_ready, 1)
            for k in range(4):
                mask_transposed(k)
            for f in range(NF):
                if f > 0:
                    expert_down(f - 1, 1)
                expert(f, 1)
                if 0 < f < NF - 1:
                    base(f + 1, 0)
                if f > 0:
                    expert_down(f - 1, 2)
                if 0 < f < NF - 1:
                    base(f + 1, 1)
                expert(f, 2)
            for t in range(T):
                if t < 2:
                    pe.wait_ge(um_made, 4)
                    o = psum(("y4", t))
                else:
                    o = begin(("y4", t))
                for f in range(NF):
                    if t == 0 and f == 6:
                        expert_down(NF - 1, 1)
                    if t == 0 and f == NF - 1:
                        expert_down(NF - 1, 2)
                    if t == 0 and f % 4 == 0:
                        pe.wait_ge(wd_split, f // 4 + 1)
                    three(o[:, :], [h0t[:, s, f, P * t:P * (t + 1)] for s in (0, 1)],
                          [wdt[:, s, f, :] for s in (0, 1)], f == 0, False)
                if t == 0:
                    pe.wait_ge(z_made, 1)
                    pe.wait_ge(bd_in, 16)
                filled(("y4", t), pe.matmul(o[:, :], hh[0][:, P * t:P * (t + 1)], bd, start=False, stop=True))

        @block.scalar
        def _(act):
            def high(dst, x, done, src=None):
                act.wait_ge(*full(x))
                act.copy(dst, psum(x)[:, :] if src is None else src).then_inc(done, 1)

            def copy_out(dst, x, src=None):
                act.wait_ge(*full(x))
                act.copy(dst, psum(x)[:, :] if src is None else src).then_inc(*freed(x))

            def high_tile(name, t, done):
                high(xt_tiles[:, 0, :, t, :], (name, t), done, psum((name, t))[:, :].rearrange("p (c n) -> p c n", c=KC))

            def key_blocks(g):
                x = ("K", g)
                act.wait_ge(*full(x))
                if g >= 2:
                    act.wait_ge(*full(("S", g - 2, 1)))
                for h in range(4):
                    r = slice(32 * h, 32 * h + 32)
                    last = act.copy(kbd[r, g % 2, :, h, :], psum(x)[r, :].rearrange("p (b k) -> p b k", b=NB))
                last.then_inc(*freed(x))

            act.wait_ge(zeroed, 2)
            key_blocks(0)
            key_blocks(1)
            for t in range(T):
                high_tile("T0", t, xt_high)
            for p in range(4):
                x = ("V", p)
                act.wait_ge(*full(x))
                for b in (0, 1):
                    src = psum(x)[64 * b:64 * b + 64, :].rearrange("p (m h x) -> p m h x", m=8, h=2)
                    for h in (0, 1):
                        last = act.copy(vbd[64 * h:64 * h + 64, :, 2 * p + b, 32 * h:32 * h + 32], src[:, :, h, :])
                last.then_inc(*freed(x))
            act.wait_ge(wout_in, 16)
            act.copy(WQO[:, 4096:6144], STG[:, 2048:4096]).then_inc(wout_high, 1)
            for m in range(KC):
                copy_out(qt[:, m, :], ("q", m))

            act.wait_ge(ssm_in, 16)
            act.activation(ssm[:, 0:2, :, :], ssm[:, 0:2, :, :], ACT.Exp, scale=-1.0).then_inc(exp_made, 1)

            def exp0(g):
                act.wait_ge(s0_ready, g + 1)
                act.activation(pr[:, g % 2, :], pr[:, g % 2, :], ACT.Exp).then_inc(p0_exp, 1)

            def probs_out0(g):
                for i in (0, 1):
                    copy_out(ptb[:, g % 2, 2 * i:2 * i + 2, :, :].rearrange("p t m n -> p (t m n)"), ("PT", g, i))

            def out0(g):
                for i in (0, 1):
                    x = ("O", g, i)
                    act.wait_ge(*full(x))
                    src = psum(x)[:, :].rearrange("p (t m b x) -> p t m b x", t=2, m=2, b=2)
                    for b in (0, 1):
                        r = slice(64 * b, 64 * b + 64)
                        dst = otok[r, 2 * i:2 * i + 2, P * g:P * (g + 1)].rearrange("p t (m x) -> p t m x", m=2)
                        last = act.copy(dst, src[r, :, :, b, :])
                    last.then_inc(*freed(x))

            def fold_high(name, n):
                high((wqk if name == "Wqk" else wvo)[:, 0, n, :], (name, n), fold0_high)

            exp0(0)
            key_blocks(2)
            fold_high("Wqk", 0)
            exp0(1)
            key_blocks(3)
            probs_out0(0)
            fold_high("Wqk", 1)
            fold_high("Wqk", 2)
            out0(0)
            exp0(2)
            probs_out0(1)
            fold_high("Wqk", 3)
            out0(1)
            exp0(3)
            probs_out0(2)
            fold_high("Wvo", 0)
            fold_high("Wvo", 1)
            out0(2)
            probs_out0(3)
            fold_high("Wvo", 2)
            fold_high("Wvo", 3)
            out0(3)
            for t in range(T):
                high_tile("TO", t, ot_high)

            for c in range(KC):
                act.wait_ge(*emptied(("T1", c)))
                act.copy(xt[:, 0, c, :], xf[:, c, :]).then_inc(xt_high, 1)
            for m in range(KC):
                copy_out(tt[:, m, :], ("t", m))
            act.wait_ge(s1_ready, 1)
            act.activation(P1[:, :], P1[:, :], ACT.Exp).then_inc(p1_exp, 1)
            for t in range(T):
                copy_out(vf[:, t, :], ("v", t))
            copy_out(PT1[:, :], ("pt1",))

            def signs(i, rounded, signed, dst):
                act.wait_ge(rounded, i + 1)
                act.activation(dst[:, 2048 * i:2048 * (i + 1)], stg4[:, i, :], ACT.Sign, bias=minus_magic).then_inc(signed, 1)

            for i in range(4):
                signs(i, fc_rounded, fc_signed, FCT)
            for t in range(T):
                high_tile("T2", t, xt_high)

            def gelu(t):
                for n in range(NFB):
                    x = ("fc", t, n)
                    act.wait_ge(*full(x))
                    act.activation(hb[:, t % 2, 512 * n:512 * (n + 1)], psum(x)[:, :], ACT.Gelu,
                                   scale=wtot[:, 2:3]).then_inc(*freed(x))

            def norm_hidden(t):
                act.wait_ge(h_scales, t + 1)
                u = 8 * (t % 2)
                act.activation(hb[:, t % 2, :], hb[:, t % 2, :], ACT.Identity, scale=hsc[:, u:u + 1],
                               bias=hsc[:, u + 1:u + 2]).then_inc(h_normed, 1)

            def hidden_high(t):
                for j in range(4):
                    high(ht[:, t % 2, 0, 4 * j:4 * j + 4, :].rearrange("p f n -> p (f n)"), ("TH", t, j), ht_high)

            gelu(0)
            norm_hidden(0)
            gelu(1)
            for i in range(4):
                signs(i, pj_rounded, pj_signed, PJT)
            hidden_high(0)
            norm_hidden(1)
            gelu(2)
            hidden_high(1)
            norm_hidden(2)
            gelu(3)
            hidden_high(2)
            norm_hidden(3)
            act.wait_ge(kv_roped, 1)
            act.copy(KVT[:, 0:2048], kv_raw).then_inc(kvt_high, 1)
            hidden_high(3)

            act.wait_ge(*full(("y2", 3)))
            act.wait_ge(kr_in, 16)
            act.copy(KR[:, 0:1024], kr_raw).then_inc(kr_high, 1)
            for j in range(4):
                high(kvn[:, 0, 2 * j:2 * j + 2, :, :].rearrange("p b k d -> p (b k d)"), ("kn", j), kvn_high)

            def fold_high1(x):
                name, g, i = x[0], x[1], x[-1]
                if name == "w12":
                    copy_out(w12, x, psum(x)[:, 0:256])
                elif name == "w3":
                    high(w3[:, 0, 2 * i:2 * i + 2, :].rearrange("p c r -> p (c r)"), x, w3_high)
                elif name == "wo2":
                    high(wo2[:, 0, i, :], x, wo2_high)
                elif name == "qr":
                    high(qr[:, 0, i, :], x, qr_high)
                elif name == "qp":
                    high(qp[g % 2][:, 0, :, i, :], x, qp_high, psum(x)[:, :].rearrange("p (b q) -> p b q", b=NB))

            for x in (("w12", 0), ("w3", 0, 0), ("w3", 0, 1)):
                fold_high1(x)
            for t in range(T):
                high_tile("T3", t, xt_high)
            for x in [("qr", 0, i) for i in (0, 1)] + [("qp", 0, h) for h in range(HG)]:
                fold_high1(x)
            for n in range(STEPS):
                for x in attention_step(n):
                    if x[0] == "sc":
                        u = 16 * (n % 4)
                        act.wait_ge(max_made, n + 1)
                        act.activation(pw[:, n % 4, 0, :], psum(x)[:, 0:256], ACT.Exp, bias=mxs[:, u:u + 1],
                                       accum_out=mxs[:, u + 2:u + 3]).then_inc(sums_made, 1)
                        act.activation(pw[:, n % 4, 1, :], psum(x)[:, 256:512], ACT.Exp, bias=mxs[:, u + 1:u + 2],
                                       accum_out=mxs[:, u + 3:u + 4]).then_inc(*freed(x))
                    elif x[0] == "ptr":
                        b = x[2]
                        if n >= 6:
                            pair = (n - 6) // 2
                            act.wait_ge(*full(("cc", pair // T, pair % T)))
                        high(ptw[b % 4][:, 0, :, :].rearrange("p k n -> p (k n)"), x, ptw_high)
                    elif x[0] == "cc":
                        t = x[2]
                        high(cc[:, 0, :, P * t:P * (t + 1)].rearrange("p h (b q) -> p b h q", b=2), x, cc_high,
                             psum(x)[:, :].rearrange("p (b h q) -> p b h q", b=2, h=HG))
                    else:
                        fold_high1(x)

            for t in range(T):
                high_tile("T4", t, xt_high)
            act.wait_ge(agu_in, 16)
            act.copy(agu[:, 0, :], STG[:, 6144:7200]).then_inc(agu_high, 1)

            def chunk_high(f):
                act.wait_ge(ring_in[f % 2], 16 * (f // 2 + 1))
                if f >= 3:
                    act.wait_ge(ring_used, f - 2)
                act.copy(ring[:, f % 3, 0, :], STG[:, 2048 * (f % 2):2048 * (f % 2) + CH]).then_inc(ring_high, 1)

            def down_high(j):
                w = slice(2048 * j, 2048 * j + 512 * min(4, NF - 4 * j))
                act.wait_ge(wd_in[j], 16)
                act.copy(WDT[:, w], WDF[:, w]).then_inc(wd_high, 1)

            chunk_high(0)
            chunk_high(1)
            for c in range(KC):
                x = ("YC", c)
                act.wait_ge(*full(x))
                act.activation(ym[:, c, :], psum(x)[:, :], ACT.Silu).then_inc(*freed(x))
            for t in range(T):
                high_tile("T5", t, xt_high)
            copy_out(rt[:, 0, :, :], ("lg",), psum(("lg",))[:, 0:T * E1].rearrange("p (t e) -> p t e", t=T))
            act.wait_ge(rt_ready, 1)
            act.activation(rt[:, 0, :, :], rt[:, 0, :, :], ACT.Exp).then_inc(rt_exp, 1)

            def gate(k):
                x = ("gu",) + gates[k]
                act.wait_ge(*full(x))
                if k == 1:
                    act.wait_ge(um_split, 3)
                if k >= 2:
                    act.wait_ge(*emptied(("gu",) + gates[k - 2]))
                act.activation(sg[k % 2], psum(x)[:, :], ACT.Silu).then_inc(silu_made, 1)

            def gated_high(k):
                f, n = gates[k]
                act.wait_ge(*emptied(("gu", f, n)))
                act.copy(h0t[:, 0, f, :] if n == 0 else hs[n - 1][:, 0, :], hh[k % 2]).then_inc(hs_high, 1)

            gate(0)
            gated_high(0)
            for k in range(4):
                copy_out(mk[:, k, :], ("tm", k))
            for k in range(4):
                act.wait_ge(um_made, k + 1)
                act.copy(um[:, k, 0, :], (sg[1], hh[1])[k % 2]).then_inc(um_high, 1)
            chunk_high(2)
            for k in range(1, len(gates)):
                f, n = gates[k]
                gate(k)
                gated_high(k)
                if n == 1 and 1 <= f < NF - 2:
                    chunk_high(f + 2)
                if n == 2 and 5 <= f < 8:
                    down_high(f - 5)

        @block.vector
        def _(dve):
            link = in_order(dve, dve_step)

            def low(dst, x, high_done, count, high, src=None):
                dve.wait_ge(high_done, count)
                dve.tensor_tensor(dst, psum(x)[:, :] if src is None else src, high.bitcast(F32),
                                  ALU.subtract).then_inc(*freed(x))

            def low_tile(name, t, high_done, count):
                low(xt_tiles[:, 1, :, t, :], (name, t), high_done, count, xt_tiles[:, 0, :, t, :],
                    psum((name, t))[:, :].rearrange("p (c n) -> p c n", c=KC))

            def rsqrt(n):
                v, y, s = var2[:, 0:n], rs[:, 0:n], rs_t[:, 0:n]
                link(dve.tensor_scalar(s.bitcast(I32), v.bitcast(I32), 1, None, ALU.logical_shift_right))
                link(dve.tensor_scalar(y.bitcast(I32), s.bitcast(I32), -1.0, RSQRT_SEED, ALU.mult, ALU.add))
                for _ in range(3):
                    link(dve.tensor_tensor(s, y, y, ALU.mult))
                    link(dve.scalar_tensor_tensor(out=s, in0=s, scalar=-0.5, in1=v, op0=ALU.mult, op1=ALU.mult))
                    link(dve.scalar_tensor_tensor(out=y, in0=s, scalar=1.5, in1=y, op0=ALU.add, op1=ALU.mult))

            def x_stats(t):
                link(dve.bn_stats(stats[:, t, :], x3[:, t, :]))
                dve.bn_aggr(mv[:, t, :], stats[:, t, :]).then_inc(x_stat, 1)

            def scales(first, eps1, eps2=None):
                dve.wait_ge(x_stat, T * (first + 1))
                v = mv[:, :, 1]
                dve.tensor_scalar(var2[:, 0:4], v, eps1, None, ALU.add).then_inc(dve_tick, 1)
                if eps2 is not None:
                    dve.tensor_scalar(var2[:, 4:8], v, 1.0 + eps2, eps1 * eps2, ALU.mult, ALU.add).then_inc(dve_tick, 1)
                ticks[0] += 1 if eps2 is None else 2
                dve.wait_ge(dve_tick, ticks[0])
                rsqrt(4 if eps2 is None else 8)

            def normalise(dst, at):
                for t in range(T):
                    dve.tensor_scalar(dst[:, t, :], x3[:, t, :], mv[:, t, 0:1], rs[:, at + t:at + t + 1],
                                      ALU.subtract, ALU.mult).then_inc(normed, 1)

            def add_to_x(x, t):
                dve.wait_ge(*full(x))
                dve.tensor_tensor(x3[:, t, :], x3[:, t, :], psum(x)[:, :], ALU.add).then_inc(*freed(x))
                dve.wait_ge(*emptied(x))

            ticks = [0]

            for t in range(T):
                dve.wait_ge(x_in[t], 16)
                x_stats(t)
            scales(0, 1e-5)
            normalise(n0, 0)
            dve.wait_ge(wq_in, 16)
            dve.tensor_copy(WQO[:, 0:2048], STG[:, 0:2048]).then_inc(wq_high, 1)
            dve.wait_ge(wq_high, 1)
            dve.tensor_tensor(WQO[:, 2048:4096], STG[:, 0:2048], WQO[:, 0:2048].bitcast(F32), ALU.subtract).then_inc(wq_split, 1)
            for t in range(T):
                low_tile("T0", t, xt_high, t + 1)
            dve.wait_ge(wout_high, 1)
            dve.tensor_tensor(WQO[:, 6144:8192], STG[:, 2048:4096], WQO[:, 4096:6144].bitcast(F32),
                              ALU.subtract).then_inc(wout_split, 1)

            def mixer_rates():
                dve.wait_ge(pool_step, 2)
                dve.reciprocal(sw[:, 0, :, :], sw[:, 1, :, :]).then_inc(rates_made, 1)

            def rows16(g):
                return pr[:, g % 2, :].rearrange("p (r k) -> p r k", k=SQ)

            def softmax0_shift(g):
                if g >= 2:
                    dve.wait_ge(*full(("PT", g - 2, 1)))
                nm = nmax0[:, 16 * (g % 2):16 * (g % 2) + 16]
                for i in (0, 1):
                    x = ("S", g, i)
                    dve.wait_ge(*full(x))
                    dve.scalar_tensor_tensor(out=rows16(g)[:, 8 * i:8 * i + 8, :],
                                             in0=psum(x)[:, :].rearrange("p (r k) -> p r k", k=SQ), scalar=HD0 ** -0.5,
                                             in1=mask0.unsqueeze(1).broadcast_to([P, 8, SQ]), op0=ALU.mult,
                                             op1=ALU.add).then_inc(*freed(x))
                    dve.wait_ge(*emptied(x))
                link(dve.tensor_reduce(nm, rows16(g), AX_X, ALU.max, negate=True))
                dve.tensor_tensor(rows16(g), rows16(g), over(nm, SQ), ALU.add).then_inc(s0_ready, 1)

            def softmax0_divide(g):
                sm = rsum0[:, 16 * (g % 2):16 * (g % 2) + 16]
                dve.wait_ge(p0_exp, g + 1)
                link(dve.tensor_reduce(sm, rows16(g), AX_X, ALU.add))
                link(dve.reciprocal(sm, sm))
                dve.tensor_tensor(rows16(g), rows16(g), over(sm, SQ), ALU.mult).then_inc(p0_ready, 1)

            def fold_low(name, n):
                w_ = wqk if name == "Wqk" else wvo
                low(w_[:, 1, n, :], (name, n), fold0_high, n + 1 + (KC if name == "Wvo" else 0), w_[:, 0, n, :])

            softmax0_shift(0)
            softmax0_divide(0)
            fold_low("Wqk", 0)
            softmax0_shift(1)
            fold_low("Wqk", 1)
            fold_low("Wqk", 2)
            softmax0_divide(1)
            mixer_rates()
            softmax0_shift(2)
            fold_low("Wqk", 3)
            softmax0_divide(2)
            softmax0_shift(3)
            fold_low("Wvo", 0)
            fold_low("Wvo", 1)
            softmax0_divide(3)
            fold_low("Wvo", 2)
            fold_low("Wvo", 3)
            dve.wait_ge(states_made, 1)
            link(dve.tensor_reduce(lagw, lags_raw, AX_X, ALU.add))
            link(dve.tensor_copy(lag2[:, 0, :, :], lagw))
            dve.tensor_tensor(lag2[:, 1, :, :], lagw, lag2[:, 0, :, :].bitcast(F32), ALU.subtract).then_inc(lags_made, 1)
            for t in range(T):
                low_tile("TO", t, ot_high, t + 1)
            for t in range(T):
                add_to_x(("y0", t), t)
                x_stats(t)

            scales(1, 1e-5, 1e-5)
            normalise(nx, 4)
            link(dve.tensor_tensor(lnb, mv[:, :, 0], rs[:, 0:4], ALU.mult))
            link(dve.tensor_scalar(lna, rs[:, 0:4], 1.0, None, ALU.add))
            for t in range(T):
                link(dve.tensor_scalar(x3[:, t, :], x3[:, t, :], lna[:, t:t + 1], lnb[:, t:t + 1], ALU.mult, ALU.subtract))
            for c in range(KC):
                x = ("T1", c)
                dve.wait_ge(*full(x))
                dve.tensor_scalar(xf[:, c, :], psum(x)[:, :], gammaT[:, c:c + 1], betaT[:, c:c + 1],
                                  ALU.mult, ALU.add).then_inc(*freed(x))
            for c in range(KC):
                dve.wait_ge(*emptied(("T1", c)))
                dve.wait_ge(xt_high, T + c + 1)
                dve.tensor_tensor(xt[:, 1, c, :], xf[:, c, :], xt[:, 0, c, :].bitcast(F32), ALU.subtract).then_inc(xt1_split, 1)
            for i in (2, 3, 0, 1):
                dve.wait_ge(fc_in[i], 16)
                dve.tensor_reduce(parts[:, i:i + 1], stg4[:, i, :], AX_X, ALU.add, apply_absolute_value=True).then_inc(fc_summed, 1)
            p1 = P1[:, :].rearrange("p (t k) -> p t k", t=T)
            dve.wait_ge(*full(("s1",)))
            dve.scalar_tensor_tensor(out=p1, in0=psum(("s1",))[:, :].rearrange("p (t k) -> p t k", t=T), scalar=D ** -0.5,
                                     in1=mask1.unsqueeze(1).broadcast_to([P, T, P]), op0=ALU.mult,
                                     op1=ALU.add).then_inc(*freed(("s1",)))
            dve.wait_ge(*emptied(("s1",)))
            link(dve.tensor_reduce(nmax1[:, 0:4], p1, AX_X, ALU.max, negate=True))
            dve.tensor_tensor(p1, p1, over(nmax1[:, 0:4], P), ALU.add).then_inc(s1_ready, 1)

            def mean_abs(x, at, size):
                dve.wait_ge(*full(x))
                dve.tensor_reduce(wtot[:, at:at + 1], psum(x)[:, 0:4], AX_X, ALU.add).then_inc(*freed(x))
                dve.wait_ge(*emptied(x))
                link(dve.tensor_scalar(wtot[:, at + 2:at + 3], wtot[:, at:at + 1], 1.0 / size, None, ALU.mult))
                link(dve.tensor_scalar(wtot[:, at + 1:at + 2], wtot[:, at + 2:at + 3], 1e-6, None, ALU.add))
                link(dve.reciprocal(wtot[:, at + 3:at + 4], wtot[:, at + 1:at + 2]))

            def round_quarter(i, at, done):
                dve.tensor_scalar(stg4[:, i, :], stg4[:, i, :], wtot[:, at + 3:at + 4], MAGIC, ALU.mult,
                                  ALU.add).then_inc(done, 1)

            mean_abs(("wf",), 0, F0 * D)
            for i in range(4):
                round_quarter(i, 0, fc_rounded)
            dve.wait_ge(p1_exp, 1)
            link(dve.tensor_reduce(rsum1[:, 0:4], p1, AX_X, ALU.add))
            link(dve.reciprocal(rsum1[:, 4:8], rsum1[:, 0:4]))
            for t in range(T):
                x = ("y1", t)
                dve.wait_ge(*full(x))
                dve.scalar_tensor_tensor(out=x3[:, t, :], in0=psum(x)[:, :], scalar=rsum1[:, 4 + t:5 + t], in1=x3[:, t, :],
                                         op0=ALU.mult, op1=ALU.add).then_inc(*freed(x))
                dve.wait_ge(*emptied(x))
                x_stats(t)

            clip = 128.0 - 1e-6

            def quantise(tile, gm, done):
                link(dve.reciprocal(gm[:, 1:2], gm[:, 0:1]))
                link(dve.tensor_scalar(gm[:, 2:3], gm[:, 1:2], 128.0, None, ALU.mult))
                link(dve.tensor_scalar(gm[:, 3:4], gm[:, 0:1], 1.0 / 128.0, None, ALU.mult))
                link(dve.tensor_scalar(tile, tile, gm[:, 2:3], clip, ALU.mult, ALU.min))
                dve.tensor_scalar(tile, tile, -clip, gm[:, 3:4], ALU.max, ALU.mult).then_inc(done, 1)

            scales(2, 1e-5, 1e-6)
            for t in range(T):
                link(dve.tensor_scalar(nx[:, t, :], x3[:, t, :], mv[:, t, 0:1], rs[:, 4 + t:5 + t], ALU.subtract, ALU.mult))
                gm = xabs[:, 4 * t:4 * t + 4]
                link(dve.tensor_reduce(gm[:, 0:1], nx[:, t, :], AX_X, ALU.max, apply_absolute_value=True))
                quantise(nx[:, t, :], gm, normed)
            for t in range(T):
                low_tile("T2", t, xt_high, 2 * T + t + 1)
            for i in range(4):
                dve.wait_ge(pj_in[i], 16)
                dve.tensor_reduce(parts[:, 4 + i:5 + i], stg4[:, i, :], AX_X, ALU.add, apply_absolute_value=True).then_inc(pj_summed, 1)

            def hidden(t):
                u = 8 * (t % 2)
                for n in range(NFB):
                    dve.wait_ge(*emptied(("fc", t, n)))
                    last = dve.bn_stats(hstats[:, t % 2, n, :], hb[:, t % 2, 512 * n:512 * (n + 1)])
                link(last)
                link(dve.bn_aggr(hmv[:, 0:2], hstats[:, t % 2, :, :].rearrange("p n k -> p (n k)")))
                link(dve.tensor_scalar(var2[:, 0:1], hmv[:, 1:2], 1e-6, None, ALU.add))
                rsqrt(1)
                link(dve.tensor_copy(hsc[:, u:u + 1], rs[:, 0:1]))
                dve.scalar_tensor_tensor(out=hsc[:, u + 1:u + 2], in0=hmv[:, 0:1], scalar=-1.0, in1=rs[:, 0:1],
                                         op0=ALU.mult, op1=ALU.mult).then_inc(h_scales, 1)
                dve.wait_ge(h_normed, t + 1)
                gm = hsc[:, u + 4:u + 8]
                link(dve.tensor_reduce(gm[:, 0:1], hb[:, t % 2, :], AX_X, ALU.max, apply_absolute_value=True))
                quantise(hb[:, t % 2, :], gm, h_quant)

            def hidden_low(t):
                for j in range(4):
                    low(ht[:, t % 2, 1, 4 * j:4 * j + 4, :].rearrange("p f n -> p (f n)"), ("TH", t, j), ht_high, 4 * t + j + 1,
                        ht[:, t % 2, 0, 4 * j:4 * j + 4, :].rearrange("p f n -> p (f n)"))

            def out_hidden(t):
                x = ("y2", t)
                dve.wait_ge(*full(x))
                dve.scalar_tensor_tensor(out=x3[:, t, :], in0=psum(x)[:, :], scalar=wtot[:, 10:11], in1=x3[:, t, :],
                                         op0=ALU.mult, op1=ALU.add).then_inc(*freed(x))
                dve.wait_ge(*emptied(x))
                x_stats(t)

            hidden(0)
            mean_abs(("wp",), 8, F0 * D)
            for i in range(4):
                round_quarter(i, 8, pj_rounded)
            hidden_low(0)
            hidden(1)
            out_hidden(0)
            hidden_low(1)
            hidden(2)
            out_hidden(1)
            hidden_low(2)
            hidden(3)
            out_hidden(2)
            hidden_low(3)
            out_hidden(3)

            scales(3, 1e-5)
            normalise(nx, 0)
            for j in range(4):
                s_ = slice(2 * j, 2 * j + 2)
                low(kvn[:, 1, s_, :, :].rearrange("p b k d -> p (b k d)"), ("kn", j), kvn_high, j + 1,
                    kvn[:, 0, s_, :, :].rearrange("p b k d -> p (b k d)"))

            def fold_low1(x):
                name, g, i = x[0], x[1], x[-1]
                if name == "w3":
                    low(w3[:, 1, 2 * i:2 * i + 2, :].rearrange("p c r -> p (c r)"), x, w3_high, 2 * g + i + 1,
                        w3[:, 0, 2 * i:2 * i + 2, :].rearrange("p c r -> p (c r)"))
                elif name == "wo2":
                    low(wo2[:, 1, i, :], x, wo2_high, HG * g + i + 1, wo2[:, 0, i, :])
                elif name == "qr":
                    low(qr[:, 1, i, :], x, qr_high, 2 * g + i + 1, qr[:, 0, i, :])
                elif name == "qp":
                    low(qp[g % 2][:, 1, :, i, :], x, qp_high, HG * g + i + 1, qp[g % 2][:, 0, :, i, :],
                        psum(x)[:, :].rearrange("p (b q) -> p b q", b=NB))

            for i in (0, 1):
                fold_low1(("w3", 0, i))
            for t in range(T):
                low_tile("T3", t, xt_high, 3 * T + t + 1)
            for x in [("qr", 0, i) for i in (0, 1)] + [("qp", 0, h) for h in range(HG)]:
                fold_low1(x)
            for n in range(STEPS):
                u = 16 * (n % 4)
                for x in attention_step(n):
                    if x[0] == "sc":
                        dve.wait_ge(*full(x))
                        dve.tensor_reduce(mxs[:, u:u + 2], psum(x)[:, :].rearrange("p (i k) -> p i k", i=2),
                                          AX_X, ALU.max, negate=True).then_inc(max_made, 1)
                    elif x[0] == "ptr":
                        b = x[2]
                        low(ptw[b % 4][:, 1, :, :].rearrange("p k n -> p (k n)"), x, ptw_high, n - 1,
                            ptw[b % 4][:, 0, :, :].rearrange("p k n -> p (k n)"))
                        if n < NB * G1:
                            dve.wait_ge(*emptied(("sc", n // NB, n % NB)))
                            dve.reciprocal(mxs[:, u + 4:u + 6], mxs[:, u + 2:u + 4]).then_inc(recip_made, 1)
                    elif x[0] == "cc":
                        g, t = x[1:]
                        view = [cc[:, k, :, P * t:P * (t + 1)].rearrange("p h (b q) -> p b h q", b=2) for k in (0, 1)]
                        low(view[1], x, cc_high, T * g + t + 1, view[0],
                            psum(x)[:, :].rearrange("p (b h q) -> p b h q", b=2, h=HG))
                    elif x[0] == "y3":
                        add_to_x(x, x[2])
                        if x[1] == G1 - 1:
                            x_stats(x[2])
                    else:
                        fold_low1(x)
                if n < 2:
                    dve.wait_ge(*emptied(("sc", 0, n)))
                    dve.reciprocal(mxs[:, u + 4:u + 6], mxs[:, u + 2:u + 4]).then_inc(recip_made, 1)

            scales(4, 1e-5)
            normalise(nx, 0)
            for t in range(T):
                low_tile("T4", t, xt_high, 4 * T + t + 1)
            for c in range(KC):
                x = ("TY", c)
                dve.wait_ge(*full(x))
                dve.tensor_tensor(x3[:, :, P * c:P * (c + 1)], x3[:, :, P * c:P * (c + 1)],
                                  psum(x)[:, :].rearrange("p (t n) -> p t n", t=T), ALU.add).then_inc(*freed(x))
            for c in range(KC):
                dve.wait_ge(*emptied(("TY", c)))
            for t in range(T):
                x_stats(t)
            scales(5, 1e-5)
            normalise(nx, 0)
            for t in range(T):
                low_tile("T5", t, xt_high, 5 * T + t + 1)

            p_, tmp, first, second = rt[:, 0, :, :], rt[:, 1, :, :], rt[:, 2, :, :], rt[:, 3, :, :]
            m4 = [small[:, 4 * k:4 * k + 4] for k in range(6)]
            dve.wait_ge(*emptied(("lg",)))
            link(dve.tensor_reduce(m4[0], p_, AX_X, ALU.max, negate=True))
            dve.tensor_tensor(p_, p_, over(m4[0], E1), ALU.add).then_inc(rt_ready, 1)
            dve.wait_ge(rt_exp, 1)
            link(dve.tensor_reduce(m4[1], p_, AX_X, ALU.add))
            link(dve.reciprocal(m4[2], m4[1]))
            link(dve.tensor_tensor(p_, p_, over(m4[2], E1), ALU.mult))

            def largest(src, best, onehot):
                link(dve.tensor_reduce(best, src, AX_X, ALU.max))
                link(dve.tensor_tensor(onehot, src, over(best, E1), ALU.is_equal))
                link(dve.tensor_tensor(onehot, onehot, expert_rank.unsqueeze(1).broadcast_to([P, T, E1]), ALU.mult))
                link(dve.tensor_reduce(m4[5], onehot, AX_X, ALU.max))
                link(dve.tensor_tensor(onehot, onehot, over(m4[5], E1), ALU.is_equal))

            largest(p_, m4[3], first)
            link(dve.scalar_tensor_tensor(out=tmp, in0=first, scalar=-2.0, in1=p_, op0=ALU.mult, op1=ALU.add))
            largest(tmp, m4[4], second)
            link(dve.tensor_tensor(tmp, second, first, ALU.subtract))
            masks = []
            for k, src in enumerate((first, tmp, first, second)):
                if k >= 2:
                    link(dve.tensor_tensor(src, src, over(m4[3 + k - 2], E1), ALU.mult))
                last = dve.tensor_scalar(maskt[:, k, :, :].rearrange("p t (e r) -> p (t e) r", r=R),
                                         over(src.rearrange("p t e -> p (t e)"), R), 2.0, None, ALU.mult)
                if k < 3:
                    link(last)
            last.then_inc(masks_ready, 1)

            def gated(k):
                x = ("gu",) + gates[k]
                dve.wait_ge(silu_made, k + 1)
                if k == 1:
                    dve.wait_ge(um_split, 4)
                if k >= 2:
                    dve.wait_ge(hs_split, k - 1)
                dve.tensor_tensor(hh[k % 2], sg[k % 2], bank[bank_of[x] + 1][:, :], ALU.mult).then_inc(*freed(x))

            def gated_low(k):
                f, n = gates[k]
                dst = h0t[:, :, f, :] if n == 0 else hs[n - 1]
                dve.wait_ge(*emptied(("gu", f, n)))
                dve.wait_ge(hs_high, k + 1)
                dve.tensor_tensor(dst[:, 1, :], hh[k % 2], dst[:, 0, :].bitcast(F32), ALU.subtract).then_inc(hs_split, 1)

            gated(0)
            gated_low(0)
            um_tile = (sg[1], hh[1])

            def um_low(k):
                dve.wait_ge(um_made, k + 1)
                dve.wait_ge(um_high, k + 1)
                dve.tensor_tensor(um[:, k, 1, :], um_tile[k % 2], um[:, k, 0, :].bitcast(F32), ALU.subtract).then_inc(um_split, 1)

            for k in range(4):
                x = ("ug",) if k % 2 == 0 else ("uu",)
                dve.wait_ge(*full(x))
                dve.wait_ge(*emptied(("tm", k // 2)))
                if k == 0:
                    dve.wait_ge(*full(("tm", 3)))
                if k >= 2:
                    um_low(k - 2)
                    dve.wait_ge(um_split, k - 1)
                ins = dve.tensor_tensor(um_tile[k % 2], psum(x)[:, :], mk[:, k // 2, :], ALU.mult)
                ins.then_inc(um_made, 1)
            um_low(2)
            um_low(3)
            for k in range(1, len(gates)):
                gated(k)
                gated_low(k)
            dve.wait_ge(hs_split, len(gates))
            for n in (1, 2):
                dve.wait_ge(*full(("z", n)))
                dve.wait_ge(*emptied(("tm", 1 + n)))
                dve.tensor_tensor(hh[n - 1], psum(("z", n))[:, :], mk[:, 1 + n, :], ALU.mult).then_inc(*freed(("z", n)))
            for n in (1, 2):
                dve.wait_ge(*emptied(("z", n)))
            dve.tensor_tensor(hh[0], hh[0], hh[1], ALU.add).then_inc(z_made, 1)
            for t in range(T):
                x = ("y4", t)
                dve.wait_ge(*full(x))
                dve.tensor_tensor(x3[:, t, :], x3[:, t, :], psum(x)[:, :], ALU.add).then_inc(x_final, 1)

        @block.gpsimd
        def _(pool):
            link = in_order(pool, pool_step)
            pool.memset(KBD[:, :], 0.0).then_inc(zeroed, 1)
            pool.memset(VBD[:, :], 0.0).then_inc(zeroed, 1)
            pool.wait_ge(exp_made, 1)
            p_, q, w = sw[:, 0, :, :], sw[:, 2, :, :], lags_raw
            link(pool.tensor_scalar(ssm[:, 0:2, :, :], ssm[:, 0:2, :, :], 1.0, None, ALU.add))
            link(pool.tensor_tensor(sw[:, 1, :, :], ssm[:, 0, :, :], ssm[:, 1, :, :], ALU.mult))
            pool.wait_ge(rates_made, 1)
            link(pool.tensor_tensor(q, p_, ssm[:, 2, :, :], ALU.mult))
            link(pool.tensor_scalar(q, q, NSSM ** -0.5, None, ALU.mult))
            link(pool.tensor_tensor(w[:, :, 0, :], q, ssm[:, 3, :, :], ALU.mult))
            link(pool.tensor_scalar(q, p_, -1.0, 1.0, ALU.mult, ALU.add))
            for l in range(1, LAGS):
                last = pool.tensor_tensor(w[:, :, l, :], w[:, :, l - 1, :], q, ALU.mult)
                if l + 1 < LAGS:
                    link(last)
            last.then_inc(states_made, 1)
            eight = lambda ap: ap.rearrange("p (b l) -> p b l", b=NB)
            pool.wait_ge(kv1_in, 3 * 16)
            link(pool.tensor_tensor(eight(kv_raw), eight(kv_raw), cos_t.unsqueeze(1).broadcast_to([P, NB, SK]), ALU.mult))
            link(pool.tensor_tensor(eight(kv_rot), eight(kv_rot), sin_t.unsqueeze(1).broadcast_to([P, NB, SK]), ALU.mult))
            pool.tensor_tensor(kv_raw, kv_raw, kv_rot, ALU.add).then_inc(kv_roped, 1)
            pool.wait_ge(kvt_high, 1)
            pool.wait_ge(lags_made, 1)
            pool.tensor_tensor(KVT[:, 2048:4096], kv_raw, KVT[:, 0:2048].bitcast(F32), ALU.subtract).then_inc(kvt_split, 1)
            pool.wait_ge(kr_high, 1)
            pool.tensor_tensor(KR[:, 1024:2048], kr_raw, KR[:, 0:1024].bitcast(F32), ALU.subtract).then_inc(kr_split, 1)

            def lag_matrices(s, c):
                pool.tensor_tensor(lag_tile[s][:, c, :, :], ident.unsqueeze(1).broadcast_to([P, LAGS, P]),
                                   over(lag2[:, s, c, :].bitcast(F32), P), ALU.mult).then_inc(lag_tiles, 1)

            for n in range(NB * G1):
                b = n % NB
                u = 16 * (b % 4)
                pool.wait_ge(recip_made, n + 1)
                for i in (0, 1):
                    last = pool.tensor_scalar(pw[:, b % 4, i, :], pw[:, b % 4, i, :], mxs[:, u + 4 + i:u + 5 + i], None, ALU.mult)
                last.then_inc(pw_ready, 1)
                if NB * (G1 - 1) <= n < NB * (G1 - 1) + KC:
                    if n == NB * (G1 - 1):
                        pool.wait_ge(*full(("sc", G1 - 2, NB - 1)))
                    lag_matrices(0, n % NB)
            pool.wait_ge(*full(("sc", G1 - 1, NB - 1)))
            for c in range(KC):
                lag_matrices(1, c)
            pool.wait_ge(agu_high, 1)
            pool.tensor_tensor(agu[:, 1, :], STG[:, 6144:7200], agu[:, 0, :].bitcast(F32), ALU.subtract).then_inc(agu_split, 1)
            for f in range(NF):
                pool.wait_ge(ring_high, f + 1)
                pool.tensor_tensor(ring[:, f % 3, 1, :], STG[:, 2048 * (f % 2):2048 * (f % 2) + CH],
                                   ring[:, f % 3, 0, :].bitcast(F32), ALU.subtract).then_inc(ring_split, 1)
                if 7 <= f < 10:
                    j = f - 7
                    w = slice(2048 * j, 2048 * j + 512 * min(4, NF - 4 * j))
                    pool.wait_ge(wd_high, j + 1)
                    pool.tensor_tensor(WDT[:, NF * 512:][:, w], WDF[:, w], WDT[:, w].bitcast(F32), ALU.subtract).then_inc(wd_split, 1)


def _constants():
    c = np.zeros((P, 465), np.float32)
    c[:, 0:128] = np.eye(P)
    row, key = np.arange(P)[:, None], np.arange(P)[None, :]
    c[:, 128:192] = np.where(key[:, :SQ] <= row % SQ, 0.0, HIDDEN)
    c[:, 192:320] = np.where((row // SQ == key // SQ) & (key <= row), 0.0, HIDDEN)
    c[:, 328:456] = 1.0
    c[:, 456:464] = np.arange(E1, 0, -1)
    c[:, 464] = -MAGIC
    return c


def _rope_tables():
    inv = (np.float32(1.0) / np.float32(10000.0) ** (np.arange(0, DCTX, 2, dtype=np.float32) / np.float32(DCTX))).astype(np.float32)
    freqs = np.arange(SK, dtype=np.float32)[:, None] * inv[None, :]
    sin, cos = np.repeat(np.sin(freqs), 2, axis=-1).T, np.repeat(np.cos(freqs), 2, axis=-1).T
    sign = np.where(np.arange(DCTX) < DCTX // 2, -1.0, 1.0).astype(np.float32)[:, None]
    return np.concatenate([cos, sin * sign], axis=1).astype(np.float32)


def _layout(i):
    def chunks(w):
        return w.reshape(-1, P, w.shape[1]).transpose(1, 0, 2).reshape(P, -1)

    def cat(*parts):
        return np.concatenate([p.reshape(P, -1) for p in parts], axis=1)

    ctx = i["ctx_512"]
    ctx_t = ctx.reshape(-1, DCTX).T
    consts = _constants()
    consts[:, 320:324] = i["L0_attn_gamma"].reshape(KC, P).T
    consts[:, 324:328] = i["L0_attn_beta"].reshape(KC, P).T
    qkv = i["L0_attn_qkv"]
    half = DCTX // 2
    kcq = i["L1_xattn_w_kc_q"].reshape(H1, P, 3, P).transpose(3, 0, 2, 1)
    wqr = i["L1_xattn_W_qr"].reshape(H1, 3, P, R1).transpose(2, 0, 1, 3)
    wq1 = i["L1_xattn_Wq"].reshape(H1, P, D).transpose(1, 0, 2)
    kckv = i["L1_xattn_w_kc_kv"].transpose(1, 0, 2)
    wo1 = i["L1_xattn_Wo"].T.reshape(H1, P, D).transpose(1, 0, 2)
    heads = lambda w, g: w[:, HG * g:HG * (g + 1)]
    kr = i["L1_xattn_W_kr"].transpose(0, 2, 1).reshape(H1 // 2, 2 * R1, DCTX).transpose(1, 0, 2)
    agu = [i[n].reshape(E1 * R, D).T for n in ("L1_ffn_Ag", "L1_ffn_Au")]
    bgu = [i[n].transpose(0, 2, 1).reshape(E1 * R, DFF) for n in ("L1_ffn_Bg", "L1_ffn_Bu")]
    ad = i["L1_ffn_Ad"].reshape(E1 * R, DFF).T

    def mlp(f):
        s = slice(P * f, P * (f + 1))
        return cat(chunks(i["L1_ffn_Wg"][s].T), chunks(i["L1_ffn_Wu"][s].T), bgu[0][:, s], bgu[1][:, s], ad[s])

    laid = {
        "x": i["x"].reshape(NB * SQ, D),
        "kv0": cat(ctx[:, :SQ].reshape(-1, DCTX).T, i["L0_xattn_Wkv_expand"].T),
        "consts": consts,
        "wq": chunks(i["L0_xattn_Wq"].T),
        "wout": chunks(i["L0_xattn_Wout"].T),
        "fold_qk": cat(chunks(qkv[:, :D].T), chunks(qkv[:, D:2 * D].T)),
        "fold_vo": cat(chunks(qkv[:, 2 * D:].T), chunks(i["L0_attn_o_proj"])),
        "fc": chunks(i["L0_ffn_w_fc"].T).reshape(P, 4, 2048).transpose(1, 0, 2),
        "pj": chunks(i["L0_ffn_w_proj"].T).reshape(P, 4, 2048).transpose(1, 0, 2),
        "kv1": cat(ctx_t, np.concatenate([ctx_t[half:], ctx_t[:half]]), _rope_tables()),
        "kr": kr.reshape(P, -1),
        "queries": np.stack([cat(heads(kcq, g), heads(wqr, g), heads(wq1, g)) for g in range(G1)]),
        "values": np.stack([cat(heads(kckv, g), heads(wo1, g)) for g in range(G1)]),
        "ssm": cat(*[chunks(i["L1_attn_" + n].reshape(D, NSSM)) for n in ("delta", "alpha", "beta", "gamma")]),
        "agu": cat(chunks(agu[0]), chunks(agu[1]), chunks(i["L1_ffn_Wr"].T)),
        "mlp": np.stack([mlp(f) for f in range(NF)]),
        "wd": chunks(i["L1_ffn_Wd"].T),
        "bd": i["L1_ffn_Bd"].transpose(0, 2, 1).reshape(E1 * R, D),
    }
    return {n: np.ascontiguousarray(v) for n, v in laid.items()}


def kernel(**inputs):
    import concourse.bacc as bacc
    from concourse.bass_utils import run_bass_kernel_spmd

    laid = _layout({n: np.asarray(v) for n, v in inputs.items()})
    nc = bacc.Bacc("TRN2", target_bir_lowering=False, num_devices=1)
    arrays = {f"in_{n}": v for n, v in laid.items()}
    aps = {n: nc.dram_tensor(f"in_{n}", v.shape, F32, kind="ExternalInput").ap() for n, v in laid.items()}
    out = nc.dram_tensor("out_x", (NB * SQ, D), F32, kind="ExternalOutput").ap()
    perceiver_blocks(nc, aps, out)
    r = run_bass_kernel_spmd(nc, [arrays], core_ids=[0])
    return r.results[0]["out_x"].reshape(NB, SQ, D)
```

```python
from contextlib import ExitStack

import numpy as np

import concourse.bass as bass
from concourse import mybir

F32 = mybir.dt.float32
F32R = mybir.dt.float32r
I32 = mybir.dt.int32
ALU = mybir.AluOpType
ACT = mybir.ActivationFunctionType
AX_X = mybir.AxisListType.X

P = 128
NB, SQ, D = 8, 64, 512
T = NB * SQ // P
KC = D // P
DCTX, SK = 128, 256
HD0 = 32
G0 = 4
F0 = 2048
NFB = F0 // 512
H1, R1 = 16, 64
G1, HG = 4, 4
NSSM, LAGS = 16, NB
DFF, E1, R = 1408, 8, 16
NF = DFF // P
CH = 8 * P + 3 * P
STEPS = NB * G1 + 4
CLIP = 128.0 - 1e-6
MAGIC = 12582912.0
RSQRT_SEED = float(0x5F3759DF)
HIDDEN = -3.0e38


def psum_plan():
    order = [("K", 0), ("K", 1)] + [("V", p) for p in range(4)]
    order += [("T0", t) for t in range(T)]
    S = lambda g: [("S", g, 0), ("S", g, 1)]
    PT = lambda g: [("PT", g, 0), ("PT", g, 1)]
    O = lambda g: [("O", g, 0), ("O", g, 1)]
    order += [("q", 0), ("q", 1)] + S(0) + [("K", 2), ("q", 2)] + S(1) + [("K", 3), ("q", 3)] + PT(0) + S(2) + O(0)
    order += [("Wqk", 0)] + PT(1) + S(3) + O(1) + [("Wqk", 1)] + PT(2) + O(2) + [("Wqk", 2)] + PT(3) + O(3)
    order += [("TO", t) for t in range(T)] + [("Wqk", 3)] + [("y0", t) for t in range(T)] + [("Wvo", 0), ("Wvo", 1)]
    order += [("T1", c) for c in range(KC)] + [("Wvo", 2), ("Wvo", 3)] + [("t", m) for m in range(KC)] + [("s1",), ("wf",)]
    order += [("v", 0), ("v", 1), ("pt1",), ("y1", 0), ("y1", 1), ("v", 2), ("v", 3), ("y1", 2), ("y1", 3)]
    fc = lambda t: [("fc", t, n) for n in range(NFB)]
    TH = lambda t: [("TH", t, j) for j in range(4)]
    order += [("T2", 0), ("T2", 1)] + fc(0) + [("T2", 2)] + fc(1) + [("wp",), ("T2", 3)] + fc(2)
    order += TH(0) + [("y2", 0)] + fc(3) + TH(1) + [("y2", 1)] + TH(2) + [("w12", 0), ("y2", 2), ("w3", 0, 0), ("w3", 0, 1)]
    order += TH(3) + [("y2", 3)] + [("T3", t) for t in range(T - 1)] + [("kn", j) for j in range(4)]
    order += [("w12", 1), ("T3", T - 1), ("qr", 0, 0), ("qr", 0, 1), ("wo2", 0, 0)] + [("qp", 0, h) for h in range(HG)] + [("wo2", 0, 1)]
    for n in range(STEPS):
        order += attention_step(n)
    order += [("T4", t) for t in range(T)] + [("YC", 0)]
    for c in range(KC):
        order += ([("YC", c + 1)] if c + 1 < KC else []) + [("TY", c)]
    bank_of, turn_of, turns = {}, {}, [0] * 8

    def take(x, b):
        turns[b] += 1
        bank_of[x], turn_of[x] = b, turns[b]

    for n, x in enumerate(order):
        take(x, n % 8)
    for x, b in mlp_order():
        take(x, b)
    return bank_of, turn_of


def attention_step(n):
    g, s = n // NB, n % NB
    order = [("sc", g, s)] if n < NB * G1 else []
    if 2 <= n < NB * G1 + 2:
        order.append(("ptr", (n - 2) // NB, (n - 2) % NB))
    if g == 0:
        order += {0: [("w3", 1, 0)], 1: [("w3", 1, 1)], 2: [("wo2", 0, 2)], 3: [("wo2", 0, 3)],
                  4: [("qr", 1, 0), ("qr", 1, 1)], 5: [("qp", 1, 0), ("qp", 1, 1)], 6: [("qp", 1, 2), ("qp", 1, 3)]}.get(s, [])
    elif g + 1 < G1:
        order += {2: [("w3", g + 1, 0)], 3: [("w3", g + 1, 1)], 4: [("qr", g + 1, 0), ("qr", g + 1, 1)],
                  5: [("qp", g + 1, 0), ("qp", g + 1, 1)], 6: [("qp", g + 1, 2), ("qp", g + 1, 3)]}.get(s, [])
    if s == NB - 1 and g + 2 < G1:
        order.append(("w12", g + 2))
    if s < T and g > 0:
        order.append(("y3", g - 1, s))
    if 0 < g < G1:
        order += {4: [("wo2", g, 0), ("wo2", g, 1)], 5: [("wo2", g, 2)], 6: [("wo2", g, 3)]}.get(s, [])
    if n >= NB * G1 and order[0][0] == "ptr":
        order.append(order.pop(0))
    if n >= 4 and n % 2 == 0:
        pair = (n - 4) // 2
        order.append(("cc", pair // T, pair % T))
    return order


def gate_order():
    order = [(0, 0)]
    for f in range(NF):
        order += [(f, 1)] + ([(f + 1, 0)] if f + 1 < NF else []) + [(f, 2)]
    return order


def mlp_order():
    order = [(("T5", t), t) for t in range(T)] + [(("lt",), 4), (("ug",), 6), (("lg",), 5), (("uu",), 7)]
    order += [(("gu", 0, 0), 0)] + [(("tm", k), 4 + k % 2) for k in range(4)]
    order += [(("gu", f, n), 2 * (f % 2)) for f, n in gate_order()[1:]]
    order += [(("z", 1), 4), (("z", 2), 5)]
    return order + [(("y4", t), (6, 7, 0, 2)[t]) for t in range(T)]


def perceiver_blocks(nc, a, out):
    bank_of, turn_of = psum_plan()
    ctx = ExitStack()
    with ctx:
        taken = [0]

        def place(name, dt, cols, at):
            with ExitStack() as s:
                if at:
                    s.enter_context(nc.sbuf_tensor("ahead_of_" + name, [P, at], F32))
                taken[0] = max(taken[0], at + cols)
                return s.enter_context(nc.sbuf_tensor(name, [P, cols], dt))

        X = place("X", F32, T * D, 0)
        XT = place("XT", F32R, 2 * KC * 512, 2048)
        CONST = place("CONST", F32, 1536, 6144)
        STG = place("STG", F32, 8192, 7680)
        M = 15872
        QT = place("QT", F32, 2048, M)
        KBD = place("KBD", F32, 4096, M + 2048)
        VBD = place("VBD", F32, 4096, M + 6144)
        OTOK = place("OTOK", F32, 2048, M + 10240)
        N0 = place("N0", F32, 2048, M + 10240)
        PR = place("PR", F32, 2048, M + 12288)
        PTB = place("PTB", F32, 2048, M + 14336)
        KVRAW = place("KVRAW", F32, 1536, M + 14336)
        WQO = place("WQO", F32R, 8192, M + 16384)
        WQKVO = place("WQKVO", F32R, 8192, M + 24576)
        XF = place("XF", F32, 2048, M)
        TT = place("TT", F32, 2048, M + 2048)
        VF = place("VF", F32, 2048, M + 4096)
        P1 = place("P1", F32, 512, M + 6144)
        PT1 = place("PT1", F32, 512, M + 6656)
        NX = place("NX", F32, 2048, M + 12288)
        HB = place("HB", F32, 4096, M)
        HT = place("HT", F32R, 8192, M + 4096)
        FCT = place("FCT", F32R, 8192, M + 16384)
        PJT = place("PJT", F32R, 8192, M + 24576)
        QP = [place("QP0", F32R, 4096, M), place("QP1", F32R, 4096, M + 26624)]
        PW = place("PW", F32, 2048, M + 4096)
        KR = place("KR", F32R, 2048, M + 6144)
        KVN = place("KVN", F32R, 4096, M + 8192)
        CC = place("CC", F32R, 4096, M + 12288)
        W3 = place("W3", F32R, 2048, M + 16384)
        QR = place("QR", F32R, 2048, M + 18432)
        PTW = [place("PTW0", F32R, 2048, M + 20480), place("PTW1", F32R, 2048, M + 30720)]
        WO2 = place("WO2", F32R, 4096, M + 22528)
        KVT = place("KVT", F32R, 4096, M + 32768)
        KVF = place("KVF", F32, 2048, M + 14336)
        KVROT = place("KVROT", F32, 2048, M + 32768)
        ROPE = place("ROPE", F32, 512, M + 34816)
        LAGH = place("LAGH", F32R, 4096, M)
        LAGL = place("LAGL", F32R, 4096, M + 32768)
        NXM = place("NXM", F32, 2048, M + 4096)
        YM = place("YM", F32, 2048, M + 4096)
        LAGS_RAW = place("LAGS_RAW", F32, 512, M + 35328)
        H0T = place("H0T", F32R, 2 * NF * 512, M)
        UM = place("UM", F32R, 4096, M + 11264)
        HS0 = place("HS0", F32R, 1024, M + 15360)
        HS1 = place("HS1", F32R, 1024, M + 16384)
        RING = place("RING", F32R, 3 * 2 * CH, M + 17408)
        WDT = place("WDT", F32R, 2 * NF * 512, M + 25856)
        WDF = place("WDF", F32, NF * 512, M + 25856 + NF * 512)
        AGU = place("AGU", F32R, 2 * 1056, M + 25856)
        MLPF = STG[:, 4096:8192]
        ctx.enter_context(nc.sbuf_tensor("all_phases", [P, taken[0]], F32))

        small = ctx.enter_context(nc.sbuf_tensor("small", [P, 64], F32))
        LAG2 = ctx.enter_context(nc.sbuf_tensor("LAG2", [P, 2 * KC * LAGS], F32R))
        bank = [ctx.enter_context(nc.psum_tensor(f"bank{b}", [P, 512], F32)) for b in range(8)]

        def sem(name):
            return ctx.enter_context(nc.semaphore(name))

        bank_full = [sem(f"bank_full{b}") for b in range(8)]
        bank_free = [sem(f"bank_free{b}") for b in range(8)]

        def psum(x):
            return bank[bank_of[x]]

        def full(x):
            return bank_full[bank_of[x]], turn_of[x]

        def emptied(x):
            return bank_free[bank_of[x]], turn_of[x]

        def freed(x):
            return bank_free[bank_of[x]], 1

        x_in = [sem(f"x_in{t}") for t in range(T)]
        consts_in, kv0_in, wq_in, wout_in, ssm_in = sem("consts_in"), sem("kv0_in"), sem("wq_in"), sem("wout_in"), sem("ssm_in")
        fold0_in = [sem("fold_qk_in"), sem("fold_vo_in")]
        fc_in = [sem(f"fc_in{i}") for i in range(4)]
        pj_in = [sem(f"pj_in{i}") for i in range(4)]
        kv1_in, kr_in, agu_in, bd_in = sem("kv1_in"), sem("kr_in"), sem("agu_in"), sem("bd_in")
        query_in = [sem(f"query_in{g}") for g in range(G1)]
        value_in = [sem(f"value_in{g}") for g in range(G1)]
        ring_in = [sem(f"ring_in{i}") for i in range(2)]
        wd_in = [sem(f"wd_in{j}") for j in range(3)]
        out_done = sem("out_done")
        zeroed = sem("zeroed")
        wq_split_rest = sem("wq_split_rest")
        wq_high, wq_split, wout_high, wout_split = sem("wq_high"), sem("wq_split"), sem("wout_high"), sem("wout_split")
        fold0_high = sem("fold0_high")
        fc_summed, pj_summed = sem("fc_summed"), sem("pj_summed")
        fc_signed, pj_signed, means_made = sem("fc_signed"), sem("pj_signed"), sem("means_made")
        fc_rounded = [sem(f"fc_rounded{i}") for i in range(4)]
        pj_rounded = [sem(f"pj_rounded{i}") for i in range(4)]
        kv_roped, kvt_high, kvt_split, kvn_high = sem("kv_roped"), sem("kvt_high"), sem("kvt_split"), sem("kvn_high")
        kr_high, kr_split = sem("kr_high"), sem("kr_split")
        w3_high, wo2_high = sem("w3_high"), sem("wo2_high")
        agu_high, agu_split = sem("agu_high"), sem("agu_split")
        ring_high, ring_split, ring_used = sem("ring_high"), sem("ring_split"), sem("ring_used")
        wd_high, wd_split = sem("wd_high"), sem("wd_split")
        normed = sem("normed")
        xt_high = sem("xt_high")
        s0_ready, p0_exp, p0_ready = sem("s0_ready"), sem("p0_exp"), sem("p0_ready")
        ot_high = sem("ot_high")
        s1_ready, p1_exp = sem("s1_ready"), sem("p1_exp")
        h_stats, var_made = sem("h_stats"), sem("var_made")
        h_scales, h_normed, h_quant, ht_high = sem("h_scales"), sem("h_normed"), sem("h_quant"), sem("ht_high")
        qr_high, qp_high, ptw_high, cc_high = sem("qr_high"), sem("qp_high"), sem("ptw_high"), sem("cc_high")
        max_made, sums_made, recip_made, pw_ready = sem("max_made"), sem("sums_made"), sem("recip_made"), sem("pw_ready")
        exp_made, states_made, lags_made = sem("exp_made"), sem("states_made"), sem("lags_made")
        rates_made, lag_tiles, lag_tiles_rest = sem("rates_made"), sem("lag_tiles"), sem("lag_tiles_rest")
        rt_ready, rt_exp, masks_ready = sem("rt_ready"), sem("rt_exp"), sem("masks_ready")
        um_made, um_high, um_split = sem("um_made"), sem("um_high"), sem("um_split")
        silu_made, hs_high, hs_split, z_made, x_final = sem("silu_made"), sem("hs_high"), sem("hs_split"), sem("z_made"), sem("x_final")
        dve_step, pool_step, factors, x_stat = sem("dve_step"), sem("pool_step"), sem("factors"), sem("x_stat")
        gates = gate_order()

        xt = XT[:, :].rearrange("p (s c n) -> p s c n", s=2, c=KC)
        xt_tiles = XT[:, :].rearrange("p (s c t n) -> p s c t n", s=2, c=KC, t=T)
        x3 = X[:, :].rearrange("p (t d) -> p t d", t=T)
        n0 = N0[:, :].rearrange("p (t d) -> p t d", t=T)
        nxm = NXM[:, :].rearrange("p (t d) -> p t d", t=T)
        nx = NX[:, :].rearrange("p (t d) -> p t d", t=T)
        ident = CONST[:, 0:128]
        mask0 = CONST[:, 128:192]
        mask1 = CONST[:, 192:320]
        gammaT, betaT = CONST[:, 320:324], CONST[:, 324:328]
        ones = CONST[:, 328:456]
        expert_rank = CONST[:, 456:464]
        minus_magic = CONST[:, 464:465]
        stats = CONST[:, 480:504].rearrange("p (t k) -> p t k", k=6)
        mv = CONST[:, 504:512].rearrange("p (t k) -> p t k", k=2)
        var2, rs, rs_t = [CONST[:, a_:a_ + 8].rearrange("p (k t) -> p k t", k=2) for a_ in (512, 520, 528)]
        lna, lnb = CONST[:, 536:540], CONST[:, 540:544]
        nmax0 = CONST[:, 544:576]
        rsum0 = CONST[:, 576:608]
        parts, wtot = CONST[:, 608:616], CONST[:, 616:632]
        lagw = CONST[:, 640:672].rearrange("p (c l) -> p c l", c=KC)
        nmax1, rsum1 = CONST[:, 672:680], CONST[:, 680:696]
        hstats = CONST[:, 696:744].rearrange("p (u n k) -> p u n k", u=2, k=6)
        hmv = CONST[:, 744:752]
        hsc = CONST[:, 752:768]
        xabs = CONST[:, 768:784]
        mxs = CONST[:, 784:848]
        ssm = CONST[:, 896:1152].rearrange("p (k c n) -> p k c n", k=4, c=KC)
        sw = CONST[:, 1152:1344].rearrange("p (k c n) -> p k c n", k=3, c=KC)
        chunk_stats = CONST[:, 1152:1248].rearrange("p (t c k) -> p t c k", t=T, c=KC)
        rt = CONST[:, 1344:1536].rearrange("p (k t e) -> p k t e", k=6, t=T)
        wq = WQO[:, 0:4096].rearrange("p (s c n) -> p s c n", s=2, c=KC)
        wout = WQO[:, 4096:8192].rearrange("p (s c n) -> p s c n", s=2, c=KC)
        wqk = WQKVO[:, 0:4096].rearrange("p (s c n) -> p s c n", s=2, c=KC)
        wvo = WQKVO[:, 4096:8192].rearrange("p (s c n) -> p s c n", s=2, c=KC)
        qt = QT[:, :].rearrange("p (m n) -> p m n", m=KC)
        kbd = KBD[:, :].rearrange("p (u b h k) -> p u b h k", u=2, b=NB, h=4)
        vbd = VBD[:, :].rearrange("p (m b x) -> p m b x", m=8, b=NB)
        otok = OTOK[:, :].rearrange("p (t d) -> p t d", t=T)
        pr = PR[:, :].rearrange("p (u w) -> p u w", u=2)
        ptb = PTB[:, :].rearrange("p (u t m n) -> p u t m n", u=2, t=T, m=2)
        stg4 = STG[:, :].rearrange("p (u w) -> p u w", u=4)
        xf = XF[:, :].rearrange("p (c n) -> p c n", c=KC)
        tt = TT[:, :].rearrange("p (c n) -> p c n", c=KC)
        vf = VF[:, :].rearrange("p (t d) -> p t d", t=T)
        hb = HB[:, :].rearrange("p (u f) -> p u f", u=2)
        ht = HT[:, :].rearrange("p (u s f n) -> p u s f n", u=2, s=2, f=F0 // P)
        fct = FCT[:, :].rearrange("p (c f) -> p c f", c=KC)
        pjt = PJT[:, :].rearrange("p (f d) -> p f d", f=F0 // P)
        kvt = KVT[:, :].rearrange("p (s b l) -> p s b l", s=2, b=NB)
        kvn = KVN[:, :].rearrange("p (s b k d) -> p s b k d", s=2, b=NB, k=2)
        w3 = W3[:, :].rearrange("p (s c r) -> p s c r", s=2, c=KC)
        qr = QR[:, :].rearrange("p (s i n) -> p s i n", s=2, i=2)
        kr = KR[:, :].rearrange("p (s j d) -> p s j d", s=2, j=H1 // 2)
        qp = [t_[:, :].rearrange("p (s b h q) -> p s b h q", s=2, b=NB, h=HG) for t_ in QP]
        pw = PW[:, :].rearrange("p (u i k) -> p u i k", u=4, i=2)
        ptw = [PTW[b // 2][:, 1024 * (b % 2):1024 * (b % 2) + 1024].rearrange("p (s k n) -> p s k n", s=2, k=2) for b in range(4)]
        wo2 = WO2[:, :].rearrange("p (s h d) -> p s h d", s=2, h=HG)
        cc = CC[:, :].rearrange("p (s h n) -> p s h n", s=2, h=HG)
        kv_raw, kv_rot = KVF[:, :], KVROT[:, :]
        cos_t, sin_t = ROPE[:, 0:256], ROPE[:, 256:512]
        kcq = STG[:, 0:1536].rearrange("p (h c k) -> p h c k", h=HG, c=3)
        wqr = STG[:, 1536:2304].rearrange("p (h c r) -> p h c r", h=HG, c=3)
        wq1 = STG[:, 2304:4352].rearrange("p (h c) -> p h c", h=HG)
        kckv = STG[:, 4352:4864].rearrange("p (h d) -> p h d", h=HG)
        woT = STG[:, 4864:6912].rearrange("p (h d) -> p h d", h=HG)
        kr_raw = STG[:, 6912:7936]
        w12 = STG[:, 7936:8192]
        lag2 = LAG2[:, :].rearrange("p (s c l) -> p s c l", s=2, c=KC)
        lags_raw = LAGS_RAW[:, :].rearrange("p (l c n) -> p c l n", l=LAGS, c=KC)
        lag_tile = [t_[:, :].rearrange("p (c l n) -> p c l n", c=KC, l=LAGS) for t_ in (LAGH, LAGL)]
        ym = YM[:, :].rearrange("p (c n) -> p c n", c=KC)
        h0t = H0T[:, :].rearrange("p (s f n) -> p s f n", s=2, f=NF)
        um = UM[:, :].rearrange("p (k s n) -> p k s n", k=4, s=2)
        hs = [t_[:, :].rearrange("p (s n) -> p s n", s=2) for t_ in (HS0, HS1)]
        ring = RING[:, :].rearrange("p (u s w) -> p u s w", u=3, s=2)
        wdt = WDT[:, :].rearrange("p (s f d) -> p s f d", s=2, f=NF)
        agu = AGU[:, :].rearrange("p (s w) -> p s w", s=2)
        sg = [MLPF[:, 0:512], MLPF[:, 512:1024]]
        hh = [MLPF[:, 1024:1536], MLPF[:, 1536:2048]]
        logits_t = MLPF[:, 0:512]
        mk = MLPF[:, 2048:4096].rearrange("p (k n) -> p k n", k=4)
        bd = mk[:, 0, :]
        maskt = NX[:, :].rearrange("p (k t e) -> p k t e", k=4, t=T)

        def over(ap, n):
            return ap.unsqueeze(2).broadcast_to([ap.shape[0], ap.shape[1], n])

        def in_order(engine, s):
            done = [0]

            def link(ins):
                done[0] += 1
                ins.then_inc(s, 1)
                engine.wait_ge(s, done[0])
            return link

        block = ctx.enter_context(nc.Block())

        @block.sync
        def _(sp):
            sp.dma_start(x3[:, 0, :], a["x"].rearrange("(t p) d -> t p d", p=P)[0]).then_inc(x_in[0], 16)
            sp.dma_start(KVRAW[:, :], a["kv0"]).then_inc(kv0_in, 16)
            for t in range(1, T):
                sp.dma_start(x3[:, t, :], a["x"].rearrange("(t p) d -> t p d", p=P)[t]).then_inc(x_in[t], 16)
            sp.dma_start(CONST[:, 0:465], a["consts"]).then_inc(consts_in, 16)
            sp.dma_start(STG[:, 0:2048], a["wq"]).then_inc(wq_in, 16)
            sp.dma_start(CONST[:, 896:1152], a["ssm"]).then_inc(ssm_in, 16)
            sp.dma_start(STG[:, 4096:8192], a["fold_qk"]).then_inc(fold0_in[0], 16)
            sp.dma_start(STG[:, 2048:4096], a["wout"]).then_inc(wout_in, 16)
            sp.dma_start(KVROT[:, :], a["kv1"][:, 2048:4096]).then_inc(kv1_in, 16)
            sp.dma_start(ROPE[:, :], a["kv1"][:, 4096:4608]).then_inc(kv1_in, 16)
            sp.wait_ge(wq_split_rest, 1)
            sp.wait_ge(wq_split, 1)
            sp.wait_ge(wout_split, 1)
            sp.dma_start(STG[:, 0:4096], a["fold_vo"]).then_inc(fold0_in[1], 16)
            sp.wait_ge(*full(("Wqk", KC - 1)))
            for i in (2, 3):
                sp.dma_start(stg4[:, i, :], a["fc"][i]).then_inc(fc_in[i], 16)
            sp.wait_ge(*full(("O", G0 - 1, 1)))
            sp.dma_start(KVF[:, :], a["kv1"][:, 0:2048]).then_inc(kv1_in, 16)
            sp.wait_ge(*full(("Wvo", KC - 1)))
            for i in (0, 1):
                sp.dma_start(stg4[:, i, :], a["fc"][i]).then_inc(fc_in[i], 16)
            for i in range(4):
                sp.wait_ge(fc_signed, i + 1)
                sp.dma_start(stg4[:, i, :], a["pj"][i]).then_inc(pj_in[i], 16)
            sp.wait_ge(pj_signed, 4)
            sp.dma_start(STG[:, 0:4352], a["queries"][0]).then_inc(query_in[0], 16)
            sp.dma_start(kr_raw, a["kr"]).then_inc(kr_in, 16)
            sp.dma_start(STG[:, 4352:6912], a["values"][0]).then_inc(value_in[0], 16)
            for g in range(1, G1):
                sp.wait_ge(*full(("w3", g - 1, 1)))
                sp.dma_start(STG[:, 0:4352], a["queries"][g]).then_inc(query_in[g], 16)
                if g >= 2:
                    sp.wait_ge(*full(("wo2", g - 2, HG - 1)))
                    sp.dma_start(STG[:, 4352:6912], a["values"][g - 1]).then_inc(value_in[g - 1], 16)
            sp.wait_ge(*full(("wo2", G1 - 2, HG - 1)))
            sp.dma_start(STG[:, 4352:6912], a["values"][G1 - 1]).then_inc(value_in[G1 - 1], 16)
            sp.wait_ge(*full(("wo2", G1 - 1, HG - 1)))
            sp.wait_ge(kr_split, 1)
            sp.dma_start(STG[:, 6144:7200], a["agu"]).then_inc(agu_in, 16)
            for f in range(NF):
                if f >= 2:
                    sp.wait_ge(ring_split, f - 1)
                sp.dma_start(STG[:, 2048 * (f % 2):2048 * (f % 2) + CH], a["mlp"][f]).then_inc(ring_in[f % 2], 16)
                if f in (4, 5, 6):
                    j = f - 4
                    w = slice(2048 * j, 2048 * j + 512 * min(4, NF - 4 * j))
                    sp.dma_start(WDF[:, w], a["wd"][:, w]).then_inc(wd_in[j], 16)
                if f == 2:
                    sp.wait_ge(um_made, 4)
                    sp.dma_start(bd, a["bd"]).then_inc(bd_in, 16)
            for t in range(T):
                sp.wait_ge(x_final, t + 1)
                sp.dma_start(out.rearrange("(t p) d -> t p d", p=P)[t], x3[:, t, :]).then_inc(out_done, 16)
            sp.wait_ge(out_done, 16 * T)

        @block.tensor
        def _(pe):
            def begin(x):
                if turn_of[x] > 1:
                    pe.wait_ge(bank_free[bank_of[x]], turn_of[x] - 1)
                return psum(x)

            def three(o, w, m, start, stop):
                pe.matmul(o, w[0], m[0], start=start, stop=False)
                pe.matmul(o, w[0], m[1], start=False, stop=False)
                return pe.matmul(o, w[1], m[0], start=False, stop=stop)

            def filled(x, last):
                last.then_inc(bank_full[bank_of[x]], 1)

            def to_features(name, i, src):
                o = begin((name, i))
                for j in range(4):
                    last = pe.transpose(o[:, P * j:P * (j + 1)], src(j), ident)
                filled((name, i), last)

            def keys0(g):
                o = begin(("K", g))
                filled(("K", g), pe.matmul(o[:, :], KVRAW[:, 512 + P * g:512 + P * (g + 1)], KVRAW[:, 0:512],
                                           start=True, stop=True))

            pe.wait_ge(kv0_in, 16)
            keys0(0)
            keys0(1)
            for p in range(4):
                o = begin(("V", p))
                filled(("V", p), pe.matmul(o[:, :], KVRAW[:, P * p:P * (p + 1)], KVRAW[:, 1024:1536],
                                           start=True, stop=True))
            pe.wait_ge(consts_in, 16)
            for t in range(T):
                pe.wait_ge(normed, t + 1)
                to_features("T0", t, lambda j: n0[:, t, P * j:P * (j + 1)])
            pe.wait_ge(wq_split, 1)
            pe.wait_ge(wq_split_rest, 1)
            for t in range(T):
                pe.wait_ge(*emptied(("T0", t)))
            def queries0(m):
                o = begin(("q", m))
                for k in range(KC):
                    last = three(o[:, :], [wq[:, s, k, P * m:P * (m + 1)] for s in (0, 1)],
                                 [xt[:, s, k, :] for s in (0, 1)], k == 0, k == KC - 1)
                filled(("q", m), last)

            def scores0(g):
                pe.wait_ge(*emptied(("q", g)))
                pe.wait_ge(*emptied(("K", g)))
                for i in (0, 1):
                    o = begin(("S", g, i))
                    for b in range(4 * i, 4 * i + 4):
                        last = pe.matmul(o[64 * (b % 2):64 * (b % 2) + 64, 256 * (b // 2 % 2):256 * (b // 2 % 2) + 256],
                                         qt[:, g, SQ * b:SQ * (b + 1)],
                                         kbd[:, g % 2, b, :, :].rearrange("p h k -> p (h k)"), start=True, stop=True)
                    filled(("S", g, i), last)

            def probs0_transposed(g):
                pe.wait_ge(p0_ready, g + 1)
                for i in (0, 1):
                    o = begin(("PT", g, i))
                    for t in (0, 1):
                        for m in (0, 1):
                            at = 256 * (2 * i + t) + P * m
                            last = pe.transpose(o[:, 256 * t + P * m:256 * t + P * (m + 1)],
                                                pr[:, g % 2, at:at + P], ident)
                    filled(("PT", g, i), last)

            def values0(g):
                for i in (0, 1):
                    pe.wait_ge(*emptied(("PT", g, i)))
                    for p in (2 * i, 2 * i + 1):
                        pe.wait_ge(*emptied(("V", p)))
                    o = begin(("O", g, i))
                    for t in (0, 1):
                        for m in (0, 1):
                            last = pe.matmul(o[:, 256 * t + P * m:256 * t + P * (m + 1)], ptb[:, g % 2, 2 * i + t, m, :],
                                             vbd[:, 2 * g + m, 2 * (2 * i + t):2 * (2 * i + t) + 2, :]
                                             .rearrange("p b x -> p (b x)"), start=True, stop=True)
                    filled(("O", g, i), last)

            def fold0(name, n, raw, loaded):
                pe.wait_ge(loaded, 16)
                o = begin((name, n))
                for k in range(KC):
                    last = pe.matmul(o[:, :], raw[:, 512 * k + P * n:512 * k + P * (n + 1)],
                                     raw[:, 2048 + 512 * k:2048 + 512 * (k + 1)], start=(k == 0), stop=(k == KC - 1))
                filled((name, n), last)

            fold_qk = lambda n: fold0("Wqk", n, STG[:, 4096:8192], fold0_in[0])
            fold_vo = lambda n: fold0("Wvo", n, STG[:, 0:4096], fold0_in[1])
            queries0(0)
            queries0(1)
            scores0(0)
            keys0(2)
            queries0(2)
            scores0(1)
            keys0(3)
            queries0(3)
            probs0_transposed(0)
            scores0(2)
            values0(0)
            fold_qk(0)
            probs0_transposed(1)
            scores0(3)
            values0(1)
            fold_qk(1)
            probs0_transposed(2)
            values0(2)
            fold_qk(2)
            probs0_transposed(3)
            values0(3)
            for t in range(T):
                pe.wait_ge(*emptied(("O", G0 - 1, t // 2)))
                to_features("TO", t, lambda j: otok[:, t, P * j:P * (j + 1)])
            fold_qk(3)
            pe.wait_ge(wout_split, 1)
            for t in range(T):
                pe.wait_ge(*emptied(("TO", t)))
                o = begin(("y0", t))
                for k in range(KC):
                    last = three(o[:, :], [xt[:, s, k, P * t:P * (t + 1)] for s in (0, 1)],
                                 [wout[:, s, k, :] for s in (0, 1)], k == 0, k == KC - 1)
                filled(("y0", t), last)

            fold_vo(0)
            fold_vo(1)
            for c in range(KC):
                begin(("T1", c))
            for t in range(T):
                pe.wait_ge(normed, T + t + 1)
                for c in range(KC):
                    last = pe.transpose(psum(("T1", c))[:, P * t:P * (t + 1)], nx[:, t, P * c:P * (c + 1)], ident)
                    if t == T - 1:
                        filled(("T1", c), last)
            fold_vo(2)
            fold_vo(3)
            for n in range(KC):
                pe.wait_ge(*emptied(("Wqk", n)))
            for c in range(KC):
                pe.wait_ge(*emptied(("T1", c)))
            for m in range(KC):
                o = begin(("t", m))
                for k in range(KC):
                    last = three(o[:, :], [wqk[:, s, k, P * m:P * (m + 1)] for s in (0, 1)],
                                 [xt[:, s, k, :] for s in (0, 1)], k == 0, k == KC - 1)
                filled(("t", m), last)
            for m in range(KC):
                pe.wait_ge(*emptied(("t", m)))
            o = begin(("s1",))
            for t in range(T):
                for k in range(KC):
                    last = pe.matmul(o[:, P * t:P * (t + 1)], tt[:, k, P * t:P * (t + 1)], xf[:, k, P * t:P * (t + 1)],
                                     start=(k == 0), stop=(k == KC - 1))
            filled(("s1",), last)
            pe.wait_ge(fc_summed, 4)
            o = begin(("wf",))
            filled(("wf",), pe.matmul(o[:, 0:4], ones, parts[:, 0:4], start=True, stop=True))
            for n in range(KC):
                pe.wait_ge(*emptied(("Wvo", n)))

            def values1(t):
                o = begin(("v", t))
                for k in range(KC):
                    last = three(o[:, :], [xt[:, s, k, P * t:P * (t + 1)] for s in (0, 1)],
                                 [wvo[:, s, k, :] for s in (0, 1)], k == 0, k == KC - 1)
                filled(("v", t), last)

            def output1(t):
                pe.wait_ge(*emptied(("v", t)))
                o = begin(("y1", t))
                filled(("y1", t), pe.matmul(o[:, :], PT1[:, P * t:P * (t + 1)], vf[:, t, :], start=True, stop=True))

            values1(0)
            values1(1)
            pe.wait_ge(p1_exp, 1)
            o = begin(("pt1",))
            for t in range(T):
                last = pe.transpose(o[:, P * t:P * (t + 1)], P1[:, P * t:P * (t + 1)], ident)
            filled(("pt1",), last)
            pe.wait_ge(*emptied(("pt1",)))
            output1(0)
            output1(1)
            values1(2)
            values1(3)
            output1(2)
            output1(3)

            def tokens0(t):
                pe.wait_ge(normed, 2 * T + t + 1)
                to_features("T2", t, lambda j: nx[:, t, P * j:P * (j + 1)])

            def up0(t):
                pe.wait_ge(*emptied(("T2", t)))
                for n in range(NFB):
                    o = begin(("fc", t, n))
                    for k in range(KC):
                        if t == 0:
                            pe.wait_ge(fc_signed, k + 1)
                        for s in (0, 1):
                            last = pe.matmul(o[:, :], xt[:, s, k, P * t:P * (t + 1)], fct[:, k, 512 * n:512 * (n + 1)],
                                             start=(k == 0 and s == 0), stop=(k == KC - 1 and s == 1))
                    filled(("fc", t, n), last)

            def hidden_transposed(t):
                pe.wait_ge(h_quant, t + 1)
                for j in range(4):
                    o = begin(("TH", t, j))
                    for i in range(4):
                        f = 4 * j + i
                        last = pe.transpose(o[:, P * i:P * (i + 1)], hb[:, t % 2, P * f:P * (f + 1)], ident)
                    filled(("TH", t, j), last)

            def tokens1(t):
                pe.wait_ge(normed, 3 * T + t + 1)
                to_features("T3", t, lambda j: nx[:, t, P * j:P * (j + 1)])

            def down0(t):
                o = begin(("y2", t))
                for f in range(F0 // P):
                    if t == T - 1 and f == 12:
                        for i in range(T - 1):
                            tokens1(i)
                    if f % 4 == 0:
                        pe.wait_ge(*emptied(("TH", t, f // 4)))
                        if t == 0:
                            pe.wait_ge(pj_signed, f // 4 + 1)
                    for s in (0, 1):
                        last = pe.matmul(o[:, :], ht[:, t % 2, s, f, :], pjt[:, f, :],
                                         start=(f == 0 and s == 0), stop=(f == F0 // P - 1 and s == 1))
                filled(("y2", t), last)

            def fold_queries(g, step):
                if step == 0:
                    pe.wait_ge(query_in[g], 16)
                    o = begin(("w12", g))
                    for h in range(HG):
                        for k in range(3):
                            last = pe.matmul(o[:, R1 * h:R1 * (h + 1)], kcq[:, h, k, :], wqr[:, h, k, :],
                                             start=(k == 0), stop=(k == 2))
                    filled(("w12", g), last)
                else:
                    i = step - 1
                    pe.wait_ge(*emptied(("w12", g)))
                    o = begin(("w3", g, i))
                    for c in (2 * i, 2 * i + 1):
                        for h in range(HG):
                            at = 256 * (c % 2) + R1 * h
                            last = pe.matmul(o[:, at:at + R1], wq1[:, h, P * c:P * (c + 1)], w12[:, R1 * h:R1 * (h + 1)],
                                             start=True, stop=True)
                    filled(("w3", g, i), last)

            tokens0(0)
            tokens0(1)
            up0(0)
            tokens0(2)
            up0(1)
            pe.wait_ge(pj_summed, 4)
            o = begin(("wp",))
            filled(("wp",), pe.matmul(o[:, 0:4], ones, parts[:, 4:8], start=True, stop=True))
            tokens0(3)
            up0(2)
            hidden_transposed(0)
            down0(0)
            up0(3)
            hidden_transposed(1)
            down0(1)
            hidden_transposed(2)
            fold_queries(0, 0)
            down0(2)
            fold_queries(0, 1)
            fold_queries(0, 2)
            hidden_transposed(3)
            down0(3)

            pe.wait_ge(kv_roped, 1)
            for j in range(4):
                o = begin(("kn", j))
                for i in range(4):
                    at = P * (4 * j + i)
                    last = pe.transpose(o[:, P * i:P * (i + 1)], kv_raw[:, at:at + P], ident)
                filled(("kn", j), last)

            def fold_values(g, h):
                if h == 0:
                    pe.wait_ge(value_in[g], 16)
                o = begin(("wo2", g, h))
                filled(("wo2", g, h), pe.matmul(o[:, :], kckv[:, h, :], woT[:, h, :], start=True, stop=True))

            def queries(g, i):
                for j in (0, 1):
                    pe.wait_ge(*emptied(("w3", g, j)))
                o = begin(("qr", g, i))
                for k in range(KC):
                    last = three(o[:, :], [w3[:, s, k, P * i:P * (i + 1)] for s in (0, 1)],
                                 [xt[:, s, k, :] for s in (0, 1)], k == 0, k == KC - 1)
                filled(("qr", g, i), last)

            def queries_in_context(g, h):
                pe.wait_ge(*emptied(("qr", g, h // 2)))
                o = begin(("qp", g, h))
                r = slice(R1 * (h % 2), R1 * (h % 2) + R1)
                last = three(o[:, :], [kr[r, s, 2 * g + h // 2, :] for s in (0, 1)],
                             [qr[r, s, h // 2, :] for s in (0, 1)], True, True)
                filled(("qp", g, h), last)

            def scores(g, b):
                if b == 0:
                    for h in range(HG):
                        pe.wait_ge(*emptied(("qp", g, h)))
                o = begin(("sc", g, b))
                for i in (0, 1):
                    last = three(o[:, 256 * i:256 * (i + 1)],
                                 [qp[g % 2][:, s, b, 2 * i:2 * i + 2, :].rearrange("p h q -> p (h q)") for s in (0, 1)],
                                 [kvt[:, s, b, :] for s in (0, 1)], True, True)
                filled(("sc", g, b), last)

            def probs_transposed(g, b):
                pe.wait_ge(pw_ready, NB * g + b + 1)
                o = begin(("ptr", g, b))
                for i in (0, 1):
                    for k in (0, 1):
                        last = pe.transpose(o[:, 256 * k + P * i:256 * k + P * (i + 1)],
                                            pw[:, b % 4, i, P * k:P * (k + 1)], ident)
                filled(("ptr", g, b), last)

            def contexts(g, n):
                if g == 0:
                    pe.wait_ge(*emptied(("kn", n)))
                o = begin(("cc", g, n))
                for b in (2 * n, 2 * n + 1):
                    pe.wait_ge(*emptied(("ptr", g, b)))
                    for k in (0, 1):
                        last = three(o[:, 256 * (b % 2):256 * (b % 2) + 256], [kvn[:, s, b, k, :] for s in (0, 1)],
                                     [ptw[b % 4][:, s, k, :] for s in (0, 1)], k == 0, k == 1)
                filled(("cc", g, n), last)

            def output(g, t):
                if t == 0:
                    for h in range(HG):
                        pe.wait_ge(*emptied(("wo2", g, h)))
                pe.wait_ge(*emptied(("cc", g, t)))
                o = begin(("y3", g, t))
                for h in range(HG):
                    last = three(o[:, :], [cc[:, s, h, P * t:P * (t + 1)] for s in (0, 1)],
                                 [wo2[:, s, h, :] for s in (0, 1)], h == 0, h == HG - 1)
                filled(("y3", g, t), last)

            fold_queries(1, 0)
            tokens1(T - 1)
            for t in range(T):
                pe.wait_ge(*emptied(("T3", t)))
            queries(0, 0)
            queries(0, 1)
            fold_values(0, 0)
            pe.wait_ge(kr_split, 1)
            for h in range(HG):
                queries_in_context(0, h)
            fold_values(0, 1)
            pe.wait_ge(kvt_split, 1)
            for n in range(STEPS):
                for x in attention_step(n):
                    if x[0] == "sc":
                        scores(*x[1:])
                    elif x[0] == "ptr":
                        probs_transposed(*x[1:])
                    elif x[0] == "w12":
                        fold_queries(x[1], 0)
                    elif x[0] == "w3":
                        fold_queries(x[1], 1 + x[2])
                    elif x[0] == "qr":
                        queries(*x[1:])
                    elif x[0] == "qp":
                        queries_in_context(*x[1:])
                    elif x[0] == "y3":
                        output(*x[1:])
                    elif x[0] == "wo2":
                        fold_values(*x[1:])
                    else:
                        contexts(*x[1:])

            for t in range(T):
                pe.wait_ge(normed, 4 * T + t + 1)
            for t in range(T):
                to_features("T4", t, lambda j: nxm[:, t, P * j:P * (j + 1)])
            for t in range(T):
                pe.wait_ge(*emptied(("T4", t)))
            pe.wait_ge(lag_tiles, KC)
            pe.wait_ge(lag_tiles_rest, KC)

            def lagged(c):
                o = begin(("YC", c))
                for l in range(LAGS):
                    n = 512 - SQ * l
                    last = three(o[:, SQ * l:], [lag_tile[s][:, c, l, :] for s in (0, 1)],
                                 [xt[:, s, c, 0:n] for s in (0, 1)], l == 0, l == LAGS - 1)
                filled(("YC", c), last)

            lagged(0)
            for c in range(KC):
                if c + 1 < KC:
                    lagged(c + 1)
                pe.wait_ge(*emptied(("YC", c)))
                to_features("TY", c, lambda j: ym[:, c, P * j:P * (j + 1)])

            for t in range(T):
                pe.wait_ge(normed, 5 * T + t + 1)
                to_features("T5", t, lambda j: nx[:, t, P * j:P * (j + 1)])
            pe.wait_ge(agu_split, 1)
            for t in range(T):
                pe.wait_ge(*emptied(("T5", t)))
            o = begin(("lt",))
            for k in range(KC):
                last = three(o[0:E1, :], [agu[:, s, 1024 + E1 * k:1024 + E1 * (k + 1)] for s in (0, 1)],
                             [xt[:, s, k, :] for s in (0, 1)], k == 0, k == KC - 1)
            filled(("lt",), last)

            def expert_inputs(n):
                x = (("ug",), ("uu",))[n]
                o = begin(x)
                for k in range(KC):
                    at = 512 * n + P * k
                    last = three(o[:, :], [agu[:, s, at:at + P] for s in (0, 1)], [xt[:, s, k, :] for s in (0, 1)],
                                 k == 0, k == KC - 1)
                filled(x, last)

            expert_inputs(0)
            pe.wait_ge(*emptied(("lt",)))
            o = begin(("lg",))
            for t in range(T):
                last = pe.transpose(o[:, E1 * t:E1 * (t + 1)], logits_t[0:E1, P * t:P * (t + 1)], ident[0:E1, 0:E1])
            filled(("lg",), last)
            expert_inputs(1)

            def mask_transposed(k):
                o = begin(("tm", k))
                for t in range(T):
                    last = pe.transpose(o[:, P * t:P * (t + 1)], maskt[:, k, t, :], ident)
                filled(("tm", k), last)

            def base(f, part):
                if part == 0:
                    begin(("gu", f, 0))
                    if f < 2:
                        pe.wait_ge(*emptied(("T5", 2 * f + 1)))
                    pe.wait_ge(ring_split, f + 1)
                o = bank[bank_of[("gu", f, 0)] + part]
                for k in range(KC):
                    at = 512 * part + P * k
                    last = three(o[:, :], [ring[:, f % 3, s, at:at + P] for s in (0, 1)],
                                 [xt[:, s, k, :] for s in (0, 1)], k == 0, k == KC - 1)
                if part == 1:
                    filled(("gu", f, 0), last)

            def expert(f, n):
                begin(("gu", f, n))
                if f == 0:
                    pe.wait_ge(um_split, 2 * n)
                for part in (0, 1):
                    at = 1024 + P * part
                    o = bank[bank_of[("gu", f, n)] + part]
                    w = [ring[:, f % 3, s, at:at + P] for s in (0, 1)]
                    m = [um[:, 2 * (n - 1) + part, s, :] for s in (0, 1)]
                    pe.matmul(o[:, :], w[0], m[0], start=False, stop=False, skip_group_check=True)
                    pe.matmul(o[:, :], w[0], m[1], start=False, stop=False, skip_group_check=True)
                    last = pe.matmul(o[:, :], w[1], m[0], start=False, stop=True, skip_group_check=True)
                filled(("gu", f, n), last)

            def expert_down(f, n):
                pe.wait_ge(hs_split, gates.index((f, n)) + 1)
                o = begin(("z", n)) if f == 0 else psum(("z", n))
                w = [ring[:, f % 3, s, 1280:1408] for s in (0, 1)]
                m = [hs[n - 1][:, s, :] for s in (0, 1)]
                pe.matmul(o[:, :], w[0], m[0], start=(f == 0), stop=False, skip_group_check=True)
                pe.matmul(o[:, :], w[0], m[1], start=False, stop=False, skip_group_check=True)
                last = pe.matmul(o[:, :], w[1], m[0], start=False, stop=(f == NF - 1), skip_group_check=True)
                if f == NF - 1:
                    filled(("z", n), last)
                elif n == 2:
                    last.then_inc(ring_used, 1)

            def down(t, chunks):
                for f in chunks:
                    if f == 0:
                        if t < 2:
                            pe.wait_ge(um_made, 4)
                        else:
                            begin(("y4", t))
                    if t == 0 and f % 4 == 0:
                        pe.wait_ge(wd_split, f // 4 + 1)
                    if f == NF - 1:
                        pe.wait_ge(hs_split, gates.index((f, 0)) + 1)
                    o = psum(("y4", t))
                    h, w = [h0t[:, s, f, P * t:P * (t + 1)] for s in (0, 1)], [wdt[:, s, f, :] for s in (0, 1)]
                    pe.matmul(o[:, :], h[0], w[0], start=(f == 0), stop=False, skip_group_check=True)
                    pe.matmul(o[:, :], h[0], w[1], start=False, stop=False, skip_group_check=True)
                    pe.matmul(o[:, :], h[1], w[0], start=False, stop=False, skip_group_check=True)

            base(0, 0)
            base(0, 1)
            pe.wait_ge(masks_ready, 1)
            mask_transposed(0)
            mask_transposed(1)
            base(1, 0)
            mask_transposed(2)
            mask_transposed(3)
            for f in range(NF):
                if f > 0:
                    expert_down(f - 1, 1)
                expert(f, 1)
                if 0 < f < NF - 1:
                    base(f + 1, 0)
                if f == NF - 1:
                    down(0, range(4))
                if f > 0:
                    expert_down(f - 1, 2)
                if f + 1 < NF:
                    base(f + 1, 1)
                expert(f, 2)
            down(0, range(4, 7))
            expert_down(NF - 1, 1)
            down(0, range(7, 10))
            expert_down(NF - 1, 2)
            down(0, range(10, NF))
            for t in range(T):
                if t > 0:
                    down(t, range(NF))
                if t == 0:
                    pe.wait_ge(z_made, 1)
                    pe.wait_ge(bd_in, 16)
                filled(("y4", t), pe.matmul(psum(("y4", t))[:, :], hh[0][:, P * t:P * (t + 1)], bd, start=False, stop=True,
                                            skip_group_check=True))

        @block.scalar
        def _(act):
            def high(dst, x, done, src=None):
                act.wait_ge(*full(x))
                act.copy(dst, psum(x)[:, :] if src is None else src).then_inc(done, 1)

            def copy_out(dst, x, src=None):
                act.wait_ge(*full(x))
                act.copy(dst, psum(x)[:, :] if src is None else src).then_inc(*freed(x))

            def high_tile(name, t, done):
                high(xt_tiles[:, 0, :, t, :], (name, t), done, psum((name, t))[:, :].rearrange("p (c n) -> p c n", c=KC))

            def key_blocks(g):
                x = ("K", g)
                act.wait_ge(*full(x))
                if g >= 2:
                    act.wait_ge(*full(("S", g - 2, 1)))
                for h in range(4):
                    r = slice(32 * h, 32 * h + 32)
                    last = act.copy(kbd[r, g % 2, :, h, :], psum(x)[r, :].rearrange("p (b k) -> p b k", b=NB))
                last.then_inc(*freed(x))

            act.wait_ge(zeroed, 2)
            key_blocks(0)
            key_blocks(1)
            for t in range(T):
                high_tile("T0", t, xt_high)
            for p in range(4):
                x = ("V", p)
                act.wait_ge(*full(x))
                for b in (0, 1):
                    src = psum(x)[64 * b:64 * b + 64, :].rearrange("p (m h x) -> p m h x", m=8, h=2)
                    for h in (0, 1):
                        last = act.copy(vbd[64 * h:64 * h + 64, :, 2 * p + b, 32 * h:32 * h + 32], src[:, :, h, :])
                last.then_inc(*freed(x))
            act.wait_ge(wout_in, 16)
            act.copy(WQO[:, 4096:6144], STG[:, 2048:4096]).then_inc(wout_high, 1)

            def queries_out0(m):
                copy_out(qt[:, m, :], ("q", m))

            def exp0(g):
                act.wait_ge(s0_ready, g + 1)
                act.activation(pr[:, g % 2, :], pr[:, g % 2, :], ACT.Exp).then_inc(p0_exp, 1)

            def probs_out0(g):
                for i in (0, 1):
                    copy_out(ptb[:, g % 2, 2 * i:2 * i + 2, :, :].rearrange("p t m n -> p (t m n)"), ("PT", g, i))

            def out0(g):
                for i in (0, 1):
                    x = ("O", g, i)
                    act.wait_ge(*full(x))
                    src = psum(x)[:, :].rearrange("p (t m b x) -> p t m b x", t=2, m=2, b=2)
                    for b in (0, 1):
                        r = slice(64 * b, 64 * b + 64)
                        dst = otok[r, 2 * i:2 * i + 2, P * g:P * (g + 1)].rearrange("p t (m x) -> p t m x", m=2)
                        last = act.copy(dst, src[r, :, :, b, :])
                    last.then_inc(*freed(x))

            def fold_high(name, n):
                high((wqk if name == "Wqk" else wvo)[:, 0, n, :], (name, n), fold0_high)

            queries_out0(0)
            queries_out0(1)
            key_blocks(2)
            queries_out0(2)
            exp0(0)
            key_blocks(3)
            queries_out0(3)
            exp0(1)
            probs_out0(0)
            out0(0)
            act.wait_ge(ssm_in, 16)
            act.activation(ssm[:, 0:2, :, :], ssm[:, 0:2, :, :], ACT.Exp, scale=-1.0).then_inc(exp_made, 1)
            fold_high("Wqk", 0)
            exp0(2)
            probs_out0(1)
            out0(1)
            exp0(3)
            fold_high("Wqk", 1)
            probs_out0(2)
            out0(2)
            fold_high("Wqk", 2)
            probs_out0(3)
            out0(3)
            for t in range(T):
                high_tile("TO", t, ot_high)
            fold_high("Wqk", 3)
            fold_high("Wvo", 0)
            fold_high("Wvo", 1)
            for c in range(KC):
                act.wait_ge(*full(("T1", c)))
                act.activation(xt[:, 0, c, :], psum(("T1", c))[:, :], ACT.Identity, scale=gammaT[:, c:c + 1],
                               bias=betaT[:, c:c + 1]).then_inc(xt_high, 1)
            fold_high("Wvo", 2)
            fold_high("Wvo", 3)
            for m in range(KC):
                copy_out(tt[:, m, :], ("t", m))
            act.wait_ge(kv_roped, 1)
            act.copy(KVT[:, 0:2048], kv_raw).then_inc(kvt_high, 1)
            act.wait_ge(s1_ready, 1)
            act.activation(P1[:, :], P1[:, :], ACT.Exp).then_inc(p1_exp, 1)
            for t in (0, 1):
                copy_out(vf[:, t, :], ("v", t))
            copy_out(PT1[:, :], ("pt1",))
            def signs(i, rounded, signed, dst):
                act.wait_ge(rounded, 1)
                act.activation(dst[:, 2048 * i:2048 * (i + 1)], stg4[:, i, :], ACT.Sign, bias=minus_magic).then_inc(signed, 1)

            signs(0, fc_rounded[0], fc_signed, FCT)
            signs(1, fc_rounded[1], fc_signed, FCT)
            copy_out(vf[:, 2, :], ("v", 2))
            signs(2, fc_rounded[2], fc_signed, FCT)
            copy_out(vf[:, 3, :], ("v", 3))
            signs(3, fc_rounded[3], fc_signed, FCT)

            def gelu(t, blocks):
                for n in blocks:
                    x = ("fc", t, n)
                    act.wait_ge(*full(x))
                    if t >= 2:
                        act.wait_ge(*full(("TH", t - 2, 3)))
                    act.activation(hb[:, t % 2, 512 * n:512 * (n + 1)], psum(x)[:, :], ACT.Gelu,
                                   scale=wtot[:, 2:3]).then_inc(*freed(x))

            def norm_hidden(t):
                act.wait_ge(h_scales, t + 1)
                u = 8 * (t % 2)
                act.activation(hb[:, t % 2, :], hb[:, t % 2, :], ACT.Identity, scale=hsc[:, u:u + 1],
                               bias=hsc[:, u + 1:u + 2]).then_inc(h_normed, 1)

            def hidden_high(t, blocks=range(4)):
                for j in blocks:
                    high(ht[:, t % 2, 0, 4 * j:4 * j + 4, :].rearrange("p f n -> p (f n)"), ("TH", t, j), ht_high)

            def fold_high1(x):
                name, g, i = x[0], x[1], x[-1]
                if name == "w12":
                    copy_out(w12, x, psum(x)[:, 0:256])
                elif name == "w3":
                    high(w3[:, 0, 2 * i:2 * i + 2, :].rearrange("p c r -> p (c r)"), x, w3_high)
                elif name == "wo2":
                    high(wo2[:, 0, i, :], x, wo2_high)
                elif name == "qr":
                    high(qr[:, 0, i, :], x, qr_high)
                elif name == "qp":
                    high(qp[g % 2][:, 0, :, i, :], x, qp_high, psum(x)[:, :].rearrange("p (b q) -> p b q", b=NB))

            def abs_sum(i):
                act.wait_ge(pj_in[i], 16)
                act.activation(PJT[:, 2048 * i:2048 * (i + 1)], stg4[:, i, :], ACT.Abs,
                               accum_out=parts[:, 4 + i:5 + i]).then_inc(pj_summed, 1)

            every = range(NFB)
            high_tile("T2", 0, xt_high)
            high_tile("T2", 1, xt_high)
            gelu(0, (0,))
            abs_sum(0)
            gelu(0, (1, 2))
            abs_sum(1)
            gelu(0, (3,))
            high_tile("T2", 2, xt_high)
            abs_sum(2)
            abs_sum(3)
            norm_hidden(0)
            gelu(1, every)
            high_tile("T2", 3, xt_high)
            signs(0, pj_rounded[0], pj_signed, PJT)
            signs(1, pj_rounded[1], pj_signed, PJT)
            hidden_high(0, (0,))
            gelu(2, (0,))
            hidden_high(0, (1, 2, 3))
            signs(2, pj_rounded[2], pj_signed, PJT)
            gelu(2, (1,))
            signs(3, pj_rounded[3], pj_signed, PJT)
            norm_hidden(1)
            gelu(2, (2, 3))
            hidden_high(1, (0,))
            gelu(3, (0,))
            hidden_high(1, (1, 2, 3))
            norm_hidden(2)
            gelu(3, (1, 2, 3))
            hidden_high(2)
            norm_hidden(3)
            for x in (("w12", 0), ("w3", 0, 0), ("w3", 0, 1)):
                fold_high1(x)
            hidden_high(3)

            for t in range(T - 1):
                high_tile("T3", t, xt_high)
            act.wait_ge(*full(("y2", 3)))
            act.wait_ge(kr_in, 16)
            act.copy(KR[:, 0:1024], kr_raw).then_inc(kr_high, 1)
            for j in range(4):
                high(kvn[:, 0, 2 * j:2 * j + 2, :, :].rearrange("p b k d -> p (b k d)"), ("kn", j), kvn_high)

            fold_high1(("w12", 1))
            high_tile("T3", T - 1, xt_high)
            for x in [("qr", 0, 0), ("qr", 0, 1), ("wo2", 0, 0)] + [("qp", 0, h) for h in range(HG)] + [("wo2", 0, 1)]:
                fold_high1(x)
            for n in range(STEPS):
                for x in attention_step(n):
                    if x[0] == "sc":
                        u = 16 * (n % 4)
                        act.wait_ge(max_made, n + 1)
                        act.activation(pw[:, n % 4, 0, :], psum(x)[:, 0:256], ACT.Exp, bias=mxs[:, u:u + 1],
                                       accum_out=mxs[:, u + 2:u + 3]).then_inc(sums_made, 1)
                        act.activation(pw[:, n % 4, 1, :], psum(x)[:, 256:512], ACT.Exp, bias=mxs[:, u + 1:u + 2],
                                       accum_out=mxs[:, u + 3:u + 4]).then_inc(*freed(x))
                    elif x[0] == "ptr":
                        b = x[2]
                        if n >= 6:
                            pair = (n - 6) // 2
                            act.wait_ge(*full(("cc", pair // T, pair % T)))
                        high(ptw[b % 4][:, 0, :, :].rearrange("p k n -> p (k n)"), x, ptw_high)
                    elif x[0] == "cc":
                        t = x[2]
                        high(cc[:, 0, :, P * t:P * (t + 1)].rearrange("p h (b q) -> p b h q", b=2), x, cc_high,
                             psum(x)[:, :].rearrange("p (b h q) -> p b h q", b=2, h=HG))
                    else:
                        fold_high1(x)

            for t in range(T):
                high_tile("T4", t, xt_high)
            act.wait_ge(agu_in, 16)
            act.copy(agu[:, 0, :], STG[:, 6144:7200]).then_inc(agu_high, 1)

            def chunk_high(f):
                act.wait_ge(ring_in[f % 2], 16 * (f // 2 + 1))
                if f >= 3:
                    act.wait_ge(ring_used, f - 2)
                act.copy(ring[:, f % 3, 0, :], STG[:, 2048 * (f % 2):2048 * (f % 2) + CH]).then_inc(ring_high, 1)

            def down_high(j):
                w = slice(2048 * j, 2048 * j + 512 * min(4, NF - 4 * j))
                act.wait_ge(wd_in[j], 16)
                act.copy(WDT[:, w], WDF[:, w]).then_inc(wd_high, 1)

            chunk_high(0)
            chunk_high(1)
            for c in range(KC):
                x = ("YC", c)
                act.wait_ge(*full(x))
                act.activation(ym[:, c, :], psum(x)[:, :], ACT.Silu).then_inc(*freed(x))
            for t in range(T):
                high_tile("T5", t, xt_high)
            chunk_high(2)
            copy_out(logits_t[0:E1, :], ("lt",), psum(("lt",))[0:E1, :])
            copy_out(rt[:, 0, :, :], ("lg",), psum(("lg",))[:, 0:T * E1].rearrange("p (t e) -> p t e", t=T))
            act.wait_ge(rt_ready, 1)
            act.activation(rt[:, 0, :, :], rt[:, 0, :, :], ACT.Exp).then_inc(rt_exp, 1)

            def gate(k):
                x = ("gu",) + gates[k]
                act.wait_ge(*full(x))
                if k == 1:
                    act.wait_ge(um_split, 3)
                if k >= 2:
                    act.wait_ge(*emptied(("gu",) + gates[k - 2]))
                act.activation(sg[k % 2], psum(x)[:, :], ACT.Silu).then_inc(silu_made, 1)

            def gated_high(k):
                f, n = gates[k]
                act.wait_ge(*emptied(("gu", f, n)))
                act.copy(h0t[:, 0, f, :] if n == 0 else hs[n - 1][:, 0, :], hh[k % 2]).then_inc(hs_high, 1)

            for k in (0, 1):
                copy_out(mk[:, k, :], ("tm", k))
            for k in range(4):
                act.wait_ge(um_made, k + 1)
                act.copy(um[:, k, 0, :], (sg[1], hh[1])[k % 2]).then_inc(um_high, 1)
                if k == 1:
                    gate(0)
                    gated_high(0)
            for k in range(1, len(gates)):
                f, n = gates[k]
                gate(k)
                gated_high(k)
                if k == 1:
                    for i in (2, 3):
                        copy_out(mk[:, i, :], ("tm", i))
                if n == 1 and 1 <= f < NF - 2:
                    chunk_high(f + 2)
                if n == 2 and 5 <= f < 8:
                    down_high(f - 5)

        @block.vector
        def _(dve):
            link = in_order(dve, dve_step)

            def low(dst, x, high_done, count, high, src=None):
                dve.wait_ge(high_done, count)
                dve.tensor_tensor(dst, psum(x)[:, :] if src is None else src, high.bitcast(F32),
                                  ALU.subtract).then_inc(*freed(x))

            def low_tile(name, t, high_done, count):
                low(xt_tiles[:, 1, :, t, :], (name, t), high_done, count, xt_tiles[:, 0, :, t, :],
                    psum((name, t))[:, :].rearrange("p (c n) -> p c n", c=KC))

            var_count = [0]

            def rsqrt(v, y, s):
                link(dve.tensor_scalar(s.bitcast(I32), v.bitcast(I32), 1, None, ALU.logical_shift_right))
                link(dve.tensor_scalar(y.bitcast(I32), s.bitcast(I32), -1.0, RSQRT_SEED, ALU.mult, ALU.add))
                for _ in range(3):
                    link(dve.tensor_tensor(s, y, y, ALU.mult))
                    link(dve.scalar_tensor_tensor(out=s, in0=s, scalar=-0.5, in1=v, op0=ALU.mult, op1=ALU.mult))
                    link(dve.scalar_tensor_tensor(out=y, in0=s, scalar=1.5, in1=y, op0=ALU.add, op1=ALU.mult))

            def rsqrt_column(v, y, s, h):
                link(dve.tensor_scalar(s.bitcast(I32), v.bitcast(I32), 1, None, ALU.logical_shift_right))
                link(dve.tensor_scalar(y.bitcast(I32), s.bitcast(I32), -1.0, RSQRT_SEED, ALU.mult, ALU.add))
                for _ in range(3):
                    link(dve.scalar_tensor_tensor(out=s, in0=y, scalar=y, in1=h, op0=ALU.mult, op1=ALU.mult))
                    link(dve.scalar_tensor_tensor(out=y, in0=s, scalar=1.5, in1=y, op0=ALU.add, op1=ALU.mult))

            def x_stats(t):
                link(dve.bn_stats(stats[:, t, :], x3[:, t, :]))
                dve.bn_aggr(mv[:, t, :], stats[:, t, :]).then_inc(x_stat, 1)

            def scales(first, lo, hi, eps1, eps2=None, both=False):
                dve.wait_ge(x_stat, T * first + hi)
                v = mv[:, lo:hi, 1]
                if hi - lo == 1 and eps2 is None:
                    h = rs_t[:, 1, lo:hi]
                    dve.tensor_scalar(var2[:, 0, lo:hi], v, eps1, None, ALU.add).then_inc(var_made, 1)
                    dve.tensor_scalar(h, v, -0.5, -0.5 * eps1, ALU.mult, ALU.add).then_inc(var_made, 1)
                    var_count[0] += 2
                    dve.wait_ge(var_made, var_count[0])
                    rsqrt_column(var2[:, 0, lo:hi], rs[:, 0, lo:hi], rs_t[:, 0, lo:hi], h)
                    return
                if eps2 is None or both:
                    link(dve.tensor_scalar(var2[:, 0, lo:hi], v, eps1, None, ALU.add))
                if eps2 is not None:
                    link(dve.tensor_scalar(var2[:, int(both), lo:hi], v, 1.0 + eps2, eps1 * eps2, ALU.mult, ALU.add))
                rows = slice(0, 2 if both else 1)
                rsqrt(var2[:, rows, lo:hi], rs[:, rows, lo:hi], rs_t[:, rows, lo:hi])

            def normalise(dst, lo, hi, row=0):
                for t in range(lo, hi):
                    dve.tensor_scalar(dst[:, t, :], x3[:, t, :], mv[:, t, 0:1], rs[:, row, t:t + 1],
                                      ALU.subtract, ALU.mult).then_inc(normed, 1)

            def add_to_x(x, t):
                dve.wait_ge(*full(x))
                dve.tensor_tensor(x3[:, t, :], x3[:, t, :], psum(x)[:, :], ALU.add).then_inc(*freed(x))
                dve.wait_ge(*emptied(x))

            for t in range(T):
                dve.wait_ge(x_in[t], 16)
                x_stats(t)
            scales(0, 0, T, 1e-5)
            normalise(n0, 0, T)
            dve.wait_ge(wq_in, 16)
            dve.tensor_copy(WQO[:, 0:2048], STG[:, 0:2048]).then_inc(wq_high, 1)
            dve.wait_ge(wq_high, 1)
            dve.tensor_tensor(WQO[:, 2048:3072], STG[:, 0:1024], WQO[:, 0:1024].bitcast(F32), ALU.subtract).then_inc(wq_split, 1)
            for t in range(T):
                low_tile("T0", t, xt_high, t + 1)
            def mixer_rates():
                dve.wait_ge(pool_step, 2)
                dve.reciprocal(sw[:, 0, :, :], sw[:, 1, :, :]).then_inc(rates_made, 1)

            def rows16(g):
                return pr[:, g % 2, :].rearrange("p (r k) -> p r k", k=SQ)

            def softmax0_shift(g):
                if g >= 2:
                    dve.wait_ge(*full(("PT", g - 2, 1)))
                nm = nmax0[:, 16 * (g % 2):16 * (g % 2) + 16]
                for i in (0, 1):
                    x = ("S", g, i)
                    dve.wait_ge(*full(x))
                    dve.scalar_tensor_tensor(out=rows16(g)[:, 8 * i:8 * i + 8, :],
                                             in0=psum(x)[:, :].rearrange("p (r k) -> p r k", k=SQ), scalar=HD0 ** -0.5,
                                             in1=mask0.unsqueeze(1).broadcast_to([P, 8, SQ]), op0=ALU.mult,
                                             op1=ALU.add).then_inc(*freed(x))
                    dve.wait_ge(*emptied(x))
                link(dve.tensor_reduce(nm, rows16(g), AX_X, ALU.max, negate=True))
                dve.tensor_tensor(rows16(g), rows16(g), over(nm, SQ), ALU.add).then_inc(s0_ready, 1)

            def softmax0_divide(g):
                sm = rsum0[:, 16 * (g % 2):16 * (g % 2) + 16]
                dve.wait_ge(p0_exp, g + 1)
                link(dve.tensor_reduce(sm, rows16(g), AX_X, ALU.add))
                link(dve.reciprocal(sm, sm))
                dve.tensor_tensor(rows16(g), rows16(g), over(sm, SQ), ALU.mult).then_inc(p0_ready, 1)

            def fold_low(name, n):
                w_ = wqk if name == "Wqk" else wvo
                low(w_[:, 1, n, :], (name, n), fold0_high, n + 1 + (KC if name == "Wvo" else 0), w_[:, 0, n, :])

            softmax0_shift(0)
            softmax0_shift(1)
            softmax0_divide(0)
            softmax0_divide(1)
            softmax0_shift(2)
            fold_low("Wqk", 0)
            softmax0_divide(2)
            softmax0_shift(3)
            fold_low("Wqk", 1)
            softmax0_divide(3)
            mixer_rates()
            fold_low("Wqk", 2)
            for t in range(T):
                low_tile("TO", t, ot_high, t + 1)
            fold_low("Wqk", 3)
            for t in range(T):
                add_to_x(("y0", t), t)
                x_stats(t)
                if t == T - 2:
                    scales(1, 0, t + 1, 1e-5, 1e-5, both=True)
                    normalise(nx, 0, t + 1, 1)

            scales(1, T - 1, T, 1e-5, 1e-5, both=True)
            normalise(nx, T - 1, T, 1)
            fold_low("Wvo", 0)
            fold_low("Wvo", 1)
            for c in range(KC):
                x = ("T1", c)
                dve.wait_ge(xt_high, T + c + 1)
                link(dve.tensor_scalar(xf[:, c, :], psum(x)[:, :], gammaT[:, c:c + 1], betaT[:, c:c + 1], ALU.mult, ALU.add))
                low(xt[:, 1, c, :], x, xt_high, T + c + 1, xt[:, 0, c, :], xf[:, c, :])
            fold_low("Wvo", 2)
            fold_low("Wvo", 3)
            dve.wait_ge(states_made, 1)
            link(dve.tensor_reduce(lagw, lags_raw, AX_X, ALU.add))
            link(dve.tensor_copy(lag2[:, 0, :, :], lagw))
            dve.tensor_tensor(lag2[:, 1, :, :], lagw, lag2[:, 0, :, :].bitcast(F32), ALU.subtract).then_inc(lags_made, 1)
            link(dve.tensor_tensor(lnb, mv[:, :, 0], rs[:, 0, :], ALU.mult))
            link(dve.tensor_scalar(lna, rs[:, 0, :], 1.0, None, ALU.add))
            for t in range(T):
                link(dve.tensor_scalar(x3[:, t, :], x3[:, t, :], lna[:, t:t + 1], lnb[:, t:t + 1], ALU.mult, ALU.subtract))
            for i in (2, 3, 0, 1):
                dve.wait_ge(fc_in[i], 16)
                dve.tensor_reduce(parts[:, i:i + 1], stg4[:, i, :], AX_X, ALU.add, apply_absolute_value=True).then_inc(fc_summed, 1)
            p1 = P1[:, :].rearrange("p (t k) -> p t k", t=T)
            dve.wait_ge(*full(("s1",)))
            dve.scalar_tensor_tensor(out=p1, in0=psum(("s1",))[:, :].rearrange("p (t k) -> p t k", t=T), scalar=D ** -0.5,
                                     in1=mask1.unsqueeze(1).broadcast_to([P, T, P]), op0=ALU.mult,
                                     op1=ALU.add).then_inc(*freed(("s1",)))
            dve.wait_ge(*emptied(("s1",)))
            link(dve.tensor_reduce(nmax1[:, 0:4], p1, AX_X, ALU.max, negate=True))
            dve.tensor_tensor(p1, p1, over(nmax1[:, 0:4], P), ALU.add).then_inc(s1_ready, 1)

            def mean_abs(x, at, size):
                dve.wait_ge(*full(x))
                dve.tensor_reduce(wtot[:, at:at + 1], psum(x)[:, 0:4], AX_X, ALU.add).then_inc(*freed(x))
                dve.wait_ge(*emptied(x))
                link(dve.tensor_scalar(wtot[:, at + 2:at + 3], wtot[:, at:at + 1], 1.0 / size, None, ALU.mult))
                link(dve.tensor_scalar(wtot[:, at + 1:at + 2], wtot[:, at + 2:at + 3], 1e-6, None, ALU.add))
                dve.reciprocal(wtot[:, at + 3:at + 4], wtot[:, at + 1:at + 2]).then_inc(means_made, 1)
                dve.wait_ge(means_made, 1 + at // 8)

            def round_quarter(i, at, done):
                dve.tensor_scalar(stg4[:, i, :], stg4[:, i, :], wtot[:, at + 3:at + 4], MAGIC, ALU.mult,
                                  ALU.add).then_inc(done[i], 1)

            mean_abs(("wf",), 0, F0 * D)
            round_quarter(0, 0, fc_rounded)
            round_quarter(1, 0, fc_rounded)
            dve.wait_ge(p1_exp, 1)
            link(dve.tensor_reduce(rsum1[:, 0:4], p1, AX_X, ALU.add))
            link(dve.reciprocal(rsum1[:, 4:8], rsum1[:, 0:4]))

            def out1(t):
                x = ("y1", t)
                dve.wait_ge(*full(x))
                dve.scalar_tensor_tensor(out=x3[:, t, :], in0=psum(x)[:, :], scalar=rsum1[:, 4 + t:5 + t], in1=x3[:, t, :],
                                         op0=ALU.mult, op1=ALU.add).then_inc(*freed(x))
                dve.wait_ge(*emptied(x))
                x_stats(t)

            ticks = [0]

            def quantise(tile, gm, done):
                link(dve.reciprocal(gm[:, 1:2], gm[:, 0:1]))
                dve.tensor_scalar(gm[:, 3:4], gm[:, 0:1], 1.0 / 128.0, None, ALU.mult).then_inc(factors, 1)
                dve.tensor_scalar(gm[:, 2:3], gm[:, 1:2], 128.0, None, ALU.mult).then_inc(factors, 1)
                ticks[0] += 2
                dve.wait_ge(factors, ticks[0])
                link(dve.tensor_scalar(tile, tile, gm[:, 2:3], CLIP, ALU.mult, ALU.min))
                dve.tensor_scalar(tile, tile, -CLIP, gm[:, 3:4], ALU.max, ALU.mult).then_inc(done, 1)

            def tokens0(t):
                link(dve.tensor_scalar(nx[:, t, :], x3[:, t, :], mv[:, t, 0:1], rs[:, 0, t:t + 1], ALU.subtract, ALU.mult))
                gm = xabs[:, 4 * t:4 * t + 4]
                link(dve.tensor_reduce(gm[:, 0:1], nx[:, t, :], AX_X, ALU.max, apply_absolute_value=True))
                quantise(nx[:, t, :], gm, normed)

            out1(0)
            out1(1)
            scales(2, 0, 2, 1e-5, 1e-6)
            tokens0(0)
            tokens0(1)
            low_tile("T2", 0, xt_high, 2 * T + 1)
            out1(2)
            low_tile("T2", 1, xt_high, 2 * T + 2)
            out1(3)
            scales(2, 2, 4, 1e-5, 1e-6)
            tokens0(2)

            def hidden_stats(t):
                for n in range(NFB):
                    dve.wait_ge(*emptied(("fc", t, n)))
                    last = dve.bn_stats(hstats[:, t % 2, n, :], hb[:, t % 2, 512 * n:512 * (n + 1)])
                last.then_inc(h_stats, 1)

            def hidden_scales(t):
                u = 8 * (t % 2)
                dve.wait_ge(h_stats, t + 1)
                link(dve.bn_aggr(hmv[:, 0:2], hstats[:, t % 2, :, :].rearrange("p n k -> p (n k)")))
                dve.tensor_scalar(hmv[:, 2:3], hmv[:, 1:2], 1e-6, None, ALU.add).then_inc(var_made, 1)
                dve.tensor_scalar(hmv[:, 4:5], hmv[:, 1:2], -0.5, -0.5e-6, ALU.mult, ALU.add).then_inc(var_made, 1)
                var_count[0] += 2
                dve.wait_ge(var_made, var_count[0])
                rsqrt_column(hmv[:, 2:3], hsc[:, u:u + 1], hmv[:, 3:4], hmv[:, 4:5])
                dve.scalar_tensor_tensor(out=hsc[:, u + 1:u + 2], in0=hmv[:, 0:1], scalar=-1.0, in1=hsc[:, u:u + 1],
                                         op0=ALU.mult, op1=ALU.mult).then_inc(h_scales, 1)
                dve.wait_ge(h_scales, t + 1)

            def hidden_quantised(t):
                dve.wait_ge(h_normed, t + 1)
                gm = hsc[:, 8 * (t % 2) + 4:8 * (t % 2) + 8]
                link(dve.tensor_reduce(gm[:, 0:1], hb[:, t % 2, :], AX_X, ALU.max, apply_absolute_value=True))
                if t == 0:
                    mean_abs(("wp",), 8, F0 * D)
                quantise(hb[:, t % 2, :], gm, h_quant)

            def hidden_low(t):
                for j in range(4):
                    low(ht[:, t % 2, 1, 4 * j:4 * j + 4, :].rearrange("p f n -> p (f n)"), ("TH", t, j), ht_high, 4 * t + j + 1,
                        ht[:, t % 2, 0, 4 * j:4 * j + 4, :].rearrange("p f n -> p (f n)"))

            def out_hidden(t):
                x = ("y2", t)
                dve.wait_ge(*full(x))
                dve.scalar_tensor_tensor(out=x3[:, t, :], in0=psum(x)[:, :], scalar=wtot[:, 10:11], in1=x3[:, t, :],
                                         op0=ALU.mult, op1=ALU.add).then_inc(*freed(x))
                dve.wait_ge(*emptied(x))
                x_stats(t)

            def fold_low1(x):
                name, g, i = x[0], x[1], x[-1]
                if name == "w3":
                    low(w3[:, 1, 2 * i:2 * i + 2, :].rearrange("p c r -> p (c r)"), x, w3_high, 2 * g + i + 1,
                        w3[:, 0, 2 * i:2 * i + 2, :].rearrange("p c r -> p (c r)"))
                elif name == "wo2":
                    low(wo2[:, 1, i, :], x, wo2_high, HG * g + i + 1, wo2[:, 0, i, :])
                elif name == "qr":
                    low(qr[:, 1, i, :], x, qr_high, 2 * g + i + 1, qr[:, 0, i, :])
                elif name == "qp":
                    low(qp[g % 2][:, 1, :, i, :], x, qp_high, HG * g + i + 1, qp[g % 2][:, 0, :, i, :],
                        psum(x)[:, :].rearrange("p (b q) -> p b q", b=NB))

            hidden_stats(0)
            hidden_scales(0)
            low_tile("T2", 2, xt_high, 2 * T + 3)
            tokens0(3)
            hidden_quantised(0)
            low_tile("T2", 3, xt_high, 2 * T + 4)
            hidden_stats(1)
            hidden_low(0)
            hidden_scales(1)
            hidden_quantised(1)
            hidden_stats(2)
            hidden_scales(2)
            out_hidden(0)
            hidden_low(1)
            hidden_quantised(2)
            hidden_stats(3)
            hidden_scales(3)
            out_hidden(1)
            hidden_low(2)
            hidden_quantised(3)
            out_hidden(2)
            for i in (0, 1):
                fold_low1(("w3", 0, i))
            hidden_low(3)

            scales(3, 0, T - 1, 1e-5)
            normalise(nx, 0, T - 1)
            for t in range(T - 1):
                low_tile("T3", t, xt_high, 3 * T + t + 1)
            out_hidden(3)
            scales(3, T - 1, T, 1e-5)
            normalise(nx, T - 1, T)
            def context_low(j):
                s_ = slice(2 * j, 2 * j + 2)
                low(kvn[:, 1, s_, :, :].rearrange("p b k d -> p (b k d)"), ("kn", j), kvn_high, j + 1,
                    kvn[:, 0, s_, :, :].rearrange("p b k d -> p (b k d)"))

            context_low(0)
            context_low(1)
            low_tile("T3", T - 1, xt_high, 4 * T)
            context_low(2)
            context_low(3)
            for x in [("qr", 0, 0), ("qr", 0, 1), ("wo2", 0, 0)] + [("qp", 0, h) for h in range(HG)] + [("wo2", 0, 1)]:
                fold_low1(x)

            def lag_matrices(s, c):
                dve.tensor_tensor(lag_tile[s][:, c, :, :], ident.unsqueeze(1).broadcast_to([P, LAGS, P]),
                                  over(lag2[:, s, c, :].bitcast(F32), P), ALU.mult).then_inc(lag_tiles, 1)

            for n in range(STEPS):
                u = 16 * (n % 4)
                for x in attention_step(n):
                    if x[0] == "sc":
                        dve.wait_ge(*full(x))
                        dve.tensor_reduce(mxs[:, u:u + 2], psum(x)[:, :].rearrange("p (i k) -> p i k", i=2),
                                          AX_X, ALU.max, negate=True).then_inc(max_made, 1)
                    elif x[0] == "ptr":
                        b = x[2]
                        low(ptw[b % 4][:, 1, :, :].rearrange("p k n -> p (k n)"), x, ptw_high, n - 1,
                            ptw[b % 4][:, 0, :, :].rearrange("p k n -> p (k n)"))
                        if n < NB * G1:
                            dve.wait_ge(*emptied(("sc", n // NB, n % NB)))
                            dve.reciprocal(mxs[:, u + 4:u + 6], mxs[:, u + 2:u + 4]).then_inc(recip_made, 1)
                    elif x[0] == "cc":
                        g, t = x[1:]
                        view = [cc[:, k, :, P * t:P * (t + 1)].rearrange("p h (b q) -> p b h q", b=2) for k in (0, 1)]
                        low(view[1], x, cc_high, T * g + t + 1, view[0],
                            psum(x)[:, :].rearrange("p (b h q) -> p b h q", b=2, h=HG))
                    elif x[0] == "y3":
                        if x[1:] == (G1 - 1, T - 1):
                            scales(4, 0, T - 1, 1e-5)
                            normalise(nxm, 0, T - 1)
                        add_to_x(x, x[2])
                        if x[1] == G1 - 1:
                            x_stats(x[2])
                    else:
                        fold_low1(x)
                if 1 <= n - NB * (G1 - 1) <= KC:
                    if n == NB * (G1 - 1) + 1:
                        dve.wait_ge(*full(("sc", G1 - 2, NB - 1)))
                    if n % 2 == 0:
                        lag_matrices(0, n - NB * (G1 - 1) - 1)
                if n in (NB * G1, NB * G1 + 1):
                    dve.wait_ge(*full(("sc", G1 - 1, NB - 1)))
                    lag_matrices(1, n - NB * G1)
                if n < 2:
                    dve.wait_ge(*emptied(("sc", 0, n)))
                    dve.reciprocal(mxs[:, u + 4:u + 6], mxs[:, u + 2:u + 4]).then_inc(recip_made, 1)

            scales(4, T - 1, T, 1e-5)
            normalise(nxm, T - 1, T)
            for t in range(T):
                low_tile("T4", t, xt_high, 4 * T + t + 1)
            for c in range(KC):
                x = ("TY", c)
                dve.wait_ge(*full(x))
                dve.tensor_tensor(x3[:, :, P * c:P * (c + 1)], x3[:, :, P * c:P * (c + 1)],
                                  psum(x)[:, :].rearrange("p (t n) -> p t n", t=T), ALU.add).then_inc(*freed(x))
                dve.wait_ge(*emptied(x))
                for t in range(T):
                    last = dve.bn_stats(chunk_stats[:, t, c, :], x3[:, t, P * c:P * (c + 1)])
            link(last)
            for t in range(T):
                dve.bn_aggr(mv[:, t, :], chunk_stats[:, t, :, :].rearrange("p c k -> p (c k)")).then_inc(x_stat, 1)
            scales(5, 0, T, 1e-5)
            normalise(nx, 0, T)
            for t in range(T):
                low_tile("T5", t, xt_high, 5 * T + t + 1)

            p_, tmp, first, second = rt[:, 0, :, :], rt[:, 1, :, :], rt[:, 2, :, :], rt[:, 3, :, :]
            m4 = [small[:, 4 * k:4 * k + 4] for k in range(6)]
            dve.wait_ge(*emptied(("lg",)))
            link(dve.tensor_reduce(m4[0], p_, AX_X, ALU.max, negate=True))
            dve.tensor_tensor(p_, p_, over(m4[0], E1), ALU.add).then_inc(rt_ready, 1)
            dve.wait_ge(rt_exp, 1)
            link(dve.tensor_reduce(m4[1], p_, AX_X, ALU.add))
            link(dve.reciprocal(m4[2], m4[1]))
            link(dve.tensor_tensor(p_, p_, over(m4[2], E1), ALU.mult))

            def largest(src, best, onehot):
                link(dve.tensor_reduce(best, src, AX_X, ALU.max))
                link(dve.tensor_tensor(onehot, src, over(best, E1), ALU.is_equal))
                link(dve.tensor_tensor(onehot, onehot, expert_rank.unsqueeze(1).broadcast_to([P, T, E1]), ALU.mult))
                link(dve.tensor_reduce(m4[5], onehot, AX_X, ALU.max))
                link(dve.tensor_tensor(onehot, onehot, over(m4[5], E1), ALU.is_equal))

            largest(p_, m4[3], first)
            link(dve.scalar_tensor_tensor(out=tmp, in0=first, scalar=-2.0, in1=p_, op0=ALU.mult, op1=ALU.add))
            largest(tmp, m4[4], second)
            link(dve.tensor_tensor(tmp, second, first, ALU.subtract))
            masks = []
            for k, src in enumerate((first, tmp, first, second)):
                if k >= 2:
                    link(dve.tensor_tensor(src, src, over(m4[3 + k - 2], E1), ALU.mult))
                last = dve.tensor_scalar(maskt[:, k, :, :].rearrange("p t (e r) -> p (t e) r", r=R),
                                         over(src.rearrange("p t e -> p (t e)"), R), 2.0, None, ALU.mult)
                if k < 3:
                    link(last)
            last.then_inc(masks_ready, 1)

            def gated(k):
                x = ("gu",) + gates[k]
                dve.wait_ge(silu_made, k + 1)
                if k == 1:
                    dve.wait_ge(um_split, 4)
                if k >= 2:
                    dve.wait_ge(hs_split, k - 1)
                dve.tensor_tensor(hh[k % 2], sg[k % 2], bank[bank_of[x] + 1][:, :], ALU.mult).then_inc(*freed(x))

            def gated_low(k):
                f, n = gates[k]
                dst = h0t[:, :, f, :] if n == 0 else hs[n - 1]
                dve.wait_ge(*emptied(("gu", f, n)))
                dve.wait_ge(hs_high, k + 1)
                dve.tensor_tensor(dst[:, 1, :], hh[k % 2], dst[:, 0, :].bitcast(F32), ALU.subtract).then_inc(hs_split, 1)

            um_tile = (sg[1], hh[1])

            def um_low(k):
                dve.wait_ge(um_made, k + 1)
                dve.wait_ge(um_high, k + 1)
                dve.tensor_tensor(um[:, k, 1, :], um_tile[k % 2], um[:, k, 0, :].bitcast(F32), ALU.subtract).then_inc(um_split, 1)

            for k in range(4):
                x = ("ug",) if k % 2 == 0 else ("uu",)
                dve.wait_ge(*full(x))
                dve.wait_ge(*emptied(("tm", k // 2)))
                if k == 2:
                    um_low(0)
                    um_low(1)
                    gated(0)
                    gated_low(0)
                    dve.wait_ge(*full(("tm", 3)))
                if k >= 2:
                    dve.wait_ge(um_split, k - 1)
                ins = dve.tensor_tensor(um_tile[k % 2], psum(x)[:, :], mk[:, k // 2, :], ALU.mult)
                ins.then_inc(um_made, 1)
            um_low(2)
            um_low(3)
            for k in range(1, len(gates)):
                gated(k)
                gated_low(k)
            dve.wait_ge(hs_split, len(gates))
            for n in (1, 2):
                dve.wait_ge(*full(("z", n)))
                dve.wait_ge(*emptied(("tm", 1 + n)))
                dve.tensor_tensor(hh[n - 1], psum(("z", n))[:, :], mk[:, 1 + n, :], ALU.mult).then_inc(*freed(("z", n)))
            for n in (1, 2):
                dve.wait_ge(*emptied(("z", n)))
            dve.tensor_tensor(hh[0], hh[0], hh[1], ALU.add).then_inc(z_made, 1)
            for t in range(T):
                x = ("y4", t)
                dve.wait_ge(*full(x))
                dve.tensor_tensor(x3[:, t, :], x3[:, t, :], psum(x)[:, :], ALU.add).then_inc(x_final, 1)

        @block.gpsimd
        def _(pool):
            link = in_order(pool, pool_step)
            pool.memset(KBD[:, :], 0.0).then_inc(zeroed, 1)
            pool.memset(VBD[:, :], 0.0).then_inc(zeroed, 1)
            pool.wait_ge(wq_high, 1)
            pool.tensor_tensor(WQO[:, 3072:4096], STG[:, 1024:2048], WQO[:, 1024:2048].bitcast(F32),
                               ALU.subtract).then_inc(wq_split_rest, 1)
            pool.wait_ge(wout_high, 1)
            pool.tensor_tensor(WQO[:, 6144:8192], STG[:, 2048:4096], WQO[:, 4096:6144].bitcast(F32),
                               ALU.subtract).then_inc(wout_split, 1)
            pool.wait_ge(exp_made, 1)
            p_, q, w = sw[:, 0, :, :], sw[:, 2, :, :], lags_raw
            link(pool.tensor_scalar(ssm[:, 0:2, :, :], ssm[:, 0:2, :, :], 1.0, None, ALU.add))
            link(pool.tensor_tensor(sw[:, 1, :, :], ssm[:, 0, :, :], ssm[:, 1, :, :], ALU.mult))
            pool.wait_ge(rates_made, 1)
            link(pool.tensor_tensor(q, p_, ssm[:, 2, :, :], ALU.mult))
            link(pool.tensor_scalar(q, q, NSSM ** -0.5, None, ALU.mult))
            link(pool.tensor_tensor(w[:, :, 0, :], q, ssm[:, 3, :, :], ALU.mult))
            link(pool.tensor_scalar(q, p_, -1.0, 1.0, ALU.mult, ALU.add))
            for l in range(1, LAGS):
                last = pool.tensor_tensor(w[:, :, l, :], w[:, :, l - 1, :], q, ALU.mult)
                if l + 1 < LAGS:
                    link(last)
            last.then_inc(states_made, 1)
            eight = lambda ap: ap.rearrange("p (b l) -> p b l", b=NB)
            pool.wait_ge(kv1_in, 3 * 16)
            link(pool.tensor_tensor(eight(kv_raw), eight(kv_raw), cos_t.unsqueeze(1).broadcast_to([P, NB, SK]), ALU.mult))
            link(pool.tensor_tensor(eight(kv_rot), eight(kv_rot), sin_t.unsqueeze(1).broadcast_to([P, NB, SK]), ALU.mult))
            pool.tensor_tensor(kv_raw, kv_raw, kv_rot, ALU.add).then_inc(kv_roped, 1)

            def round_quarter(i, at, done):
                pool.tensor_scalar(stg4[:, i, :], stg4[:, i, :], wtot[:, at + 3:at + 4], MAGIC, ALU.mult,
                                   ALU.add).then_inc(done[i], 1)

            pool.wait_ge(means_made, 1)
            round_quarter(2, 0, fc_rounded)
            round_quarter(3, 0, fc_rounded)
            pool.wait_ge(kvt_high, 1)
            pool.wait_ge(lags_made, 1)
            pool.tensor_tensor(KVT[:, 2048:4096], kv_raw, KVT[:, 0:2048].bitcast(F32), ALU.subtract).then_inc(kvt_split, 1)

            pool.wait_ge(means_made, 2)
            for i in range(4):
                round_quarter(i, 8, pj_rounded)
            pool.wait_ge(kr_high, 1)
            pool.tensor_tensor(KR[:, 1024:2048], kr_raw, KR[:, 0:1024].bitcast(F32), ALU.subtract).then_inc(kr_split, 1)
            for n in range(NB * G1):
                b = n % NB
                u = 16 * (b % 4)
                pool.wait_ge(recip_made, n + 1)
                for i in (0, 1):
                    last = pool.tensor_scalar(pw[:, b % 4, i, :], pw[:, b % 4, i, :], mxs[:, u + 4 + i:u + 5 + i], None, ALU.mult)
                last.then_inc(pw_ready, 1)
                if n in (NB * (G1 - 1) + 1, NB * (G1 - 1) + 3):
                    c = n - NB * (G1 - 1) - 1
                    pool.wait_ge(*full(("sc", G1 - 2, NB - 1)))
                    pool.tensor_tensor(lag_tile[0][:, c, :, :], ident.unsqueeze(1).broadcast_to([P, LAGS, P]),
                                       over(lag2[:, 0, c, :].bitcast(F32), P), ALU.mult).then_inc(lag_tiles_rest, 1)
            pool.wait_ge(*full(("sc", G1 - 1, NB - 1)))
            for c in (2, 3):
                pool.tensor_tensor(lag_tile[1][:, c, :, :], ident.unsqueeze(1).broadcast_to([P, LAGS, P]),
                                   over(lag2[:, 1, c, :].bitcast(F32), P), ALU.mult).then_inc(lag_tiles_rest, 1)
            pool.wait_ge(agu_high, 1)
            pool.tensor_tensor(agu[:, 1, :], STG[:, 6144:7200], agu[:, 0, :].bitcast(F32), ALU.subtract).then_inc(agu_split, 1)
            for f in range(NF):
                pool.wait_ge(ring_high, f + 1)
                pool.tensor_tensor(ring[:, f % 3, 1, :], STG[:, 2048 * (f % 2):2048 * (f % 2) + CH],
                                   ring[:, f % 3, 0, :].bitcast(F32), ALU.subtract).then_inc(ring_split, 1)
                if 7 <= f < 10:
                    j = f - 7
                    w = slice(2048 * j, 2048 * j + 512 * min(4, NF - 4 * j))
                    pool.wait_ge(wd_high, j + 1)
                    pool.tensor_tensor(WDT[:, NF * 512:][:, w], WDF[:, w], WDT[:, w].bitcast(F32), ALU.subtract).then_inc(wd_split, 1)


def _constants():
    c = np.zeros((P, 465), np.float32)
    c[:, 0:128] = np.eye(P)
    row, key = np.arange(P)[:, None], np.arange(P)[None, :]
    c[:, 128:192] = np.where(key[:, :SQ] <= row % SQ, 0.0, HIDDEN)
    c[:, 192:320] = np.where((row // SQ == key // SQ) & (key <= row), 0.0, HIDDEN)
    c[:, 328:456] = 1.0
    c[:, 456:464] = np.arange(E1, 0, -1)
    c[:, 464] = -MAGIC
    return c


def _rope_tables():
    inv = (np.float32(1.0) / np.float32(10000.0) ** (np.arange(0, DCTX, 2, dtype=np.float32) / np.float32(DCTX))).astype(np.float32)
    freqs = np.arange(SK, dtype=np.float32)[:, None] * inv[None, :]
    sin, cos = np.repeat(np.sin(freqs), 2, axis=-1).T, np.repeat(np.cos(freqs), 2, axis=-1).T
    sign = np.where(np.arange(DCTX) < DCTX // 2, -1.0, 1.0).astype(np.float32)[:, None]
    return np.concatenate([cos, sin * sign], axis=1).astype(np.float32)


def _layout(i):
    def chunks(w):
        return w.reshape(-1, P, w.shape[1]).transpose(1, 0, 2).reshape(P, -1)

    def cat(*parts):
        return np.concatenate([p.reshape(P, -1) for p in parts], axis=1)

    ctx = i["ctx_512"]
    ctx_t = ctx.reshape(-1, DCTX).T
    consts = _constants()
    consts[:, 320:324] = i["L0_attn_gamma"].reshape(KC, P).T
    consts[:, 324:328] = i["L0_attn_beta"].reshape(KC, P).T
    qkv = i["L0_attn_qkv"]
    half = DCTX // 2
    kcq = i["L1_xattn_w_kc_q"].reshape(H1, P, 3, P).transpose(3, 0, 2, 1)
    wqr = i["L1_xattn_W_qr"].reshape(H1, 3, P, R1).transpose(2, 0, 1, 3)
    wq1 = i["L1_xattn_Wq"].reshape(H1, P, D).transpose(1, 0, 2)
    kckv = i["L1_xattn_w_kc_kv"].transpose(1, 0, 2)
    wo1 = i["L1_xattn_Wo"].T.reshape(H1, P, D).transpose(1, 0, 2)
    heads = lambda w, g: w[:, HG * g:HG * (g + 1)]
    kr = i["L1_xattn_W_kr"].transpose(0, 2, 1).reshape(H1 // 2, 2 * R1, DCTX).transpose(1, 0, 2)
    agu = [i[n].reshape(E1 * R, D).T for n in ("L1_ffn_Ag", "L1_ffn_Au")]
    bgu = [i[n].transpose(0, 2, 1).reshape(E1 * R, DFF) for n in ("L1_ffn_Bg", "L1_ffn_Bu")]
    ad = i["L1_ffn_Ad"].reshape(E1 * R, DFF).T

    def mlp(f):
        s = slice(P * f, P * (f + 1))
        return cat(chunks(i["L1_ffn_Wg"][s].T), chunks(i["L1_ffn_Wu"][s].T), bgu[0][:, s], bgu[1][:, s], ad[s])

    laid = {
        "x": i["x"].reshape(NB * SQ, D),
        "kv0": cat(ctx[:, :SQ].reshape(-1, DCTX).T, i["L0_xattn_Wkv_expand"].T),
        "consts": consts,
        "wq": chunks(i["L0_xattn_Wq"].T),
        "wout": chunks(i["L0_xattn_Wout"].T),
        "fold_qk": cat(chunks(qkv[:, :D].T), chunks(qkv[:, D:2 * D].T)),
        "fold_vo": cat(chunks(qkv[:, 2 * D:].T), chunks(i["L0_attn_o_proj"])),
        "fc": chunks(i["L0_ffn_w_fc"].T).reshape(P, 4, 2048).transpose(1, 0, 2),
        "pj": chunks(i["L0_ffn_w_proj"].T).reshape(P, 4, 2048).transpose(1, 0, 2),
        "kv1": cat(ctx_t, np.concatenate([ctx_t[half:], ctx_t[:half]]), _rope_tables()),
        "kr": kr.reshape(P, -1),
        "queries": np.stack([cat(heads(kcq, g), heads(wqr, g), heads(wq1, g)) for g in range(G1)]),
        "values": np.stack([cat(heads(kckv, g), heads(wo1, g)) for g in range(G1)]),
        "ssm": cat(*[chunks(i["L1_attn_" + n].reshape(D, NSSM)) for n in ("delta", "alpha", "beta", "gamma")]),
        "agu": cat(chunks(agu[0]), chunks(agu[1]), chunks(i["L1_ffn_Wr"].T)),
        "mlp": np.stack([mlp(f) for f in range(NF)]),
        "wd": chunks(i["L1_ffn_Wd"].T),
        "bd": i["L1_ffn_Bd"].transpose(0, 2, 1).reshape(E1 * R, D),
    }
    return {n: np.ascontiguousarray(v) for n, v in laid.items()}


def kernel(**inputs):
    import concourse.bacc as bacc
    from concourse.bass_utils import run_bass_kernel_spmd

    laid = _layout({n: np.asarray(v) for n, v in inputs.items()})
    nc = bacc.Bacc("TRN2", target_bir_lowering=False, num_devices=1)
    arrays = {f"in_{n}": v for n, v in laid.items()}
    aps = {n: nc.dram_tensor(f"in_{n}", v.shape, F32, kind="ExternalInput").ap() for n, v in laid.items()}
    out = nc.dram_tensor("out_x", (NB * SQ, D), F32, kind="ExternalOutput").ap()
    perceiver_blocks(nc, aps, out)
    r = run_bass_kernel_spmd(nc, [arrays], core_ids=[0])
    return r.results[0]["out_x"].reshape(NB, SQ, D)
```
